# Optimizing a Trainium2 kernel written in Bass

```python
import numpy as np
import jax
import jax.numpy as jnp

def _softmax(x, axis=-1):
    return jax.nn.softmax(x, axis=axis)

def _gelu(x):
    return jax.nn.gelu(x, approximate=True)

def _silu(x):
    return jax.nn.silu(x)

def _sigmoid(x):
    return jax.nn.sigmoid(x)

def _layernorm(x, axis=-1, eps=1e-05):
    m = jnp.mean(x, axis=axis, keepdims=True)
    v = jnp.var(x, axis=axis, keepdims=True)
    return (x - m) / jnp.sqrt(v + eps)

def _scatter_add(tgt, idx, src, axis=0):
    return tgt.at[idx].add(src)

def _segment_sum(src, seg, n):
    return jax.ops.segment_sum(src, seg, n)
kernel_name = 'mk_macaron_d1_jaxref_r4_82ab8d'

def setup_inputs(seed: int=0):
    np.random.seed(seed)
    _w = jnp.asarray

    def _L0_attn_setup():
        import jax, jax.numpy as jnp
        import numpy as np
        B, T, C = (2, 512, 256)
        NHEADS = 16
        HEAD_DIM = C // NHEADS
        THETA = 10000.0
        SCALE_BASE = 512.0
        GN_EPS = 1e-05

        def _rotate_half(x):
            x1 = x[..., 0::2]
            x2 = x[..., 1::2]
            return jnp.stack([-x2, x1], axis=-1).reshape(x.shape)

        def _rope_xpos(q, k, T):
            d = q.shape[-1]
            half = jnp.arange(0, d, 2, dtype=jnp.float32)
            inv_freq = 1.0 / THETA ** (half / d)
            t = jnp.arange(T, dtype=jnp.float32)
            freqs = t[:, None] * inv_freq[None, :]
            freqs = jnp.repeat(freqs, 2, axis=-1)
            scale_vec = (half + 0.4 * d) / (1.4 * d)
            power = (t - T // 2) / SCALE_BASE
            scale = scale_vec[None, :] ** power[:, None]
            scale = jnp.repeat(scale, 2, axis=-1)
            cos, sin = (jnp.cos(freqs), jnp.sin(freqs))
            q = q * (cos * scale) + _rotate_half(q) * (sin * scale)
            k = k * (cos / scale) + _rotate_half(k) * (sin / scale)
            return (q, k)

        def _decay_mask(T):
            gamma = 1.0 - 2.0 ** (-5.0 - jnp.arange(NHEADS, dtype=jnp.float32))
            idx = jnp.arange(T)
            diff = idx[:, None] - idx[None, :]
            causal = diff >= 0
            expn = jnp.where(causal, diff, 0).astype(jnp.float32)
            return jnp.where(causal[None], gamma[:, None, None] ** expn[None], 0.0)
        key = jax.random.key(seed)
        ks = jax.random.split(key, 4)
        s = 0.02
        return {'x': jax.random.normal(ks[0], (B, T, C), jnp.float32), 'w_qkv': jax.random.normal(ks[1], (3 * C, C), jnp.float32) * s, 'w_gated': jax.random.normal(ks[2], (C, C), jnp.float32) * s, 'w_proj': jax.random.normal(ks[3], (C, C), jnp.float32) * s, 'gn_weight': jnp.ones((C,), jnp.float32), 'gn_bias': jnp.zeros((C,), jnp.float32)}
    _L0_attn_in = _L0_attn_setup()

    def _L0_ffn_setup():
        import jax, jax.numpy as jnp
        import numpy as np
        NUM_EXPERTS = 8
        TOP_K = 2
        CAPACITY_FACTOR = 1.0

        def _dispatch_compute(xf, top_expert, w1, w2, capacity):
            tokens, hs = xf.shape
            tpe = jnp.bincount(top_expert, length=NUM_EXPERTS)
            indices = jnp.argsort(top_expert)
            offsets = jnp.concatenate([jnp.zeros((1,), tpe.dtype), jnp.cumsum(tpe)[:-1]])
            slot = jnp.arange(capacity)
            pos = offsets[:, None] + slot[None, :]
            valid = slot[None, :] < tpe[:, None]
            tok_idx = indices[jnp.minimum(pos, tokens - 1)]
            xe = jnp.where(valid[..., None], xf[tok_idx], 0.0)
            h = jax.nn.gelu(jnp.einsum('ech,ehf->ecf', xe, w1), approximate=True)
            ye = jnp.einsum('ecf,efh->ech', h, w2)
            tok_safe = jnp.where(valid, tok_idx, tokens)
            out = jnp.zeros((tokens + 1, hs), xf.dtype).at[tok_safe.reshape(-1)].add(ye.reshape(-1, hs))
            return out[:tokens]
        key = jax.random.key(seed)
        k1, k2, k3, k4 = jax.random.split(key, 4)
        hs, ffn = (256, 1024)
        x = jax.random.normal(k1, (512, 2, hs), dtype=jnp.float32)
        router_w = jax.random.normal(k2, (hs, NUM_EXPERTS), dtype=jnp.float32) * hs ** (-0.5)
        w1 = jax.random.normal(k3, (NUM_EXPERTS, hs, ffn), dtype=jnp.float32) * 0.02
        w2 = jax.random.normal(k4, (NUM_EXPERTS, ffn, hs), dtype=jnp.float32) * 0.02
        bias = jnp.zeros((1, 1, hs), dtype=jnp.float32)
        return {'x': x, 'router_w': router_w, 'w1': w1, 'w2': w2, 'bias': bias}
    _L0_ffn_in = _L0_ffn_setup()
    _d = {'L0_attn_x': _L0_attn_in['x'], 'L0_attn_w_qkv': _L0_attn_in['w_qkv'], 'L0_attn_w_gated': _L0_attn_in['w_gated'], 'L0_attn_w_proj': _L0_attn_in['w_proj'], 'L0_attn_gn_weight': _L0_attn_in['gn_weight'], 'L0_attn_gn_bias': _L0_attn_in['gn_bias'], 'L0_ffn_router_w': _L0_ffn_in['router_w'], 'L0_ffn_w1': _L0_ffn_in['w1'], 'L0_ffn_w2': _L0_ffn_in['w2'], 'L0_ffn_bias': _L0_ffn_in['bias']}
    _x0 = _d['L0_attn_x']
    _d['L0_attn_x'] = jax.random.normal(jax.random.fold_in(jax.random.key(seed), 1), (8, 1024, 256), dtype=_x0.dtype)
    del _x0
    return _d

def reference(L0_attn_x, L0_attn_w_qkv, L0_attn_w_gated, L0_attn_w_proj, L0_attn_gn_weight, L0_attn_gn_bias, L0_ffn_router_w, L0_ffn_w1, L0_ffn_w2, L0_ffn_bias):

    def _L0_attn_ref(x, w_qkv, w_gated, w_proj, gn_weight, gn_bias):
        import jax, jax.numpy as jnp
        import numpy as np
        B, T, C = (2, 512, 256)
        NHEADS = 16
        HEAD_DIM = C // NHEADS
        THETA = 10000.0
        SCALE_BASE = 512.0
        GN_EPS = 1e-05

        def _rotate_half(x):
            x1 = x[..., 0::2]
            x2 = x[..., 1::2]
            return jnp.stack([-x2, x1], axis=-1).reshape(x.shape)

        def _rope_xpos(q, k, T):
            d = q.shape[-1]
            half = jnp.arange(0, d, 2, dtype=jnp.float32)
            inv_freq = 1.0 / THETA ** (half / d)
            t = jnp.arange(T, dtype=jnp.float32)
            freqs = t[:, None] * inv_freq[None, :]
            freqs = jnp.repeat(freqs, 2, axis=-1)
            scale_vec = (half + 0.4 * d) / (1.4 * d)
            power = (t - T // 2) / SCALE_BASE
            scale = scale_vec[None, :] ** power[:, None]
            scale = jnp.repeat(scale, 2, axis=-1)
            cos, sin = (jnp.cos(freqs), jnp.sin(freqs))
            q = q * (cos * scale) + _rotate_half(q) * (sin * scale)
            k = k * (cos / scale) + _rotate_half(k) * (sin / scale)
            return (q, k)

        def _decay_mask(T):
            gamma = 1.0 - 2.0 ** (-5.0 - jnp.arange(NHEADS, dtype=jnp.float32))
            idx = jnp.arange(T)
            diff = idx[:, None] - idx[None, :]
            causal = diff >= 0
            expn = jnp.where(causal, diff, 0).astype(jnp.float32)
            return jnp.where(causal[None], gamma[:, None, None] ** expn[None], 0.0)
        Bx, Tx, Cx = x.shape
        qkv = x @ w_qkv.T
        q, k, v = jnp.split(qkv, 3, axis=-1)

        def to_heads(u):
            return u.reshape(Bx, Tx, NHEADS, HEAD_DIM).transpose(0, 2, 1, 3)
        q, k, v = (to_heads(q), to_heads(k), to_heads(v))
        q, k = _rope_xpos(q, k, Tx)
        mask = _decay_mask(Tx)
        scores = jnp.einsum('bhtd,bhsd->bhts', q, k) * HEAD_DIM ** (-0.5)
        scores = scores * mask[None]
        y = jnp.einsum('bhts,bhsd->bhtd', scores, v)
        y = y.transpose(0, 2, 1, 3).reshape(Bx, Tx, Cx)
        yt = y.transpose(0, 2, 1).reshape(Bx, NHEADS, HEAD_DIM, Tx)
        mean = yt.mean(axis=(2, 3), keepdims=True)
        var = yt.var(axis=(2, 3), keepdims=True)
        yn = (yt - mean) / jnp.sqrt(var + GN_EPS)
        yn = yn.reshape(Bx, Cx, Tx)
        yn = yn * gn_weight[None, :, None] + gn_bias[None, :, None]
        yn = yn.transpose(0, 2, 1)
        out = jax.nn.silu(x @ w_gated.T) * yn
        return out @ w_proj.T

    def _L0_ffn_ref(x, router_w, w1, w2, bias):
        import jax, jax.numpy as jnp
        import numpy as np
        NUM_EXPERTS = 8
        TOP_K = 2
        CAPACITY_FACTOR = 1.0

        def _dispatch_compute(xf, top_expert, w1, w2, capacity):
            tokens, hs = xf.shape
            tpe = jnp.bincount(top_expert, length=NUM_EXPERTS)
            indices = jnp.argsort(top_expert)
            offsets = jnp.concatenate([jnp.zeros((1,), tpe.dtype), jnp.cumsum(tpe)[:-1]])
            slot = jnp.arange(capacity)
            pos = offsets[:, None] + slot[None, :]
            valid = slot[None, :] < tpe[:, None]
            tok_idx = indices[jnp.minimum(pos, tokens - 1)]
            xe = jnp.where(valid[..., None], xf[tok_idx], 0.0)
            h = jax.nn.gelu(jnp.einsum('ech,ehf->ecf', xe, w1), approximate=True)
            ye = jnp.einsum('ecf,efh->ech', h, w2)
            tok_safe = jnp.where(valid, tok_idx, tokens)
            out = jnp.zeros((tokens + 1, hs), xf.dtype).at[tok_safe.reshape(-1)].add(ye.reshape(-1, hs))
            return out[:tokens]
        sl, bs, hs = x.shape
        tokens = sl * bs
        capacity = int(CAPACITY_FACTOR * tokens / NUM_EXPERTS)
        xf = x.reshape(tokens, hs)
        scores = jax.nn.softmax(xf @ router_w, axis=-1)
        expert_weights, top_experts = jax.lax.top_k(scores, TOP_K)
        out = jnp.zeros_like(xf)
        for k in range(TOP_K):
            y = _dispatch_compute(xf, top_experts[:, k].astype(jnp.int32), w1, w2, capacity)
            out = out + y * expert_weights[:, k][:, None]
        return out.reshape(sl, bs, hs) + bias
    x = L0_attn_x
    x = x + 0.5 * _L0_ffn_ref(_layernorm(x, axis=-1), L0_ffn_router_w, L0_ffn_w1, L0_ffn_w2, L0_ffn_bias)
    x = x + _L0_attn_ref(_layernorm(x, axis=-1), L0_attn_w_qkv, L0_attn_w_gated, L0_attn_w_proj, L0_attn_gn_weight, L0_attn_gn_bias)
    x = x + 0.5 * _L0_ffn_ref(_layernorm(x, axis=-1), L0_ffn_router_w, L0_ffn_w1, L0_ffn_w2, L0_ffn_bias)
    return x

_drawn_inputs = setup_inputs


def setup_inputs(seed=0):
    import zlib

    import numpy as np

    out = dict(_drawn_inputs(seed))
    spreads = {'L0_attn_gn_weight': (1.0, 0.6), 'L0_attn_gn_bias': (0.0, 0.8), 'L0_ffn_bias': (0.0, 0.1)}
    factors = {}
    for name, (base, spread) in spreads.items():
        noise = np.random.default_rng([zlib.crc32(name.encode()), seed]).standard_normal(out[name].shape)
        drawn = base * np.exp(spread * noise) if base else spread * noise
        out[name] = jnp.asarray(drawn.astype(out[name].dtype))
    for name, factor in factors.items():
        out[name] = (out[name] * factor).astype(out[name].dtype)
    return out
```

```python
import numpy as np
import concourse.bass as bass
from concourse import mybir
from contextlib import ExitStack

DT = mybir.dt
ALU = mybir.AluOpType
ACT = mybir.ActivationFunctionType
AX = mybir.AxisListType

P = 128
B, T, C = 8, 1024, 256
N = B * T
NT = T // P
KC = C // P
H, D = 16, 16
HH = H // KC
E, TOPK, FF = 8, 2, 1024
CAP = N // E
FJ = FF // P
G = 512
GT = G // P
GE = TOPK * CAP // G
NG = E * GE
SLOTS = NG * G
ROWS = N + G
EPS = 1e-5
BIG = 1.0e6
RT = TOPK * NT

CONST_COLS = dict(ident=P, before=P, causal=P, headmean=P, stateblk=C, headsel=HH, decay=KC,
                  revexp=E, restart=RT * E, slotbase=RT, mhalf=RT, ids=NT)


def const_at():
    at, out = 0, {}
    for name, n in CONST_COLS.items():
        out[name] = (at, at + n)
        at += n
    return out, at


class Names(dict):
    __getattr__ = dict.__getitem__


class Count:

    def __init__(self):
        self.n, self.shift = 0, 0

    def up(self, k=1):
        self.n += k
        return self.n + self.shift

    def enter(self, i, per):
        self.per, self.start, self.shift = per, self.n, i * per

    def leave(self, times):
        assert self.n - self.start == self.per, (self.n - self.start, self.per)
        self.n, self.shift = self.start + self.per * times, 0


def macaron_kernel(nc, x_in, w_qkv, w_gated, w_proj, gn_w, gn_b, router_w, w1, w2, f_bias,
                   consts_in, rope_in, slots_in, out):
    fp32, f32r, u32 = DT.float32, DT.float32r, DT.uint32
    ctx = ExitStack()
    with ctx:
        def sb(name, shape, dt=fp32):
            return ctx.enter_context(nc.sbuf_tensor(name, shape, dt))

        def sems(prefix, names):
            return Names({n: ctx.enter_context(nc.semaphore(f"{prefix}_{n}")) for n in names.split()})

        acc1 = nc.dram_tensor("acc1", [ROWS, C], fp32).ap()
        xn_d = nc.dram_tensor("xn_rows", [ROWS, C], fp32).ap()
        slot_d = [nc.dram_tensor(f"slot_table{r}", [SLOTS, 2], fp32).ap() for r in range(2)]

        at, ncol = const_at()
        cst = sb("cst", [P, ncol])
        K_ = {n: cst[:, a:b] for n, (a, b) in at.items()}
        ident, before, causal, headmean = (K_[n] for n in ("ident", "before", "causal", "headmean"))
        ones = sb("ones", [P, P])
        hbias = sb("hbias", [P, C])
        gnw, gnb = sb("gnw", [P, KC]), sb("gnb", [P, KC])
        rw = sb("rw", [P, KC, E])
        wqkT, wvT, wgT, wpT = sb("wqkT", [P, KC, 2 * C]), sb("wvT", [P, KC, C]), sb("wgT", [P, KC, C]), sb("wpT", [P, KC, C])

        w1h, w1l = sb("w1h", [P, KC, FF], f32r), sb("w1l", [P, KC, FF], f32r)
        w2h, w2l = sb("w2h", [P, FJ, C], f32r), sb("w2l", [P, FJ, C], f32r)
        xh = [sb(f"xh{i}", [P, KC, G], f32r) for i in range(2)]
        xl = [sb(f"xl{i}", [P, KC, G], f32r) for i in range(2)]
        hh, hl = sb("hh", [P, FJ, G], f32r), sb("hl", [P, FJ, G], f32r)
        tab = sb("tab", [P, GE, GT, 2])

        arena = sb("arena", [P, 2 * 2048 + 2 * GT * C * 2 + 2 * G])
        cut = [0]

        def take(n):
            cut[0] += n
            return arena[:, cut[0] - n:cut[0]]

        stg1 = take(KC * FF).rearrange("p (k f) -> p k f", k=KC)
        stg2 = take(FJ * C).rearrange("p (j c) -> p j c", j=FJ)
        xe = [take(GT * C).rearrange("p (t c) -> p t c", t=GT) for _ in range(2)]
        yb = [take(GT * C).rearrange("p (t c) -> p t c", t=GT) for _ in range(2)]
        h32 = [take(G) for _ in range(2)]
        cut[0] = 0
        rope = take(NT * 4 * C).rearrange("p (t w c) -> p t w c", t=NT, w=2)
        rt1, rt2 = take(2 * C), take(2 * C)
        xn_f, xn_r = (a.rearrange("p (n c) -> p n c", n=2) for a in (rt1, rt2))
        wraw = arena[:, 0:10 * C].rearrange("p (j c) -> p j c", j=10)
        zrow = arena[:, 10 * C:14 * C]

        xb = sb("xb", [P, NT, C])
        xr = sb("xr", [P, NT, C])
        xnT = sb("xnT", [P, KC, T])
        xrT = sb("xrT", [P, 2, KC, P])
        gT, yT = sb("gT", [P, KC, T]), sb("yT", [P, KC, T])
        qk = sb("qk", [P, 2, 2 * C])
        vz = sb("vz", [P, 2, H * 2 * D])
        qkT = sb("qkT", [P, 2 * KC, P])
        km = sb("km", [P, KC, HH, P])
        aw = sb("aw", [P, 4, 4, P])
        state, stmp = sb("state", [P, KC, P]), sb("stmp", [P, KC, P])

        def stats(n):
            return Names(st=sb(n + "_st", [P, NT, 6]), mv=sb(n + "_mv", [P, 5, NT]), rv=sb(n + "_rv", [P, NT]),
                                   rs=sb(n + "_rs", [P, NT]), nm=sb(n + "_nm", [P, NT]))

        lnf, lnr = stats("lnf"), stats("lnr")
        gst, gmv = sb("gst", [P, KC, 2, 6]), sb("gmv", [P, KC, 2])
        gsm, gdv = sb("gsm", [P, 8, KC]), sb("gdv", [P, KC, 4])
        lg, dl, ex, d2 = (sb(n, [P, NT, E]) for n in ("lg", "dl", "ex", "d2"))
        key = sb("key", [P, TOPK, NT, E])
        oh = sb("oh", [P, TOPK, NT, E])
        cnt, scn = sb("cnt", [P, TOPK, E, NT]), sb("scn", [P, TOPK, E, NT])
        pos = sb("pos", [P, TOPK, NT, E])
        base = sb("base", [P, TOPK, E])
        red = sb("red", [P, 4, NT])
        sel = sb("sel", [P, 8, RT])
        ids = sb("ids", [P, NT])
        pay = sb("pay", [P, RT, 2])
        idx = sb("idx", [P, RT], u32)

        bank = [ctx.enter_context(nc.psum_tensor(f"bank{i}", [P, 512], fp32)) for i in range(8)]

        S0 = sems("setup", "const vec rw zero acc_z out_z xn_z slot0 slot1 rope wraw wT wTc bias memset base passed")
        RN = "x ready lnst lnmv lnrv lnrs lnnm xn xnst trp trp_r xT xT_r sm sm_r exp link pay sent scat stored half o"
        R = [sems(f"route{r}", RN) for r in range(2)]
        F = [sems(f"ffn{r}", "w1raw w2raw w1h w1l w2h w2l tab0 tab1 tab2 tab3 xe0 xe1 xT xh xl up gelu hh hl down y add")
             for r in range(2)]
        A = sems("attn", "x lnst lnmv lnrv lnrs lnnm xn qk qk_r v v_r t t_r roped vz qkT kmd kma "
                         "sc sc_r aw y y_r st st_r stt state0 g f gst gst2 gmv gs gs_r glink grv grs gaff yg gated")

        block = ctx.enter_context(nc.Block())
        tok = lambda a: a[0:N, :].rearrange("(b t p) c -> b p t c", t=NT, p=P)
        x_t, acc1_t, xn_t, out_t = tok(x_in), tok(acc1), tok(xn_d), tok(out)
        spare = lambda a: a[N:ROWS, :].rearrange("(t p) c -> p t c", p=P)

        def held(eng, sem, value):
            eng.wait_ge(sem, value)
            eng.sem_inc(S0.passed, 1)

        @block.sync
        def _(sp):
            sp.dma_start(cst[:], consts_in).then_inc(S0.const, 16)
            sp.dma_start(wraw[:, 0:6, :], w_qkv.rearrange("(j p) c -> p j c", p=P)).then_inc(S0.wraw, 16)
            sp.dma_start(wraw[:, 6:8, :], w_gated.rearrange("(j p) c -> p j c", p=P)).then_inc(S0.wraw, 16)
            sp.dma_start(wraw[:, 8:10, :], w_proj.rearrange("(j p) c -> p j c", p=P)).then_inc(S0.wraw, 16)
            sp.dma_start(rw[:], router_w.rearrange("(k p) e -> p k e", p=P)).then_inc(S0.rw, 16)
            for k in range(KC):
                half = lambda v: v[k * P:(k + 1) * P].rearrange("(p a) -> p a", a=1)
                sp.dma_start(gnw[:, k:k + 1], half(gn_w)).then_inc(S0.vec, 16)
                sp.dma_start(gnb[:, k:k + 1], half(gn_b)).then_inc(S0.vec, 16)
            sp.dma_start(hbias[:], f_bias.rearrange("a b c -> (a b) c").to_broadcast([P, C])).then_inc(S0.vec, 16)
            sp.dma_start(slot_d[0], slots_in).then_inc(S0.slot0, 16)
            sp.dma_start(slot_d[1], slots_in).then_inc(S0.slot1, 16)
            sp.wait_ge(S0.zero, 1)
            zt = zrow.rearrange("p (t c) -> p t c", t=GT)
            sp.dma_start(spare(acc1), zt).then_inc(S0.acc_z, 16)
            sp.dma_start(spare(out), zt).then_inc(S0.out_z, 16)
            sp.dma_start(spare(xn_d), zt).then_inc(S0.xn_z, 16)

            def route_store(S, b, dst):
                for t in range(NT):
                    sp.wait_ge(S.xn, b * NT + t + 1)
                    sp.dma_start(xn_t[b, :, t, :], xn_r[:, t % 2, :]).then_inc(S.xnst, 16)
                    sp.wait_ge(S.xnst, b * NT * 16 + t * 16 + 16)
                    sp.sem_inc(S.ready, 1)
                sp.wait_ge(S.half, b + 1)
                sp.dma_start(dst[b, :, :, :], xr[:]).then_inc(S.stored, 16)

            with sp.Fori(0, B) as b:
                sp.dma_start(xr[:], x_t[b, :, :, :]).then_inc(R[0].x, 16)
                route_store(R[0], b, acc1_t)
                held(sp, R[0].stored, b * 16 + 16)

            def ffn(r):
                f = F[r]
                w1_t = w1.rearrange("e (k p) f -> e p k f", p=P)
                w2_t = w2.rearrange("e (j p) c -> e p j c", p=P)
                tab_t = slot_d[r].rearrange("(g p t) w -> g p t w", p=P, t=GT)

                def weights(e):
                    sp.dma_start(stg1, w1_t[e, :, :, :]).then_inc(f.w1raw, 16)
                    sp.dma_start(stg2, w2_t[e, :, :, :]).then_inc(f.w2raw, 16)

                def expert(e, last):
                    if not last:
                        sp.wait_ge(f.w1l, e * FJ + FJ)
                        sp.dma_start(stg1, w1_t[e + 1, :, :, :]).then_inc(f.w1raw, 16)
                        sp.wait_ge(f.w2l, e * FJ + FJ)
                        sp.dma_start(stg2, w2_t[e + 1, :, :, :]).then_inc(f.w2raw, 16)
                    for j in range(GE):
                        if last and j > 0:
                            break
                        if not last:
                            held(sp, f.add, e * (GE * GT * 16) + (j + 1) * GT * 16)
                            sp.dma_start(tab[:, j, :, :], tab_t[e * GE + GE + j, :, :, :]).then_inc(tabs[j], 16)

                tabs = [f.tab0, f.tab1, f.tab2, f.tab3]
                if r == 0:
                    sp.wait_ge(S0.wT, 20)
                    sp.wait_ge(S0.acc_z, 16)
                    sp.wait_ge(S0.out_z, 16)
                    sp.wait_ge(S0.xn_z, 16)
                else:
                    sp.wait_ge(A.roped, B * NT)
                weights(0)
                sp.wait_ge(R[r].scat, B * RT * 16)
                for j in range(GE):
                    sp.dma_start(tab[:, j, :, :], tab_t[j, :, :, :]).then_inc(tabs[j], 16)
                with sp.Fori(0, E - 1) as e:
                    expert(e, False)

            ffn(0)

            def front(b):
                sp.wait_ge(A.xn, b * NT + 1)
                sp.dma_start(xb[:], acc1_t[b, :, :, :]).then_inc(A.x, 16)

            def tail(b):
                sp.dma_start(xr[:], acc1_t[b, :, :, :]).then_inc(R[1].x, 16)
                route_store(R[1], b, out_t)
                held(sp, R[1].stored, b * 16 + 16)

            sp.wait_ge(F[0].add, NG * GT * 16)
            sp.sem_inc(A.xn, 1)
            front(0)
            for t in range(NT):
                sp.dma_start(rope[:, t, :, :], rope_in[t, :, :, :]).then_inc(S0.rope, 16)
            with sp.Fori(0, B - 1) as b:
                front(b + 1)
                tail(b)
            tail(B - 1)
            ffn(1)
            sp.wait_ge(F[1].add, NG * GT * 16)

        @block.gpsimd
        def _(pool):
            pool.memset(zrow, 0.0).then_inc(S0.zero, 1)
            pool.memset(ones[:], 1.0).then_inc(S0.memset, 1)
            pool.memset(vz[:], 0.0).then_inc(S0.memset, 1)
            pool.wait_ge(S0.const, 16)
            pool.wait_ge(S0.slot0, 16)
            pool.wait_ge(S0.slot1, 16)

            def power(S, ln, b):
                held(pool, S.lnrv, b + 1)
                pool.tensor_tensor(ln.rs[:], ln.rv[:], K_["mhalf"][:, 0:NT], ALU.pow).then_inc(S.lnrs, 1)

            def scatter(r, b):
                held(pool, R[r].pay, b + 1)
                for n in range(RT):
                    pool.indirect_dma_start(
                        out=slot_d[r], out_offset=bass.IndirectOffsetOnAxis(ap=idx[:, n:n + 1], axis=0),
                        in_=pay[:, n, :], in_offset=None, bounds_check=SLOTS - 1, oob_is_err=False).then_inc(R[r].scat, 16)
                pool.wait_ge(R[r].scat, b * RT * 16 + RT * 16)
                pool.sem_inc(R[r].sent, 1)

            with pool.Fori(0, B) as b:
                power(R[0], lnr, b)
                scatter(0, b)

            def ffn(r):
                f = F[r]
                tabs = [f.tab0, f.tab1, f.tab2, f.tab3]
                xes = [f.xe0, f.xe1]
                dst = acc1 if r == 0 else out
                tabu = tab[:].bitcast(u32)

                def gather(j, waits):
                    for sem, value in waits:
                        held(pool, sem, value)
                    for t in range(GT):
                        pool.indirect_dma_start(
                            out=xe[j % 2][:, t, :], out_offset=None, in_=xn_d,
                            in_offset=bass.IndirectOffsetOnAxis(ap=tabu[:, j, t, 0:1], axis=0),
                            bounds_check=ROWS - 1, oob_is_err=True).then_inc(xes[j % 2], 16)

                def add(e, j):
                    held(pool, f.y, e * GE * GT + (j + 1) * GT)
                    if not (isinstance(e, int) and e == 0 and j == 0):
                        held(pool, f.add, e * (GE * GT * 16) + j * GT * 16)
                    for t in range(GT):
                        pool.indirect_dma_start(
                            out=dst, out_offset=bass.IndirectOffsetOnAxis(ap=tabu[:, j, t, 0:1], axis=0),
                            in_=yb[j % 2][:, t, :], in_offset=None, compute_op=ALU.add,
                            bounds_check=ROWS - 1, oob_is_err=True).then_inc(f.add, 16)

                held(pool, R[r].stored, B * 16)
                held(pool, R[r].xnst, N // P * 16)
                gather(0, [(f.tab0, 16)])
                gather(1, [(f.tab1, 16)])
                gather(2, [(f.tab2, 16), (f.xT, 1)])

                def expert(e, last):
                    for j in range(GE):
                        add(e, j)
                        g3 = j + 3
                        if last and g3 >= GE:
                            continue
                        gather(g3 % GE, [(tabs[g3 % GE], e * 16 + 16 * (g3 // GE) + 16), (f.xT, e * GE + j + 2)])

                expert(0, False)
                with pool.Fori(1, E - 1) as e:
                    expert(e, False)
                expert(E - 1, True)

            ffn(0)

            def gn_power(b):
                held(pool, A.grv, b + 1)
                pool.tensor_tensor(gsm[:, 3, :], gsm[:, 2, :], K_["mhalf"][:, 0:KC], ALU.pow).then_inc(A.grs, 1)

            power(A, lnf, 0)
            with pool.Fori(0, B - 1) as b:
                power(A, lnf, b + 1)
                gn_power(b)
                power(R[1], lnr, b)
                scatter(1, b)
            gn_power(B - 1)
            power(R[1], lnr, B - 1)
            scatter(1, B - 1)
            ffn(1)

        @block.tensor
        def _(pe):
            pe.wait_ge(S0.const, 16)
            pe.wait_ge(S0.wraw, 48)
            for n in range(20):
                j, k = n // KC, n % KC
                if n >= 4:
                    pe.wait_ge(S0.wTc, n - 3)
                pe.transpose(bank[n % 4][:, 0:P], wraw[:, j, k * P:(k + 1) * P], ident).then_inc(S0.wT, 1)

            def route(r, b, tr_free, tr_full):
                S = R[r]
                for t in range(NT):
                    pe.wait_ge(S.xn, b * NT + t + 1)
                    tr_free(t)
                    for k in range(KC):
                        last = pe.transpose(bank[1 + t % 2][:, k * P:(k + 1) * P], xn_r[:, t % 2, k * P:(k + 1) * P], ident)
                    last.then_inc(tr_full(t), 1)
                    if t:
                        logits(S, b, t - 1)
                logits(S, b, NT - 1)
                pe.wait_ge(S.link, b * LINKS + OH_LINK)
                pe.wait_ge(S.sm_r, b * 2 + 2)
                pe.matmul(bank[7][:, 0:RT * E], before, oh[:].rearrange("p k t e -> p (k t e)"), start=True, stop=True)
                pe.matmul(bank[7][:, RT * E:2 * RT * E], ones[:], oh[:].rearrange("p k t e -> p (k t e)"), start=True, stop=True)\
                    .then_inc(S.sm, 1)

            def logits(S, b, t):
                pe.wait_ge(S.xT, b * NT + t + 1)
                if t == 0:
                    pe.wait_ge(S.sm_r, b * 2 + 1)
                for k in range(KC):
                    last = pe.matmul(bank[7][:, t * E:(t + 1) * E], xrT[:, t % 2, k, :], rw[:, k, :],
                                     start=(k == 0), stop=(k == KC - 1))
                last.then_inc(S.xT_r if t < NT - 1 else S.sm, 1)

            pe.wait_ge(S0.wTc, 20)
            pe.wait_ge(S0.rw, 16)
            pe.wait_ge(S0.memset, 2)
            with pe.Fori(0, B) as b:
                route(0, b, lambda t: pe.wait_ge(R[0].trp_r, b * NT + t + 1), lambda t: R[0].trp)

            def ffn(r):
                f = F[r]
                xes = [f.xe0, f.xe1]

                def transposes(j, xe_value, xl_value):
                    pe.wait_ge(xes[j % 2], xe_value)
                    if xl_value is not None:
                        pe.wait_ge(f.xl, xl_value)
                    for k in range(KC):
                        for t in range(GT):
                            last = pe.transpose(bank[6 + k][:, t * P:(t + 1) * P], xe[j % 2][:, t, k * P:(k + 1) * P], ident)
                    last.then_inc(f.xT, 1)

                def up(j, fj, up_free):
                    if up_free is not None:
                        pe.wait_ge(f.gelu, up_free)
                    n = 0
                    for k in range(KC):
                        w = slice(fj * P, (fj + 1) * P)
                        for a, c in ((w1h, xh), (w1h, xl), (w1l, xh)):
                            last = pe.matmul(bank[fj % 2][:], a[:, k, w], c[j % 2][:, k, :], start=(n == 0), stop=(n == 5))
                            n += 1
                    last.then_inc(f.up, 1)

                def down(j, fj):
                    for t in range(GT):
                        s = slice(t * P, (t + 1) * P)
                        o = bank[2 + 2 * (j % 2) + t // 2][:, (t % 2) * C:(t % 2 + 1) * C]
                        for n, (a, c) in enumerate(((hh, w2h), (hh, w2l), (hl, w2h))):
                            last = pe.matmul(o, a[:, fj, s], c[:, fj, :], start=(fj == 0 and n == 0 and t % 2 == 0),
                                             stop=(fj == FJ - 1 and n == 2), skip_group_check=True)
                    if fj == FJ - 1:
                        last.then_inc(f.down, 1)

                transposes(0, GT * 16, None)
                transposes(1, GT * 16, KC)
                pe.wait_ge(f.w1l, FJ)
                pe.wait_ge(f.xl, KC)
                for fj in range(FJ):
                    up(0, fj, None if fj < 2 else fj - 1)

                def expert(e, last, first):
                    for j in range(GE):
                        end = last and j == GE - 1
                        for fj in range(FJ):
                            if fj == 0:
                                if not first or j >= 2:
                                    pe.wait_ge(f.y, (e * GE + j - 1) * GT)
                            if j == 0:
                                pe.wait_ge(f.w2l, e * FJ + fj + 1)
                            pe.wait_ge(f.hl, (e * GE + j) * FJ + fj + 1)
                            down(j, fj)
                            if not end:
                                if fj == 0:
                                    pe.wait_ge(f.xl, (e * GE + j + 2) * KC)
                                if j == GE - 1:
                                    pe.wait_ge(f.w1l, (e + 1) * FJ + fj + 1)
                                up((j + 1) % GE, fj, (e * GE + j + 1) * FJ + fj - 1)
                            if fj == 5 and not (last and j + 2 >= GE):
                                jj = (j + 2) % GE
                                transposes(jj, (e * (GE // 2) + (j + 2) // 2 + 1) * GT * 16, (e * GE + j + 2) * KC)

                expert(0, False, True)
                with pe.Fori(1, E - 1) as e:
                    expert(e, False, False)
                expert(E - 1, True, False)

            pe.wait_ge(R[0].sm_r, 2 * B + 1)
            pe.wait_ge(R[0].trp_r, N // P + 2)
            ffn(0)

            c1, c2, cs = Count(), Count(), Count()
            shared = (c1, c2)
            frees = (A.v_r, A.t_r)
            fulls = (A.v, A.t)

            def front(b):
                for t in range(NT):
                    pe.wait_ge(A.xn, b * NT + t + 2)
                    pe.wait_ge(frees[t % 2], shared[t % 2].up())
                    for k in range(KC):
                        last = pe.transpose(bank[1 + t % 2][:, k * P:(k + 1) * P], xn_f[:, t % 2, k * P:(k + 1) * P], ident)
                    last.then_inc(fulls[t % 2], 1)

            def tiles(b):
                def project(i):
                    s = slice(i * P, (i + 1) * P)
                    if i == 0:
                        pe.wait_ge(A.f, b * NT + NT)
                    pe.wait_ge(A.qk_r, b * NT + i + 1)
                    for k in range(KC):
                        last = pe.matmul(bank[0][:], xnT[:, k, s], wqkT[:, k, :], start=(k == 0), stop=(k == KC - 1))
                    last.then_inc(A.qk, 1)
                    pe.wait_ge(A.v_r, c1.up())
                    for k in range(KC):
                        last = pe.matmul(bank[1][:, 0:C], xnT[:, k, s], wvT[:, k, :], start=(k == 0), stop=(k == KC - 1))
                    last.then_inc(A.v, 1)

                def scores(i, q):
                    half, four = q % 2, q // 2
                    if four == 0:
                        pe.wait_ge(A.kmd, b * NT + i + 1)
                    else:
                        pe.wait_ge(A.kma, b * NT + i + 1)
                    pe.wait_ge(A.sc_r, cs.up())
                    for m in range(4):
                        last = pe.matmul(bank[3 + q % 2][:, m * P:(m + 1) * P], km[:, half, four * 4 + m, :],
                                         qkT[:, half, :], start=True, stop=True)
                    last.then_inc(A.sc, 1)

                def attend(i, q):
                    half, four = q % 2, q // 2
                    pe.wait_ge(A.aw, (b * NT + i) * 4 + q + 1)
                    for m in range(4):
                        h = half * HH + four * 4 + m
                        r = 32 * ((four * 4 + m) // 2)
                        last = pe.matmul(bank[5][r:r + 32, half * P:(half + 1) * P], vz[:, i % 2, h * 32:(h + 1) * 32],
                                         aw[:, q, m, :], start=False, stop=(m % 2 == 1), skip_group_check=True)
                    if q == 3:
                        last.then_inc(A.y, 1)

                project(0)
                for i in range(NT):
                    pe.wait_ge(A.roped, b * NT + i + 1)
                    pe.wait_ge(A.t_r, c2.up())
                    for n in range(2 * KC):
                        last = pe.transpose(bank[2][:, n * P:(n + 1) * P], qk[:, i % 2, n * P:(n + 1) * P], ident)
                    last.then_inc(A.t, 1)
                    if i + 1 < NT:
                        project(i + 1)
                    else:
                        for n in range(4):
                            m, half = n // 2, n % 2
                            pe.wait_ge(frees[n % 2], shared[n % 2].up())
                            for k in range(KC):
                                last = pe.matmul(bank[1 + n % 2][:], wgT[:, k, m * P:(m + 1) * P], xnT[:, k, half * 512:(half + 1) * 512],
                                                 start=(k == 0), stop=(k == KC - 1))
                            last.then_inc(fulls[n % 2], 1)
                    scores(i, 0)
                    scores(i, 1)
                    pe.wait_ge(A.stt, b * NT + i + 1)
                    pe.wait_ge(A.y_r, b * NT + i + 1)
                    for k in range(KC):
                        last = pe.matmul(bank[5][:, k * P:(k + 1) * P], state[:, k, :], qkT[:, k, :],
                                         start=(k == 0), stop=False, skip_group_check=True)
                    pe.wait_ge(A.vz, b * NT + i + 1)
                    pe.wait_ge(A.st_r, b * NT + i + 1)
                    for k in range(KC):
                        v = vz[:, i % 2, k * HH * 32:(k + 1) * HH * 32].rearrange("p (m x) -> p m x", x=64)
                        v = v.rearrange("p m (a y) -> p m a y", y=16)[:, :, 0:4:3, :]
                        last = pe.matmul(bank[6][:, k * P:(k + 1) * P], qk[:, i % 2, C + k * P:C + (k + 1) * P], v, start=True, stop=True)
                    last.then_inc(A.st, 1)
                    attend(i, 0)
                    scores(i, 2)
                    attend(i, 1)
                    scores(i, 3)
                    attend(i, 2)
                    attend(i, 3)

            def tail(b):
                pe.wait_ge(A.gmv, b + 1)
                pe.wait_ge(R[1].sm_r, b * 2 + 1)
                pe.matmul(bank[7][:, 0:KC], headmean, gmv[:, :, 0], start=True, stop=True).then_inc(A.gs, 1)
                pe.wait_ge(A.gs_r, b + 1)
                pe.matmul(bank[7][:, 0:KC], headmean, gsm[:, 1, :], start=True, stop=True).then_inc(A.gs, 1)
                for t in range(NT):
                    if t == 0:
                        pe.wait_ge(A.gated, b * KC + KC)
                    pe.wait_ge(A.sc_r, cs.up())
                    for k in range(KC):
                        last = pe.matmul(bank[3 + t % 2][:, 0:C], yT[:, k, t * P:(t + 1) * P], wpT[:, k, :],
                                         start=(k == 0), stop=(k == KC - 1))
                    last.then_inc(A.sc, 1)
                pe.wait_ge(A.grv, b + 1)
                route(1, b, lambda t: pe.wait_ge(frees[t % 2], shared[t % 2].up()), lambda t: fulls[t % 2])

            per = {c1: NT + 2 + NT, c2: NT + 2 + NT, cs: NT * 4 + NT}
            pe.wait_ge(F[0].y, NG * GT)
            front(0)
            with pe.Fori(0, B - 1) as b:
                for c in per:
                    c.enter(b, per[c])
                tiles(b)
                front(b + 1)
                tail(b)
            for c in per:
                c.leave(B - 1)
            tiles(B - 1)
            tail(B - 1)
            pe.wait_ge(R[1].sm_r, 2 * B + 1)
            ffn(1)

        @block.scalar
        def _(act):
            dst = [wqkT[:, :, (j * P):(j + 1) * P] for j in range(4)] + [wvT[:, :, j * P:(j + 1) * P] for j in range(2)] \
                + [wgT[:, :, j * P:(j + 1) * P] for j in range(2)] + [wpT[:, :, j * P:(j + 1) * P] for j in range(2)]
            for n in range(20):
                act.wait_ge(S0.wT, n + 1)
                act.activation(dst[n // KC][:, n % KC, :], bank[n % 4][:, 0:P], ACT.Copy).then_inc(S0.wTc, 1)
            act.sem_inc(R[0].trp_r, 2)

            def normalise(S, ln, src, dst, t):
                act.activation(dst[:, t % 2, :], src[:, t, :], ACT.Identity, bias=ln.nm[:, t:t + 1], scale=ln.rs[:, t:t + 1])\
                    .then_inc(S.xn, 1)

            def route(r, b, tr_full, tr_read):
                S = R[r]
                act.wait_ge(S.lnnm, b + 1)
                for t in range(NT + 1):
                    if t < NT:
                        if t >= 2:
                            act.wait_ge(S.ready, b * NT + t - 1)
                            act.wait_ge(S.xT, b * NT + t - 1)
                        normalise(S, lnr, xr, xn_r, t)
                    if t >= 1:
                        evac(S, b, t - 1, tr_full, tr_read)
                act.wait_ge(S.link, b * LINKS + EXP_LINK)
                act.activation(ex[:], dl[:], ACT.Exp).then_inc(S.exp, 1)

            def evac(S, b, t, tr_full, tr_read):
                tr_full(t)
                if t >= 2:
                    act.wait_ge(S.xT_r, b * (NT - 1) + t - 1)
                act.activation(xrT[:, t % 2, :, :], bank[1 + t % 2][:, 0:KC * P].rearrange("p (k x) -> p k x", k=KC), ACT.Copy)\
                    .then_inc(S.xT, 1)
                tr_read(t)

            with act.Fori(0, B) as b:
                route(0, b, lambda t: act.wait_ge(R[0].trp, b * NT + t + 1),
                      lambda t: (act.wait_ge(R[0].xT, b * NT + t + 1), act.sem_inc(R[0].trp_r, 1)))

            def ffn(r):
                f = F[r]

                def split_x(j, xT_value):
                    act.wait_ge(f.xT, xT_value)
                    for k in range(KC):
                        act.activation(xh[j % 2][:, k, :], bank[6 + k][:], ACT.Copy).then_inc(f.xh, 1)

                def gelu(j, fj, up_value, lo_value):
                    act.wait_ge(f.up, up_value)
                    if lo_value is not None:
                        act.wait_ge(f.hl, lo_value)
                    act.activation(h32[fj % 2], bank[fj % 2][:], ACT.Gelu_apprx_tanh).then_inc(f.gelu, 1)

                def high1(fj):
                    w = slice(fj * P, (fj + 1) * P)
                    act.activation(w1h[:, :, w], stg1[:, :, w], ACT.Copy).then_inc(f.w1h, 1)

                def high2(fj):
                    act.activation(w2h[:, fj, :], stg2[:, fj, :], ACT.Copy).then_inc(f.w2h, 1)

                def weigh(e, j):
                    act.wait_ge(f.down, e * GE + j + 1)
                    if not (isinstance(e, int) and e == 0 and j < 2):
                        act.wait_ge(f.add, (e * GE + j - 1) * GT * 16)
                    for t in range(GT):
                        act.activation(yb[j % 2][:, t, :], bank[2 + 2 * (j % 2) + t // 2][:, (t % 2) * C:(t % 2 + 1) * C],
                                       ACT.Copy, scale=tab[:, j, t, 1:2]).then_inc(f.y, 1)

                act.wait_ge(f.w1raw, 16)
                for fj in range(FJ):
                    high1(fj)
                split_x(0, 1)
                act.wait_ge(f.w2raw, 16)
                for fj in range(FJ):
                    high2(fj)
                split_x(1, 2)
                for fj in range(FJ):
                    gelu(0, fj, fj + 1, None if fj < 2 else fj - 1)

                def expert(e, last):
                    for j in range(GE):
                        for fj in range(FJ):
                            if not (last and j == GE - 1):
                                g1 = (e * GE + j + 1) * FJ + fj
                                gelu((j + 1) % GE, fj, g1 + 1, g1 - 1)
                            if not last and j == GE - 2:
                                if fj == 0:
                                    act.wait_ge(f.w1raw, e * 16 + 32)
                                high1(fj)
                            if not last and j == GE - 1:
                                if fj == 0:
                                    act.wait_ge(f.w2raw, e * 16 + 32)
                                high2(fj)
                            if fj == 5 and not (last and j + 2 >= GE):
                                split_x((j + 2) % GE, e * GE + j + 3)
                        weigh(e, j)

                expert(0, False)
                with act.Fori(1, E - 1) as e:
                    expert(e, False)
                expert(E - 1, True)

            ffn(0)

            c1, c2 = Count(), Count()
            shared, fulls, frees = (c1, c2), (A.v, A.t), (A.v_r, A.t_r)
            act.sem_inc(A.v_r, 1)
            act.sem_inc(A.t_r, 1)
            act.sem_inc(A.y_r, 1)

            def front(b):
                act.wait_ge(A.lnnm, b + 1)
                for t in range(NT + 1):
                    if t < NT:
                        if t >= 2:
                            act.wait_ge(A.f, b * NT + t - 1)
                        normalise(A, lnf, xb, xn_f, t)
                    if t >= 1:
                        u = t - 1
                        act.wait_ge(fulls[u % 2], shared[u % 2].up())
                        act.activation(xnT[:, :, u * P:(u + 1) * P], bank[1 + u % 2][:, 0:C].rearrange("p (k x) -> p k x", k=KC), ACT.Copy)\
                            .then_inc(A.f, 1)
                        act.wait_ge(A.f, b * NT + u + 1)
                        act.sem_inc(frees[u % 2], 1)

            def tiles(b):
                def values(i):
                    act.wait_ge(A.v, c1.up())
                    if i >= 2:
                        act.wait_ge(A.y, b * NT + i - 1)
                    dst = vz[:, i % 2, :].rearrange("p (m a y) -> p m a y", a=4, y=D)[:, :, 0:4:3, :]
                    act.activation(dst, bank[1][:, 0:C].rearrange("p (m a y) -> p m a y", a=2, y=D), ACT.Copy).then_inc(A.vz, 1)
                    act.wait_ge(A.vz, b * NT + i + 1)
                    act.sem_inc(A.v_r, 1)

                values(0)
                for i in range(NT):
                    act.wait_ge(A.t, c2.up())
                    act.activation(qkT[:, :, :], bank[2][:].rearrange("p (n x) -> p n x", x=P), ACT.Copy).then_inc(A.qkT, 1)
                    act.wait_ge(A.qkT, b * NT + i + 1)
                    act.sem_inc(A.t_r, 1)
                    if i:
                        act.wait_ge(A.y, b * NT + i)
                    for m in range(4, HH):
                        last = act.activation(km[:, :, m, :], qkT[:, KC:2 * KC, :], ACT.Copy, scale=K_["headsel"][:, m:m + 1])
                    last.then_inc(A.kma, 1)
                    if i + 1 < NT:
                        values(i + 1)
                    else:
                        for n in range(4):
                            m, half = n // 2, n % 2
                            act.wait_ge(fulls[n % 2], shared[n % 2].up())
                            act.activation(gT[:, m, half * 512:(half + 1) * 512], bank[1 + n % 2][:], ACT.Silu).then_inc(A.g, 1)
                            act.wait_ge(A.g, b * 4 + n + 1)
                            act.sem_inc(frees[n % 2], 1)
                    act.wait_ge(A.y, b * NT + i + 1)
                    act.activation(yT[:, :, i * P:(i + 1) * P], bank[5][:, 0:C].rearrange("p (k x) -> p k x", k=KC), ACT.Copy)\
                        .then_inc(A.y_r, 1)

            def tail(b):
                act.wait_ge(A.gaff, b + 1)
                for k in range(KC):
                    act.activation(yT[:, k, :], yT[:, k, :], ACT.Identity, bias=gsm[:, 6, k:k + 1], scale=gsm[:, 4, k:k + 1])\
                        .then_inc(A.yg, 1)
                route(1, b, lambda t: act.wait_ge(fulls[t % 2], shared[t % 2].up()),
                      lambda t: (act.wait_ge(R[1].xT, b * NT + t + 1), act.sem_inc(frees[t % 2], 1)))

            per = {c1: NT + 2 + NT, c2: NT + 2 + NT}
            front(0)
            with act.Fori(0, B - 1) as b:
                for c in per:
                    c.enter(b, per[c])
                tiles(b)
                front(b + 1)
                tail(b)
            for c in per:
                c.leave(B - 1)
            tiles(B - 1)
            tail(B - 1)
            ffn(1)

        @block.vector
        def _(dve):
            def bc(ap, shape):
                return ap.to_broadcast(shape)

            dve.wait_ge(S0.vec, 80)
            dve.tensor_scalar(hbias[:], hbias[:], 0.5, None, ALU.mult).then_inc(S0.bias, 1)
            dve.wait_ge(S0.bias, 1)
            dve.wait_ge(S0.const, 16)

            def norm_stats(S, ln, x, b, before_tile=None):
                for t in range(NT):
                    if before_tile:
                        before_tile(t)
                    dve.bn_stats(ln.st[:, t, :], x[:, t, :]).then_inc(S.lnst, 1)
                dve.wait_ge(S.lnst, b * NT + NT)
                mean, sq = (lambda a: ln.st[:, :, 3 * a + 1]), (lambda a: ln.st[:, :, 3 * a + 2])
                dve.tensor_tensor(ln.mv[:, 0], mean(0), mean(1), ALU.add).then_inc(S.lnmv, 1)
                dve.tensor_tensor(ln.mv[:, 1], mean(0), mean(1), ALU.subtract).then_inc(S.lnmv, 1)
                dve.tensor_tensor(ln.mv[:, 2], sq(0), sq(1), ALU.add).then_inc(S.lnmv, 1)
                dve.wait_ge(S.lnmv, b * LN_STEPS + 2)
                dve.tensor_tensor(ln.mv[:, 3], ln.mv[:, 1], ln.mv[:, 1], ALU.mult).then_inc(S.lnmv, 1)
                dve.wait_ge(S.lnmv, b * LN_STEPS + 4)
                dve.scalar_tensor_tensor(ln.mv[:, 4], ln.mv[:, 3], C / 4.0, ln.mv[:, 2], ALU.mult, ALU.add).then_inc(S.lnmv, 1)
                dve.wait_ge(S.lnmv, b * LN_STEPS + LN_STEPS)
                dve.tensor_scalar(ln.rv[:], ln.mv[:, 4], 1.0 / C, EPS, ALU.mult, ALU.add).then_inc(S.lnrv, 1)
                dve.wait_ge(S.lnrs, b + 1)
                dve.scalar_tensor_tensor(ln.nm[:], ln.mv[:, 0], -0.5, ln.rs[:], ALU.mult, ALU.mult).then_inc(S.lnnm, 1)

            def half_bias(S, b):
                dve.wait_ge(S.xn, b * NT + NT)
                dve.tensor_tensor(xr[:], xr[:], hbias[:].unsqueeze(1).to_broadcast([P, NT, C]), ALU.add).then_inc(S.half, 1)

            def choose(r, b):
                S = R[r]
                n = [0]

                def link(ins):
                    ins.then_inc(S.link, 1)
                    n[0] += 1
                    dve.wait_ge(S.link, b * LINKS + n[0])

                te = [P, NT, E]
                over_t = lambda a: a.unsqueeze(1).to_broadcast(te)
                over_e = lambda a: a.unsqueeze(2).to_broadcast(te)
                dve.wait_ge(S.sm, b * 2 + 1)
                dve.tensor_copy(lg[:], bank[7][:, 0:NT * E].rearrange("p (t e) -> p t e", e=E)).then_inc(S.sm_r, 1)
                dve.wait_ge(S.sm_r, b * 2 + 2)
                link(dve.tensor_reduce(red[:, 0, :], lg[:], AX.X, ALU.max))
                link(dve.tensor_tensor(dl[:], lg[:], over_e(red[:, 0, :]), ALU.subtract))
                link(dve.tensor_scalar(dl[:], dl[:], -87.0, None, ALU.max))
                assert n[0] == EXP_LINK
                link(dve.scalar_tensor_tensor(key[:, 0], dl[:], 0.0, over_t(K_["revexp"]), ALU.is_ge, ALU.mult))
                link(dve.tensor_reduce(sel[:, 0, 0:NT], key[:, 0], AX.X, ALU.max))
                link(dve.tensor_tensor(oh[:, 0], key[:, 0], over_e(sel[:, 0, 0:NT]), ALU.is_equal))
                link(dve.scalar_tensor_tensor(d2[:], oh[:, 0], -1.0e30, dl[:], ALU.mult, ALU.add))
                link(dve.tensor_reduce(red[:, 1, :], d2[:], AX.X, ALU.max))
                link(dve.tensor_tensor(key[:, 1], d2[:], over_e(red[:, 1, :]), ALU.is_equal))
                link(dve.tensor_tensor(key[:, 1], key[:, 1], over_t(K_["revexp"]), ALU.mult))
                link(dve.tensor_reduce(sel[:, 0, NT:RT], key[:, 1], AX.X, ALU.max))
                link(dve.tensor_tensor(oh[:, 1], key[:, 1], over_e(sel[:, 0, NT:RT]), ALU.is_equal))
                assert n[0] == OH_LINK
                dve.wait_ge(S.exp, b + 1)
                link(dve.tensor_reduce(red[:, 2, :], ex[:], AX.X, ALU.add))
                link(dve.reciprocal(red[:, 3, :], red[:, 2, :]))
                for k in range(TOPK):
                    link(dve.tensor_tensor(key[:, k], oh[:, k], ex[:], ALU.mult))
                link(dve.tensor_reduce(sel[:, 1, :], key[:].rearrange("p k t e -> p (k t) e"), AX.X, ALU.add))
                kt = lambda a: a.rearrange("p (k t) -> p k t", k=TOPK)
                link(dve.tensor_tensor(kt(sel[:, 2, :]), kt(sel[:, 1, :]), red[:, 3, :].unsqueeze(1).to_broadcast([P, TOPK, NT]), ALU.mult))
                dve.wait_ge(S.sm, b * 2 + 2)
                ahead = bank[7][:, 0:RT * E].rearrange("p (k t e) -> p k t e", k=TOPK, t=NT)
                whole = bank[7][:, RT * E:2 * RT * E].rearrange("p (k t e) -> p k t e", k=TOPK, t=NT)
                for k in range(TOPK):
                    link(dve.tensor_copy(cnt[:, k].rearrange("p e t -> p t e"), whole[:, k]))
                flat = lambda a: a.rearrange("p k e t -> p (k e t)")
                link(dve.tensor_tensor_scan(flat(scn[:]), K_["restart"], flat(cnt[:]), 0.0, ALU.mult, ALU.add))
                dve.tensor_tensor(pos[:, 0], ahead[:, 0], cnt[:, 0].rearrange("p e t -> p t e"), ALU.subtract)
                dve.tensor_tensor(pos[:, 1], ahead[:, 1], cnt[:, 1].rearrange("p e t -> p t e"), ALU.subtract).then_inc(S.sm_r, 1)
                dve.wait_ge(S.sm_r, b * 2 + 3)
                for k in range(TOPK):
                    link(dve.tensor_tensor(pos[:, k], pos[:, k], scn[:, k].rearrange("p e t -> p t e"), ALU.add))
                for k in range(TOPK):
                    link(dve.tensor_tensor(pos[:, k], pos[:, k], over_t(base[:, k, :]), ALU.add))
                link(dve.tensor_tensor(base[:], base[:], scn[:, :, :, NT - 1], ALU.add))
                link(dve.tensor_tensor(pos[:], pos[:], oh[:], ALU.mult))
                link(dve.tensor_reduce(sel[:, 3, :], pos[:].rearrange("p k t e -> p (k t) e"), AX.X, ALU.add))
                link(dve.tensor_scalar(sel[:, 4, :], sel[:, 3, :], float(CAP), None, ALU.is_lt))
                link(dve.scalar_tensor_tensor(sel[:, 5, :], sel[:, 0, :], -float(TOPK * CAP), sel[:, 3, :], ALU.mult, ALU.add))
                link(dve.tensor_tensor(sel[:, 5, :], sel[:, 5, :], K_["slotbase"], ALU.add))
                link(dve.tensor_scalar(sel[:, 6, :], sel[:, 4, :], -BIG, BIG, ALU.mult, ALU.add))
                dve.wait_ge(S.sent, b + 1)
                link(dve.tensor_tensor(idx[:], sel[:, 5, :], sel[:, 6, :], ALU.add))
                link(dve.scalar_tensor_tensor(pay[:, :, 1], sel[:, 2, :], 0.5, sel[:, 4, :], ALU.mult, ALU.mult))
                link(dve.tensor_copy(pay[:].bitcast(u32).rearrange("p (k t) w -> p k t w", k=TOPK)[:, :, :, 0],
                                     ids[:].unsqueeze(1).to_broadcast([P, TOPK, NT])))
                dve.wait_ge(S.xnst, (b * NT + NT) * 16)
                dve.tensor_scalar(ids[:], ids[:], float(T), None, ALU.add).then_inc(S.pay, 1)
                dve.wait_ge(S.pay, b + 1)
                assert n[0] == LINKS, n[0]

            def start_route(r):
                dve.memset(base[:], 0.0).then_inc(S0.base, 1)
                dve.tensor_copy(ids[:], K_["ids"]).then_inc(S0.base, 1)
                dve.wait_ge(S0.base, 2 * r + 2)
                dve.sem_inc(R[r].sm_r, 1)
                dve.sem_inc(R[r].sent, 1)

            start_route(0)
            with dve.Fori(0, B) as b:
                dve.wait_ge(R[0].x, b * 16 + 16)
                norm_stats(R[0], lnr, xr, b)
                half_bias(R[0], b)
                choose(0, b)

            def ffn(r):
                f = F[r]

                def split_x(j, xh_value):
                    for k in range(KC):
                        dve.wait_ge(f.xh, xh_value + k)
                        dve.tensor_tensor(xl[j % 2][:, k, :], bank[6 + k][:], xh[j % 2][:, k, :].bitcast(fp32), ALU.subtract).then_inc(f.xl, 1)

                def low1(fj, value):
                    w = slice(fj * P, (fj + 1) * P)
                    dve.wait_ge(f.w1h, value)
                    dve.tensor_tensor(w1l[:, :, w], stg1[:, :, w], w1h[:, :, w].bitcast(fp32), ALU.subtract).then_inc(f.w1l, 1)

                def low2(fj, value):
                    dve.wait_ge(f.w2h, value)
                    dve.tensor_tensor(w2l[:, fj, :], stg2[:, fj, :], w2h[:, fj, :].bitcast(fp32), ALU.subtract).then_inc(f.w2l, 1)

                def high(fj, value):
                    dve.wait_ge(f.gelu, value)
                    dve.tensor_copy(hh[:, fj, :], h32[fj % 2]).then_inc(f.hh, 1)

                def low(fj, value):
                    dve.wait_ge(f.hh, value)
                    dve.tensor_tensor(hl[:, fj, :], h32[fj % 2], hh[:, fj, :].bitcast(fp32), ALU.subtract).then_inc(f.hl, 1)

                for fj in range(FJ):
                    low1(fj, fj + 1)
                split_x(0, 1)
                for fj in range(FJ):
                    low2(fj, fj + 1)
                split_x(1, KC + 1)
                for fj in range(FJ):
                    high(fj, fj + 1)
                    low(fj, fj + 1)

                def expert(e, last):
                    for j in range(GE):
                        for fj in range(FJ):
                            go = not (last and j == GE - 1)
                            value = (e * GE + j + 1) * FJ + fj + 1
                            if go:
                                high(fj, value)
                            if not last and j == GE - 2:
                                low1(fj, (e + 1) * FJ + fj + 1)
                            if not last and j == GE - 1:
                                low2(fj, (e + 1) * FJ + fj + 1)
                            if go:
                                low(fj, value)
                            if fj == 5 and not (last and j + 2 >= GE):
                                split_x((j + 2) % GE, (e * GE + j + 2) * KC + 1)

                expert(0, False)
                with dve.Fori(1, E - 1) as e:
                    expert(e, False)
                expert(E - 1, True)

            ffn(0)

            cs = Count()
            dve.sem_inc(A.qk_r, 1)
            dve.sem_inc(A.sc_r, 2)
            dve.sem_inc(A.st_r, 1)

            def front(b):
                dve.wait_ge(A.x, b * 16 + 16)
                norm_stats(A, lnf, xb, b)

            def tiles(b):
                dve.memset(state[:], 0.0).then_inc(A.state0, 1)
                dve.wait_ge(A.state0, b + 1)
                dve.sem_inc(A.stt, 1)

                def rotate(i):
                    nb = b * NT + i
                    dve.wait_ge(A.qk, nb + 1)
                    if i >= 2:
                        dve.wait_ge(A.st, nb - 1)
                    two = lambda a: a.rearrange("p (c w) -> p c w", w=2)
                    dve.tensor_tensor(rt1, bank[0][:], rope[:, i, 0, :], ALU.mult)
                    dve.tensor_tensor(two(rt2)[:, :, 0], two(bank[0][:])[:, :, 1], two(rope[:, i, 1, :])[:, :, 0], ALU.mult)
                    dve.tensor_tensor(two(rt2)[:, :, 1], two(bank[0][:])[:, :, 0], two(rope[:, i, 1, :])[:, :, 1], ALU.mult).then_inc(A.qk_r, 1)
                    dve.wait_ge(A.qk_r, nb + 2)
                    dve.tensor_tensor(qk[:, i % 2, :], rt1, rt2, ALU.add).then_inc(A.roped, 1)
                    dve.wait_ge(A.roped, nb + 1)

                def mask(i, q):
                    dve.wait_ge(A.sc, cs.up())
                    if i:
                        dve.wait_ge(A.y, b * NT + i)
                    dve.tensor_tensor(aw[:, q], bank[3 + q % 2][:].rearrange("p (m x) -> p m x", m=4),
                                      causal.unsqueeze(1).to_broadcast([P, 4, P]), ALU.mult).then_inc(A.aw, 1)
                    dve.wait_ge(A.aw, (b * NT + i) * 4 + q + 1)
                    dve.sem_inc(A.sc_r, 1)

                dve.wait_ge(S0.rope, NT * 16)
                rotate(0)
                for i in range(NT):
                    nb = b * NT + i
                    dve.wait_ge(A.qkT, nb + 1)
                    if i:
                        dve.wait_ge(A.y, nb)
                    for m in range(4):
                        last = dve.tensor_scalar(km[:, :, m, :], qkT[:, KC:2 * KC, :], K_["headsel"][:, m:m + 1], None, ALU.mult)
                    last.then_inc(A.kmd, 1)
                    if i + 1 < NT:
                        rotate(i + 1)
                    mask(i, 0)
                    mask(i, 1)
                    dve.wait_ge(A.st, nb + 1)
                    dve.tensor_tensor(stmp[:], bank[6][:, 0:C].rearrange("p (k x) -> p k x", k=KC),
                                      K_["stateblk"].rearrange("p (k x) -> p k x", k=KC), ALU.mult).then_inc(A.st_r, 1)
                    dve.wait_ge(A.st_r, nb + 2)
                    if i + 1 < NT:
                        for k in range(KC):
                            last = dve.scalar_tensor_tensor(state[:, k, :], state[:, k, :], K_["decay"][:, k:k + 1], stmp[:, k, :],
                                                            ALU.mult, ALU.add)
                        last.then_inc(A.stt, 1)
                        dve.wait_ge(A.stt, nb + 2)
                    mask(i, 2)
                    mask(i, 3)

            def tail(b):
                for k in range(KC):
                    for n in range(2):
                        if n == 0 and k == 0:
                            dve.wait_ge(A.y_r, b * NT + NT + 1)
                        dve.bn_stats(gst[:, k, n, :], yT[:, k, n * 512:(n + 1) * 512]).then_inc(A.gst, 1)
                n = [0]

                def link(ins):
                    ins.then_inc(A.glink, 1)
                    n[0] += 1
                    dve.wait_ge(A.glink, b * GLINKS + n[0])

                part = gst[:].rearrange("p k n (a s) -> p k (n a) s", s=3)
                dve.wait_ge(A.gst, b * 4 + 4)
                link(dve.tensor_reduce(gsm[:, 7, :], part[:, :, :, 1], AX.X, ALU.add))
                dve.tensor_scalar(gmv[:, :, 0], gsm[:, 7, :], 0.25, None, ALU.mult).then_inc(A.gmv, 1)
                dve.wait_ge(A.gmv, b + 1)
                link(dve.tensor_tensor(gdv[:], part[:, :, :, 1], gmv[:, :, 0:1].to_broadcast([P, KC, 4]), ALU.subtract))
                link(dve.tensor_tensor(gdv[:], gdv[:], gdv[:], ALU.mult))
                link(dve.scalar_tensor_tensor(gdv[:], gdv[:], T / 4.0, part[:, :, :, 2], ALU.mult, ALU.add))
                dve.tensor_reduce(gmv[:, :, 1], gdv[:], AX.X, ALU.add).then_inc(A.gst2, 1)
                dve.wait_ge(A.gs, b * 2 + 1)
                link(dve.tensor_copy(gsm[:, 0, :], bank[7][:, 0:KC]))
                link(dve.tensor_tensor(gsm[:, 1, :], gmv[:, :, 0], gsm[:, 0, :], ALU.subtract))
                link(dve.tensor_tensor(gsm[:, 1, :], gsm[:, 1, :], gsm[:, 1, :], ALU.mult))
                dve.wait_ge(A.gst2, b + 1)
                dve.scalar_tensor_tensor(gsm[:, 1, :], gmv[:, :, 1], 1.0 / T, gsm[:, 1, :], ALU.mult, ALU.add).then_inc(A.gs_r, 1)
                dve.wait_ge(A.gs, b * 2 + 2)
                dve.tensor_scalar(gsm[:, 2, :], bank[7][:, 0:KC], EPS, None, ALU.add).then_inc(A.grv, 1)
                dve.wait_ge(A.grs, b + 1)
                link(dve.tensor_tensor(gsm[:, 4, :], gsm[:, 3, :], gnw[:], ALU.mult))
                link(dve.tensor_tensor(gsm[:, 5, :], gsm[:, 0, :], gsm[:, 4, :], ALU.mult))
                assert n[0] == GLINKS
                dve.tensor_tensor(gsm[:, 6, :], gnb[:], gsm[:, 5, :], ALU.subtract).then_inc(A.gaff, 1)
                for k in range(KC):
                    dve.wait_ge(A.yg, b * KC + k + 1)
                    if k == 0:
                        dve.wait_ge(A.g, b * 4 + 4)
                    dve.tensor_tensor(yT[:, k, :], yT[:, k, :], gT[:, k, :], ALU.mult).then_inc(A.gated, 1)

                def residual(t):
                    if t == 0:
                        dve.wait_ge(R[1].x, b * 16 + 16)
                    dve.wait_ge(A.sc, cs.up())
                    dve.tensor_tensor(xr[:, t, :], xr[:, t, :], bank[3 + t % 2][:, 0:C], ALU.add).then_inc(R[1].o, 1)
                    dve.wait_ge(R[1].o, b * NT + t + 1)
                    dve.sem_inc(A.sc_r, 1)

                norm_stats(R[1], lnr, xr, b, residual)
                half_bias(R[1], b)
                choose(1, b)

            start_route(1)
            front(0)
            per = {cs: NT * 4 + NT}
            with dve.Fori(0, B - 1) as b:
                for c in per:
                    c.enter(b, per[c])
                tiles(b)
                front(b + 1)
                tail(b)
            for c in per:
                c.leave(B - 1)
            tiles(B - 1)
            tail(B - 1)
            ffn(1)


EXP_LINK, OH_LINK, LINKS = 3, 12, 35
GLINKS = 9
LN_STEPS = 5


def shape_constants():
    p = np.arange(P)
    h = np.arange(H, dtype=np.float32)
    gamma = (np.float32(1.0) - np.float32(2.0) ** (np.float32(-5.0) - h)).astype(np.float64)
    at, n = const_at()
    c = np.zeros((P, n), np.float32)

    def put(name, a):
        c[:, at[name][0]:at[name][1]] = a

    head = p // D
    put("ident", np.eye(P))
    put("before", p[:, None] < p[None, :])
    put("causal", p[:, None] <= p[None, :])
    same = head[:, None] == head[None, :]
    put("headmean", same / D)
    decay = np.stack([gamma[k * HH + head] ** P for k in range(KC)], 1)
    put("stateblk", np.concatenate([same * decay[:, k:k + 1] for k in range(KC)], 1))
    put("headsel", head[:, None] == np.arange(HH)[None, :])
    put("decay", decay)
    put("revexp", (E - np.arange(E))[None, :])
    put("restart", (np.arange(RT * E) % NT != 0)[None, :])
    put("slotbase", (E * TOPK * CAP + np.arange(RT) // NT * CAP)[None, :])
    put("mhalf", -0.5)
    put("ids", np.arange(NT)[None, :] * P + p[:, None])
    half = np.arange(0, D, 2, dtype=np.float32)
    inv = (np.float32(1.0) / np.float32(10000.0) ** (half / np.float32(D))).astype(np.float32)
    t = np.arange(T, dtype=np.float32)
    ang = (t[:, None] * inv[None, :]).astype(np.float32).astype(np.float64)
    vec = ((half + np.float32(0.4 * D)) / np.float32(1.4 * D)).astype(np.float64)
    scale = vec[None, :] ** ((t.astype(np.float64) - T // 2) / 512.0)[:, None]
    tau = (np.arange(T) % P).astype(np.float64)
    rope = np.zeros((T, 2, 2, H, D))
    for w, s, g in ((0, scale * D ** -0.5, tau), (1, 1.0 / scale, -tau)):
        dec = gamma[None, :] ** g[:, None]
        for half_ in range(2):
            rope[:, 0, w, :, half_::2] = (np.cos(ang) * s)[:, None, :] * dec[:, :, None]
            rope[:, 1, w, :, half_::2] = (np.sin(ang) * s * (-1.0 if half_ == 0 else 1.0))[:, None, :] * dec[:, :, None]
    rope = rope.reshape(NT, P, 2, 2 * C).astype(np.float32)
    slots = np.zeros((SLOTS, 2), np.uint32)
    slots[:, 0] = N + np.arange(SLOTS) % G
    return c, rope, slots.view(np.float32)


_INS = ["L0_attn_x", "L0_attn_w_qkv", "L0_attn_w_gated", "L0_attn_w_proj", "L0_attn_gn_weight", "L0_attn_gn_bias",
        "L0_ffn_router_w", "L0_ffn_w1", "L0_ffn_w2", "L0_ffn_bias"]


def kernel(**inputs):
    import concourse.bacc as bacc
    from concourse.bass_utils import run_bass_kernel_spmd

    nc = bacc.Bacc("TRN2", target_bir_lowering=False, num_devices=1)
    arrays = {name: np.ascontiguousarray(inputs[name]) for name in _INS}
    arrays["L0_attn_x"] = arrays["L0_attn_x"].reshape(N, C)
    arrays["consts"], arrays["rope"], arrays["slots"] = shape_constants()
    args = [nc.dram_tensor(f"in_{n}", a.shape, mybir.dt.from_np(a.dtype), kind="ExternalInput").ap() for n, a in arrays.items()]
    out = nc.dram_tensor("out_rows", (ROWS, C), DT.float32, kind="ExternalOutput").ap()
    macaron_kernel(nc, *args, out)
    r = run_bass_kernel_spmd(nc, [{f"in_{n}": a for n, a in arrays.items()}], core_ids=[0])
    return r.results[0]["out_rows"][0:N].reshape(B, T, C)
```

```python
import numpy as np
import concourse.bass as bass
from concourse import mybir
from contextlib import ExitStack

DT = mybir.dt
ALU = mybir.AluOpType
ACT = mybir.ActivationFunctionType
AX = mybir.AxisListType

P = 128
B, T, C = 8, 1024, 256
N = B * T
NT = T // P
KC = C // P
H, D = 16, 16
HH = H // KC
E, TOPK, FF = 8, 2, 1024
CAP = N // E
FJ = FF // P
G = 512
GT = G // P
GE = TOPK * CAP // G
NG = E * GE
SLOTS = NG * G
ROWS = N + G
EPS = 1e-5
BIG = 1.0e6
RT = TOPK * NT

CONST_COLS = dict(ident=P, before=P, causal=P, headmean=P, stateblk=C, headsel=HH, decay=KC,
                  revexp=E, restart=RT * E, slotbase=RT, mhalf=RT, ids=NT)


def const_at():
    at, out = 0, {}
    for name, n in CONST_COLS.items():
        out[name] = (at, at + n)
        at += n
    return out, at


class Names(dict):
    __getattr__ = dict.__getitem__


class Count:

    def __init__(self):
        self.n, self.shift = 0, 0

    def up(self, k=1):
        self.n += k
        return self.n + self.shift

    def enter(self, i, per):
        self.per, self.start, self.shift = per, self.n, i * per

    def leave(self, times):
        assert self.n - self.start == self.per, (self.n - self.start, self.per)
        self.n, self.shift = self.start + self.per * times, 0


def macaron_kernel(nc, x_in, w_qkv, w_gated, w_proj, gn_w, gn_b, router_w, w1, w2, f_bias,
                   consts_in, rope_in, slots_in, out):
    fp32, f32r, u32 = DT.float32, DT.float32r, DT.uint32
    ctx = ExitStack()
    with ctx:
        def sb(name, shape, dt=fp32, mem=ctx):
            return mem.enter_context(nc.sbuf_tensor(name, shape, dt))

        def sems(prefix, names):
            return Names({n: ctx.enter_context(nc.semaphore(f"{prefix}_{n}")) for n in names.split()})

        acc1 = nc.dram_tensor("acc1", [ROWS, C], fp32).ap()
        xn_d = nc.dram_tensor("xn_rows", [ROWS, C], fp32).ap()
        slot_d = [nc.dram_tensor(f"slot_table{r}", [SLOTS, 2], fp32).ap() for r in range(2)]

        at, ncol = const_at()
        cst = sb("cst", [P, ncol])
        K_ = {n: cst[:, a:b] for n, (a, b) in at.items()}
        ident, before, causal, headmean = (K_[n] for n in ("ident", "before", "causal", "headmean"))
        ones = sb("ones", [P, P])
        hbias = sb("hbias", [P, C])
        gnw, gnb = sb("gnw", [P, KC]), sb("gnb", [P, KC])
        rw = sb("rw", [P, KC, E])
        wqkT, wvT, wgT, wpT = sb("wqkT", [P, KC, 2 * C]), sb("wvT", [P, KC, C]), sb("wgT", [P, KC, C]), sb("wpT", [P, KC, C])

        wraw = sb("wraw", [P, 10, C])
        zrow = sb("zrow", [P, GT, C])

        xb = sb("xb", [P, NT, C])
        xr = sb("xr", [P, NT, C])
        xn_r = sb("xn_r", [P, NT, C])
        xrT = sb("xrT", [P, 2, KC, P])
        vz = sb("vz", [P, 2, H * 2 * D])

        def stats(n):
            return Names(st=sb(n + "_st", [P, NT, 6]), mv=sb(n + "_mv", [P, 5, NT]), rv=sb(n + "_rv", [P, NT]),
                                   rs=sb(n + "_rs", [P, NT]), nm=sb(n + "_nm", [P, NT]))

        lnf, lnr = stats("lnf"), stats("lnr")
        gst, gmv = sb("gst", [P, KC, NT, 6]), sb("gmv", [P, KC, 2])
        gsm, gdv = sb("gsm", [P, 8, KC]), sb("gdv", [P, KC, 2 * NT])
        lg, dl, ex, d2 = (sb(n, [P, NT, E]) for n in ("lg", "dl", "ex", "d2"))
        key = sb("key", [P, TOPK, NT, E])
        oh = sb("oh", [P, TOPK, NT, E])
        cnt, scn = sb("cnt", [P, TOPK, E, NT]), sb("scn", [P, TOPK, E, NT])
        pos = sb("pos", [P, TOPK, NT, E])
        base = sb("base", [P, TOPK, E])
        red = sb("red", [P, 4, NT])
        sel = sb("sel", [P, 8, RT])
        ids = sb("ids", [P, NT])
        pay = sb("pay", [P, 2, RT, 2])
        idx = sb("idx", [P, 2, RT], u32)
        tab = sb("tab", [P, GE, GT, 2])

        with ExitStack() as mem:
            stg1, stg2 = sb("stg1", [P, KC, FF], fp32, mem), sb("stg2", [P, FJ, C], fp32, mem)
            w1h, w1l = sb("w1h", [P, KC, FF], f32r, mem), sb("w1l", [P, KC, FF], f32r, mem)
            w2h, w2l = sb("w2h", [P, FJ, C], f32r, mem), sb("w2l", [P, FJ, C], f32r, mem)
            xe = [sb(f"xe{i}", [P, GT, C], fp32, mem) for i in range(2)]
            xh = [sb(f"xh{i}", [P, KC, G], f32r, mem) for i in range(2)]
            xl = [sb(f"xl{i}", [P, KC, G], f32r, mem) for i in range(2)]
            h32 = [sb(f"h32_{i}", [P, G], fp32, mem) for i in range(2)]
            hh, hl = sb("hh", [P, FJ, G], f32r, mem), sb("hl", [P, FJ, G], f32r, mem)
            yb = [sb(f"yb{i}", [P, GT, C], fp32, mem) for i in range(2)]

        rope = sb("rope", [P, NT, 2, 2 * C])
        xnT = sb("xnT", [P, KC, T])
        qk = sb("qk", [P, 2, 2 * C])
        qkT = sb("qkT", [P, 2 * KC, P])
        km = sb("km", [P, KC, HH, P])
        aw = sb("aw", [P, 4, 4, P])
        rt1, rt2 = sb("rt1", [P, 2 * C]), sb("rt2", [P, 2 * C])
        state, stmp = sb("state", [P, KC, P]), sb("stmp", [P, KC, P])
        xn_f = sb("xn_f", [P, 4, C])
        gT, yT, yg = sb("gT", [P, KC, T]), sb("yT", [P, KC, T]), sb("yg", [P, KC, T])

        bank = [ctx.enter_context(nc.psum_tensor(f"bank{i}", [P, 512], fp32)) for i in range(8)]

        S0 = sems("setup", "const vec rw zero acc_z out_z xn_z slot0 slot1 rope wraw wT wTc bias memset base passed")
        RN = "x x_odd lnst lnmv lnrv lnrs lnnm xn xnst trp trp_r xT xT_r sm sm_r exp link pay sent scat stored half o"
        R = [sems(f"route{r}", RN) for r in range(2)]
        F = [sems(f"ffn{r}", "w1raw w2raw w1h w1l w2h w2l tab0 tab1 tab2 tab3 xe0 xe1 xT xh xl up gelu hh hl down y add")
             for r in range(2)]
        A = sems("attn", "x lnst lnmv lnrv lnrs lnnm xn qk qk_r v v_r t t_r roped vz qkT kmd kma "
                         "sc aw y y_r st st_r stt state0 g f gst gst2 gmv gs gs_r glink grv grs gaff yg gated out")

        block = ctx.enter_context(nc.Block())
        tok = lambda a: a[0:N, :].rearrange("(b t p) c -> b p t c", t=NT, p=P)
        x_t, acc1_t, xn_t, out_t = tok(x_in), tok(acc1), tok(xn_d), tok(out)
        spare = lambda a: a[N:ROWS, :].rearrange("(t p) c -> p t c", p=P)

        def held(eng, sem, value):
            eng.wait_ge(sem, value)
            eng.sem_inc(S0.passed, 1)

        @block.sync
        def _(sp):
            sp.dma_start(cst[:], consts_in).then_inc(S0.const, 16)
            sp.dma_start(wraw[:, 0:6, :], w_qkv.rearrange("(j p) c -> p j c", p=P)).then_inc(S0.wraw, 16)
            sp.dma_start(wraw[:, 6:8, :], w_gated.rearrange("(j p) c -> p j c", p=P)).then_inc(S0.wraw, 16)
            sp.dma_start(wraw[:, 8:10, :], w_proj.rearrange("(j p) c -> p j c", p=P)).then_inc(S0.wraw, 16)
            sp.dma_start(rw[:], router_w.rearrange("(k p) e -> p k e", p=P)).then_inc(S0.rw, 16)
            for k in range(KC):
                half = lambda v: v[k * P:(k + 1) * P].rearrange("(p a) -> p a", a=1)
                sp.dma_start(gnw[:, k:k + 1], half(gn_w)).then_inc(S0.vec, 16)
                sp.dma_start(gnb[:, k:k + 1], half(gn_b)).then_inc(S0.vec, 16)
            sp.dma_start(hbias[:], f_bias.rearrange("a b c -> (a b) c").to_broadcast([P, C])).then_inc(S0.vec, 16)
            sp.dma_start(slot_d[0], slots_in).then_inc(S0.slot0, 16)
            sp.dma_start(slot_d[1], slots_in).then_inc(S0.slot1, 16)
            sp.wait_ge(S0.zero, 1)
            sp.dma_start(spare(acc1), zrow[:]).then_inc(S0.acc_z, 16)
            sp.dma_start(spare(out), zrow[:]).then_inc(S0.out_z, 16)
            sp.dma_start(spare(xn_d), zrow[:]).then_inc(S0.xn_z, 16)

            def ffn_weights(r):
                sp.dma_start(stg1[:], w1_t[0, :, :, :]).then_inc(F[r].w1raw, 16)
                sp.dma_start(stg2[:], w2_t[0, :, :, :]).then_inc(F[r].w2raw, 16)

            w1_t = w1.rearrange("e (k p) f -> e p k f", p=P)
            w2_t = w2.rearrange("e (j p) c -> e p j c", p=P)

            def route_store(S, b, x, dst):
                sp.wait_ge(S.xn, b * NT + NT)
                sp.dma_start(xn_t[b, :, :, :], xn_r[:]).then_inc(S.xnst, 16)
                sp.wait_ge(S.half, b + 1)
                sp.dma_start(dst[b, :, :, :], x[:]).then_inc(S.stored, 16)

            xs, x_here = (xr, xb), (R[0].x, R[0].x_odd)
            for q in range(2):
                sp.dma_start(xs[q][:], x_t[q, :, :, :]).then_inc(x_here[q], 16)
            with sp.Fori(0, B // 2 - 1) as p:
                for q in range(2):
                    b = p * 2 + q
                    route_store(R[0], b, xs[q], acc1_t)
                    held(sp, R[0].stored, b * 16 + 16)
                    sp.dma_start(xs[q][:], x_t[b + 2, :, :, :]).then_inc(x_here[q], 16)
            ffn_weights(0)
            for q in range(2):
                route_store(R[0], B - 2 + q, xs[q], acc1_t)

            def ffn(r):
                f = F[r]
                tab_t = slot_d[r].rearrange("(g p t) w -> g p t w", p=P, t=GT)

                def expert(e, last):
                    if not last:
                        sp.wait_ge(f.w1l, e * FJ + FJ)
                        sp.dma_start(stg1[:], w1_t[e + 1, :, :, :]).then_inc(f.w1raw, 16)
                        sp.wait_ge(f.w2l, e * FJ + FJ)
                        sp.dma_start(stg2[:], w2_t[e + 1, :, :, :]).then_inc(f.w2raw, 16)
                    for j in range(GE):
                        if last and j > 0:
                            break
                        if not last:
                            held(sp, f.add, e * (GE * GT * 16) + (j + 1) * GT * 16)
                            sp.dma_start(tab[:, j, :, :], tab_t[e * GE + GE + j, :, :, :]).then_inc(tabs[j], 16)

                tabs = [f.tab0, f.tab1, f.tab2, f.tab3]
                if r == 0:
                    sp.wait_ge(S0.acc_z, 16)
                    sp.wait_ge(S0.out_z, 16)
                    sp.wait_ge(S0.xn_z, 16)
                sp.wait_ge(R[r].scat, B * RT * 16)
                for j in range(GE):
                    sp.dma_start(tab[:, j, :, :], tab_t[j, :, :, :]).then_inc(tabs[j], 16)
                with sp.Fori(0, E - 1) as e:
                    expert(e, False)

            ffn(0)

            def front(b):
                sp.wait_ge(A.xn, b * NT + 1)
                sp.dma_start(xb[:], acc1_t[b, :, :, :]).then_inc(A.x, 16)

            def tail(b):
                sp.dma_start(xr[:], acc1_t[b, :, :, :]).then_inc(R[1].x, 16)
                route_store(R[1], b, xr, out_t)
                held(sp, R[1].stored, b * 16 + 16)

            sp.wait_ge(F[0].add, NG * GT * 16)
            sp.sem_inc(A.xn, 1)
            front(0)
            for t in range(NT):
                sp.dma_start(rope[:, t, :, :], rope_in[t, :, :, :]).then_inc(S0.rope, 16)
            front(1)
            with sp.Fori(0, B - 2) as i:
                front(i + 2)
                tail(i)
            tail(B - 2)
            sp.wait_ge(A.y, B * NT)
            ffn_weights(1)
            tail(B - 1)
            ffn(1)
            sp.wait_ge(F[1].add, NG * GT * 16)

        @block.gpsimd
        def _(pool):
            pool.memset(zrow[:], 0.0).then_inc(S0.zero, 1)
            pool.memset(ones[:], 1.0).then_inc(S0.memset, 1)
            pool.memset(vz[:], 0.0).then_inc(S0.memset, 1)
            pool.wait_ge(S0.const, 16)
            pool.wait_ge(S0.slot0, 16)
            pool.wait_ge(S0.slot1, 16)

            def power(S, ln, b):
                held(pool, S.lnrv, b + 1)
                pool.tensor_tensor(ln.rs[:], ln.rv[:], K_["mhalf"][:, 0:NT], ALU.pow).then_inc(S.lnrs, 1)

            def scatter(r, b, q):
                held(pool, R[r].pay, b + 1)
                for n in range(RT):
                    pool.indirect_dma_start(
                        out=slot_d[r], out_offset=bass.IndirectOffsetOnAxis(ap=idx[:, q, n:n + 1], axis=0),
                        in_=pay[:, q, n, :], in_offset=None, bounds_check=SLOTS - 1, oob_is_err=False).then_inc(R[r].scat, 16)

            def scattered(r, b):
                held(pool, R[r].scat, b * RT * 16 + RT * 16)
                pool.sem_inc(R[r].sent, 1)

            power(R[0], lnr, 0)
            power(R[0], lnr, 1)
            scatter(0, 0, 0)
            with pool.Fori(0, B // 2 - 1) as p:
                for q in range(2):
                    b = p * 2 + q
                    power(R[0], lnr, b + 2)
                    scattered(0, b)
                    scatter(0, b + 1, 1 - q)
            scattered(0, B - 2)
            scatter(0, B - 1, 1)

            def ffn(r):
                f = F[r]
                tabs = [f.tab0, f.tab1, f.tab2, f.tab3]
                xes = [f.xe0, f.xe1]
                dst = acc1 if r == 0 else out
                tabu = tab[:].bitcast(u32)

                def gather(j, waits):
                    for sem, value in waits:
                        held(pool, sem, value)
                    for t in range(GT):
                        pool.indirect_dma_start(
                            out=xe[j % 2][:, t, :], out_offset=None, in_=xn_d,
                            in_offset=bass.IndirectOffsetOnAxis(ap=tabu[:, j, t, 0:1], axis=0),
                            bounds_check=ROWS - 1, oob_is_err=True).then_inc(xes[j % 2], 16)

                def add(e, j):
                    held(pool, f.y, e * GE * GT + (j + 1) * GT)
                    if not (isinstance(e, int) and e == 0 and j == 0):
                        held(pool, f.add, e * (GE * GT * 16) + j * GT * 16)
                    for t in range(GT):
                        pool.indirect_dma_start(
                            out=dst, out_offset=bass.IndirectOffsetOnAxis(ap=tabu[:, j, t, 0:1], axis=0),
                            in_=yb[j % 2][:, t, :], in_offset=None, compute_op=ALU.add,
                            bounds_check=ROWS - 1, oob_is_err=True).then_inc(f.add, 16)

                held(pool, R[r].stored, B * 16)
                held(pool, R[r].xnst, B * 16)
                gather(0, [(f.tab0, 16)])
                gather(1, [(f.tab1, 16)])
                gather(2, [(f.tab2, 16), (f.xT, 1)])

                def expert(e, last):
                    for j in range(GE):
                        add(e, j)
                        g3 = j + 3
                        if last and g3 >= GE:
                            continue
                        gather(g3 % GE, [(tabs[g3 % GE], e * 16 + 16 * (g3 // GE) + 16), (f.xT, e * GE + j + 2)])

                expert(0, False)
                with pool.Fori(1, E - 1) as e:
                    expert(e, False)
                expert(E - 1, True)

            ffn(0)

            def gn_power(b):
                held(pool, A.grv, b + 1)
                pool.tensor_tensor(gsm[:, 3, :], gsm[:, 2, :], K_["mhalf"][:, 0:KC], ALU.pow).then_inc(A.grs, 1)

            def residual_power(b):
                power(R[1], lnr, b)

            def half_bias(b):
                held(pool, R[1].xn, b * NT + NT)
                pool.tensor_tensor(xr[:], xr[:], hbias[:].unsqueeze(1).to_broadcast([P, NT, C]), ALU.add).then_inc(R[1].half, 1)

            power(A, lnf, 0)
            power(A, lnf, 1)
            gn_power(0)
            residual_power(0)
            power(A, lnf, 2)
            half_bias(0)
            with pool.Fori(1, B - 2) as b:
                gn_power(b)
                scatter(1, b - 1, 0)
                scattered(1, b - 1)
                residual_power(b)
                power(A, lnf, b + 2)
                half_bias(b)
            for b in (B - 2, B - 1):
                gn_power(b)
                scatter(1, b - 1, 0)
                scattered(1, b - 1)
                residual_power(b)
                half_bias(b)
            scatter(1, B - 1, 0)
            ffn(1)

        @block.tensor
        def _(pe):
            pe.wait_ge(S0.const, 16)
            pe.wait_ge(S0.wraw, 48)
            for n in range(20):
                j, k = n // KC, n % KC
                if n >= 4:
                    pe.wait_ge(S0.wTc, n - 3)
                pe.transpose(bank[n % 4][:, 0:P], wraw[:, j, k * P:(k + 1) * P], ident).then_inc(S0.wT, 1)

            def route_tile(r, b, t, tr_free, tr_full):
                S = R[r]
                pe.wait_ge(S.xn, b * NT + t + 1)
                tr_free(t)
                for k in range(KC):
                    last = pe.transpose(bank[1 + t % 2][:, k * P:(k + 1) * P], xn_r[:, t, k * P:(k + 1) * P], ident)
                last.then_inc(tr_full(t), 1)
                if t:
                    logits(S, b, t - 1)
                if t == NT - 1:
                    logits(S, b, t)

            def counts(r, b):
                S = R[r]
                pe.wait_ge(S.link, b * LINKS + OH_LINK)
                pe.wait_ge(S.sm_r, b * 2 + 2)
                pe.matmul(bank[7][:, 0:RT * E], before, oh[:].rearrange("p k t e -> p (k t e)"), start=True, stop=True)
                pe.matmul(bank[7][:, RT * E:2 * RT * E], ones[:], oh[:].rearrange("p k t e -> p (k t e)"), start=True, stop=True)\
                    .then_inc(S.sm, 1)

            def logits(S, b, t):
                pe.wait_ge(S.xT, b * NT + t + 1)
                if t == 0:
                    pe.wait_ge(S.sm_r, b * 2 + 1)
                for k in range(KC):
                    last = pe.matmul(bank[7][:, t * E:(t + 1) * E], xrT[:, t % 2, k, :], rw[:, k, :],
                                     start=(k == 0), stop=(k == KC - 1))
                last.then_inc(S.xT_r if t < NT - 1 else S.sm, 1)

            pe.wait_ge(S0.wTc, 20)
            pe.wait_ge(S0.rw, 16)
            pe.wait_ge(S0.memset, 2)
            with pe.Fori(0, B) as b:
                for t in range(NT):
                    route_tile(0, b, t, lambda t: pe.wait_ge(R[0].trp_r, b * NT + t + 1), lambda t: R[0].trp)
                counts(0, b)

            def ffn(r):
                f = F[r]
                xes = [f.xe0, f.xe1]

                def transposes(j, xe_value, xl_value):
                    pe.wait_ge(xes[j % 2], xe_value)
                    if xl_value is not None:
                        pe.wait_ge(f.xl, xl_value)
                    for k in range(KC):
                        for t in range(GT):
                            last = pe.transpose(bank[6 + k][:, t * P:(t + 1) * P], xe[j % 2][:, t, k * P:(k + 1) * P], ident)
                    last.then_inc(f.xT, 1)

                def up(j, fj, up_free):
                    if up_free is not None:
                        pe.wait_ge(f.gelu, up_free)
                    n = 0
                    for k in range(KC):
                        w = slice(fj * P, (fj + 1) * P)
                        for a, c in ((w1h, xh), (w1h, xl), (w1l, xh)):
                            last = pe.matmul(bank[fj % 2][:], a[:, k, w], c[j % 2][:, k, :], start=(n == 0), stop=(n == 5))
                            n += 1
                    last.then_inc(f.up, 1)

                def down(j, fj):
                    for t in range(GT):
                        s = slice(t * P, (t + 1) * P)
                        o = bank[2 + 2 * (j % 2) + t // 2][:, (t % 2) * C:(t % 2 + 1) * C]
                        for n, (a, c) in enumerate(((hh, w2h), (hh, w2l), (hl, w2h))):
                            last = pe.matmul(o, a[:, fj, s], c[:, fj, :], start=(fj == 0 and n == 0 and t % 2 == 0),
                                             stop=(fj == FJ - 1 and n == 2), skip_group_check=True)
                    if fj == FJ - 1:
                        last.then_inc(f.down, 1)

                transposes(0, GT * 16, None)
                transposes(1, GT * 16, KC)
                pe.wait_ge(f.w1l, FJ)
                pe.wait_ge(f.xl, KC)
                for fj in range(FJ):
                    up(0, fj, None if fj < 2 else fj - 1)

                def expert(e, last, first):
                    for j in range(GE):
                        end = last and j == GE - 1
                        for fj in range(FJ):
                            if fj == 0:
                                if not first or j >= 2:
                                    pe.wait_ge(f.y, (e * GE + j - 1) * GT)
                            if j == 0:
                                pe.wait_ge(f.w2l, e * FJ + fj + 1)
                            pe.wait_ge(f.hl, (e * GE + j) * FJ + fj + 1)
                            down(j, fj)
                            if not end:
                                if fj == 0:
                                    pe.wait_ge(f.xl, (e * GE + j + 2) * KC)
                                if j == GE - 1:
                                    pe.wait_ge(f.w1l, (e + 1) * FJ + fj + 1)
                                up((j + 1) % GE, fj, (e * GE + j + 1) * FJ + fj - 1)
                            if fj == 5 and not (last and j + 2 >= GE):
                                jj = (j + 2) % GE
                                transposes(jj, (e * (GE // 2) + (j + 2) // 2 + 1) * GT * 16, (e * GE + j + 2) * KC)

                expert(0, False, True)
                with pe.Fori(1, E - 1) as e:
                    expert(e, False, False)
                expert(E - 1, True, False)

            pe.wait_ge(R[0].sm_r, 2 * B + 1)
            pe.wait_ge(R[0].trp_r, N // P + 2)
            ffn(0)

            c1, c2 = Count(), Count()
            shared, fulls, frees = (c1, c2), (A.v, A.t), (A.v_r, A.t_r)

            def front_tile(b, t):
                pe.wait_ge(A.xn, b * NT + t + 2)
                pe.wait_ge(frees[t % 2], shared[t % 2].up())
                for k in range(KC):
                    last = pe.transpose(bank[1 + t % 2][:, k * P:(k + 1) * P], xn_f[:, t % 4, k * P:(k + 1) * P], ident)
                last.then_inc(fulls[t % 2], 1)

            def project(b, i):
                s = slice(i % NT * P, (i % NT + 1) * P)
                pe.wait_ge(A.f, b * NT + i + 1)
                pe.wait_ge(A.qk_r, b * NT + i + 1)
                for k in range(KC):
                    last = pe.matmul(bank[0][:], xnT[:, k, s], wqkT[:, k, :], start=(k == 0), stop=(k == KC - 1))
                last.then_inc(A.qk, 1)
                pe.wait_ge(A.v_r, c1.up())
                for k in range(KC):
                    last = pe.matmul(bank[1][:, 0:C], xnT[:, k, s], wvT[:, k, :], start=(k == 0), stop=(k == KC - 1))
                last.then_inc(A.v, 1)

            def gate(half):
                for m in range(KC):
                    pe.wait_ge(frees[m], shared[m].up())
                    for k in range(KC):
                        last = pe.matmul(bank[1 + m][:], wgT[:, k, m * P:(m + 1) * P], xnT[:, k, half * 512:(half + 1) * 512],
                                         start=(k == 0), stop=(k == KC - 1))
                    last.then_inc(fulls[m], 1)

            def scores(b, i, q):
                half, four = q % 2, q // 2
                if four == 0:
                    pe.wait_ge(A.kmd, b * NT + i + 1)
                else:
                    pe.wait_ge(A.kma, b * NT + i + 1)
                pe.wait_ge(A.aw, (b * NT + i) * 4 + q + 1)
                for m in range(4):
                    last = pe.matmul(bank[3 + half][:, m * P:(m + 1) * P], km[:, half, four * 4 + m, :],
                                     qkT[:, half, :], start=True, stop=True)
                last.then_inc(A.sc, 1)

            def attend(b, i, q):
                half, four = q % 2, q // 2
                pe.wait_ge(A.aw, (b * NT + i) * 4 + q + 3)
                for m in range(4):
                    h = half * HH + four * 4 + m
                    r = 32 * ((four * 4 + m) // 2)
                    last = pe.matmul(bank[5][r:r + 32, half * P:(half + 1) * P], vz[:, i % 2, h * 32:(h + 1) * 32],
                                     aw[:, q, m, :], start=False, stop=(m % 2 == 1), skip_group_check=True)
                if q == 3:
                    last.then_inc(A.y, 1)

            def head_means(b):
                pe.wait_ge(A.gmv, b + 1)
                pe.wait_ge(R[1].sm_r, b * 2 + 1)
                pe.matmul(bank[7][:, 0:KC], headmean, gmv[:, :, 0], start=True, stop=True).then_inc(A.gs, 1)

            def head_variances(b):
                pe.wait_ge(A.gs_r, b + 1)
                pe.matmul(bank[7][:, 0:KC], headmean, gsm[:, 1, :], start=True, stop=True).then_inc(A.gs, 1)

            def out_tile(b, t, nth):
                if t == 0:
                    pe.wait_ge(A.gated, b * KC + KC)
                if nth >= 2:
                    pe.wait_ge(R[1].o, b * NT + t - 1)
                for k in range(KC):
                    last = pe.matmul(bank[3 + nth % 2][:, 0:C], yg[:, k, t * P:(t + 1) * P], wpT[:, k, :],
                                     start=(k == 0), stop=(k == KC - 1))
                last.then_inc(A.out, 1)

            def residual_route(b, t):
                if t == 0:
                    pe.wait_ge(A.grv, b + 1)
                route_tile(1, b, t, lambda t: pe.wait_ge(frees[t % 2], shared[t % 2].up()), lambda t: fulls[t % 2])

            def turn(b, i):
                pe.wait_ge(A.roped, b * NT + i + 1)
                pe.wait_ge(A.t_r, c2.up())
                for n in range(2 * KC):
                    last = pe.transpose(bank[2][:, n * P:(n + 1) * P], qk[:, i % 2, n * P:(n + 1) * P], ident)
                last.then_inc(A.t, 1)

            def sequence(b, tail, front):
                for i in range(NT):
                    more = i + 1 < NT or front is not None
                    if more:
                        project(b, i + 1)
                    if tail is not None and i == COUNT_STEP:
                        counts(1, tail)
                    if i in GATE_AT:
                        gate(GATE_AT.index(i))
                    if tail is not None and OUT_AT[i - 1]:
                        pe.wait_ge(R[1].o, tail * NT + OUT_AT[i - 1][-1] + 1)
                    scores(b, i, 0)
                    scores(b, i, 1)
                    pe.wait_ge(A.stt, b * NT + i + 1)
                    pe.wait_ge(A.y_r, b * NT + i + 1)
                    for k in range(KC):
                        last = pe.matmul(bank[5][:, k * P:(k + 1) * P], state[:, k, :], qkT[:, k, :],
                                         start=(k == 0), stop=False, skip_group_check=True)
                    pe.wait_ge(A.vz, b * NT + i + 1)
                    pe.wait_ge(A.st_r, b * NT + i + 1)
                    for k in range(KC):
                        v = vz[:, i % 2, k * HH * 32:(k + 1) * HH * 32].rearrange("p (m x) -> p m x", x=64)
                        v = v.rearrange("p m (a y) -> p m a y", y=16)[:, :, 0:4:3, :]
                        last = pe.matmul(bank[6][:, k * P:(k + 1) * P], qk[:, i % 2, C + k * P:C + (k + 1) * P], v, start=True, stop=True)
                    last.then_inc(A.st, 1)
                    if tail is not None and i == 0:
                        head_means(tail)
                    for q in range(4):
                        if q == 3 and more:
                            turn(b, i + 1)
                        attend(b, i, q)
                        if q < 2:
                            scores(b, i, q + 2)
                        if tail is not None and i == 0 and q == 2:
                            head_variances(tail)
                        if tail is not None:
                            for t in third(ROUTE_AT[i], q):
                                residual_route(tail, t)
                        if front is not None:
                            for t in third(FRONT_AT[i], q):
                                front_tile(front, t)
                    if tail is not None:
                        for n, t in enumerate(OUT_AT[i]):
                            out_tile(tail, t, n)

            pe.wait_ge(F[0].y, NG * GT)
            for t in range(NT):
                front_tile(0, t)
            project(0, 0)
            turn(0, 0)
            sequence(0, None, 1)
            with pe.Fori(0, B - 2) as i:
                for c in shared:
                    c.enter(i, BANK_USES)
                sequence(i + 1, i, i + 2)
            for c in shared:
                c.leave(B - 2)
            sequence(B - 1, B - 2, None)
            head_means(B - 1)
            head_variances(B - 1)
            for t in range(NT):
                out_tile(B - 1, t, t)
            for t in range(NT):
                residual_route(B - 1, t)
            counts(1, B - 1)
            pe.wait_ge(R[1].sm_r, 2 * B + 1)
            ffn(1)

        @block.scalar
        def _(act):
            dst = [wqkT[:, :, (j * P):(j + 1) * P] for j in range(4)] + [wvT[:, :, j * P:(j + 1) * P] for j in range(2)] \
                + [wgT[:, :, j * P:(j + 1) * P] for j in range(2)] + [wpT[:, :, j * P:(j + 1) * P] for j in range(2)]
            for n in range(20):
                act.wait_ge(S0.wT, n + 1)
                act.activation(dst[n // KC][:, n % KC, :], bank[n % 4][:, 0:P], ACT.Copy).then_inc(S0.wTc, 1)
            act.sem_inc(R[0].trp_r, 2)

            def normalise(S, ln, dst, src, t):
                act.activation(dst, src[:, t, :], ACT.Identity, bias=ln.nm[:, t:t + 1], scale=ln.rs[:, t:t + 1]).then_inc(S.xn, 1)

            def evac(S, b, t, tr_full, tr_read):
                tr_full(t)
                if t >= 2:
                    act.wait_ge(S.xT_r, b * (NT - 1) + t - 1)
                act.activation(xrT[:, t % 2, :, :], bank[1 + t % 2][:, 0:KC * P].rearrange("p (k x) -> p k x", k=KC), ACT.Copy)\
                    .then_inc(S.xT, 1)
                tr_read(t)

            def exponents(S, b):
                act.wait_ge(S.link, b * LINKS + EXP_LINK)
                act.activation(ex[:], dl[:], ACT.Exp).then_inc(S.exp, 1)

            xs = (xr, xb)
            with act.Fori(0, B // 2) as p:
                for q in range(2):
                    b = p * 2 + q
                    act.wait_ge(R[0].lnnm, b + 1)
                    for t in range(NT + 1):
                        if t < NT:
                            normalise(R[0], lnr, xn_r[:, t, :], xs[q], t)
                        if t >= 1:
                            evac(R[0], b, t - 1, lambda t: act.wait_ge(R[0].trp, b * NT + t + 1),
                                 lambda t: (act.wait_ge(R[0].xT, b * NT + t + 1), act.sem_inc(R[0].trp_r, 1)))
                    exponents(R[0], b)

            def ffn(r):
                f = F[r]

                def split_x(j, xT_value):
                    act.wait_ge(f.xT, xT_value)
                    for k in range(KC):
                        act.activation(xh[j % 2][:, k, :], bank[6 + k][:], ACT.Copy).then_inc(f.xh, 1)

                def gelu(j, fj, up_value, lo_value):
                    act.wait_ge(f.up, up_value)
                    if lo_value is not None:
                        act.wait_ge(f.hl, lo_value)
                    act.activation(h32[fj % 2][:], bank[fj % 2][:], ACT.Gelu_apprx_tanh).then_inc(f.gelu, 1)

                def high1(fj):
                    w = slice(fj * P, (fj + 1) * P)
                    act.activation(w1h[:, :, w], stg1[:, :, w], ACT.Copy).then_inc(f.w1h, 1)

                def high2(fj):
                    act.activation(w2h[:, fj, :], stg2[:, fj, :], ACT.Copy).then_inc(f.w2h, 1)

                def weigh(e, j):
                    act.wait_ge(f.down, e * GE + j + 1)
                    if not (isinstance(e, int) and e == 0 and j < 2):
                        act.wait_ge(f.add, (e * GE + j - 1) * GT * 16)
                    for t in range(GT):
                        act.activation(yb[j % 2][:, t, :], bank[2 + 2 * (j % 2) + t // 2][:, (t % 2) * C:(t % 2 + 1) * C],
                                       ACT.Copy, scale=tab[:, j, t, 1:2]).then_inc(f.y, 1)

                act.wait_ge(f.w1raw, 16)
                for fj in range(FJ):
                    high1(fj)
                split_x(0, 1)
                act.wait_ge(f.w2raw, 16)
                for fj in range(FJ):
                    high2(fj)
                split_x(1, 2)
                for fj in range(FJ):
                    gelu(0, fj, fj + 1, None if fj < 2 else fj - 1)

                def expert(e, last):
                    for j in range(GE):
                        for fj in range(FJ):
                            if not (last and j == GE - 1):
                                g1 = (e * GE + j + 1) * FJ + fj
                                gelu((j + 1) % GE, fj, g1 + 1, g1 - 1)
                            if not last and j == GE - 2:
                                if fj == 0:
                                    act.wait_ge(f.w1raw, e * 16 + 32)
                                high1(fj)
                            if not last and j == GE - 1:
                                if fj == 0:
                                    act.wait_ge(f.w2raw, e * 16 + 32)
                                high2(fj)
                            if fj == 5 and not (last and j + 2 >= GE):
                                split_x((j + 2) % GE, e * GE + j + 3)
                        weigh(e, j)

                expert(0, False)
                with act.Fori(1, E - 1) as e:
                    expert(e, False)
                expert(E - 1, True)

            ffn(0)

            c1, c2 = Count(), Count()
            shared, fulls, frees = (c1, c2), (A.v, A.t), (A.v_r, A.t_r)
            act.sem_inc(A.v_r, 1)
            act.sem_inc(A.t_r, 1)
            act.sem_inc(A.y_r, 1)

            def front_norm(b, t):
                if t == 0:
                    act.wait_ge(A.lnnm, b + 1)
                if t >= 4:
                    act.wait_ge(A.f, b * NT + t - 3)
                normalise(A, lnf, xn_f[:, t % 4, :], xb, t)

            def front_evac(b, t):
                act.wait_ge(fulls[t % 2], shared[t % 2].up())
                act.activation(xnT[:, :, t * P:(t + 1) * P], bank[1 + t % 2][:, 0:C].rearrange("p (k x) -> p k x", k=KC), ACT.Copy)\
                    .then_inc(A.f, 1)
                act.wait_ge(A.f, b * NT + t + 1)
                act.sem_inc(frees[t % 2], 1)

            def values(b, i):
                act.wait_ge(A.v, c1.up())
                dst = vz[:, i % 2, :].rearrange("p (m a y) -> p m a y", a=4, y=D)[:, :, 0:4:3, :]
                act.activation(dst, bank[1][:, 0:C].rearrange("p (m a y) -> p m a y", a=2, y=D), ACT.Copy).then_inc(A.vz, 1)
                act.wait_ge(A.vz, b * NT + i + 1)
                act.sem_inc(A.v_r, 1)

            def gate(b, half, tail):
                if half == 0 and tail is not None:
                    act.wait_ge(A.gated, tail * KC + KC)
                for m in range(KC):
                    act.wait_ge(fulls[m], shared[m].up())
                    act.activation(gT[:, m, half * 512:(half + 1) * 512], bank[1 + m][:], ACT.Silu).then_inc(A.g, 1)
                    act.wait_ge(A.g, b * 4 + half * KC + m + 1)
                    act.sem_inc(frees[m], 1)

            def head_norm(b):
                act.wait_ge(A.gaff, b + 1)
                for k in range(KC):
                    act.activation(yg[:, k, :], yT[:, k, :], ACT.Identity, bias=gsm[:, 6, k:k + 1], scale=gsm[:, 4, k:k + 1])\
                        .then_inc(A.yg, 1)

            def residual_norm(b, t):
                if t == 0:
                    act.wait_ge(R[1].lnnm, b + 1)
                normalise(R[1], lnr, xn_r[:, t, :], xr, t)

            def residual_evac(b, t):
                evac(R[1], b, t, lambda t: act.wait_ge(fulls[t % 2], shared[t % 2].up()),
                     lambda t: (act.wait_ge(R[1].xT, b * NT + t + 1), act.sem_inc(frees[t % 2], 1)))

            def sequence(b, tail, front):
                for i in range(NT):
                    act.wait_ge(A.t, c2.up())
                    act.activation(qkT[:, :, :], bank[2][:].rearrange("p (n x) -> p n x", x=P), ACT.Copy).then_inc(A.qkT, 1)
                    act.wait_ge(A.qkT, b * NT + i + 1)
                    act.sem_inc(A.t_r, 1)
                    for m in range(4, HH):
                        last = act.activation(km[:, :, m, :], qkT[:, KC:2 * KC, :], ACT.Copy, scale=K_["headsel"][:, m:m + 1])
                    last.then_inc(A.kma, 1)
                    if i + 1 < NT or front is not None:
                        values(b, i + 1)
                    if i in GATE_AT:
                        gate(b, GATE_AT.index(i), tail)
                    if tail is not None:
                        if i == 0:
                            head_norm(tail)
                        for t in ROUTE_AT[i]:
                            residual_norm(tail, t)
                        if i == COUNT_STEP:
                            exponents(R[1], tail)
                    if front is not None:
                        for t in FRONT_AT[i]:
                            front_norm(front, t)
                    for q in range(3):
                        if tail is not None:
                            for t in third(ROUTE_AT[i], q):
                                residual_evac(tail, t)
                        if front is not None:
                            for t in third(FRONT_AT[i], q):
                                front_evac(front, t)
                    if tail is not None and i == 0:
                        act.wait_ge(A.yg, tail * KC + KC)
                    act.wait_ge(A.y, b * NT + i + 1)
                    act.activation(yT[:, :, i * P:(i + 1) * P], bank[5][:, 0:C].rearrange("p (k x) -> p k x", k=KC), ACT.Copy)\
                        .then_inc(A.y_r, 1)

            for t in range(NT + 2):
                if t < NT:
                    front_norm(0, t)
                if t >= 2:
                    front_evac(0, t - 2)
            values(0, 0)
            sequence(0, None, 1)
            with act.Fori(0, B - 2) as i:
                for c in shared:
                    c.enter(i, BANK_USES)
                sequence(i + 1, i, i + 2)
            for c in shared:
                c.leave(B - 2)
            sequence(B - 1, B - 2, None)
            head_norm(B - 1)
            for t in range(NT + 1):
                if t < NT:
                    residual_norm(B - 1, t)
                if t >= 1:
                    residual_evac(B - 1, t - 1)
            exponents(R[1], B - 1)
            ffn(1)

        @block.vector
        def _(dve):
            def bc(ap, shape):
                return ap.to_broadcast(shape)

            dve.wait_ge(S0.vec, 80)
            dve.tensor_scalar(hbias[:], hbias[:], 0.5, None, ALU.mult).then_inc(S0.bias, 1)
            dve.wait_ge(S0.bias, 1)
            dve.wait_ge(S0.const, 16)

            def tile_stats(S, ln, x, t):
                dve.bn_stats(ln.st[:, t, :], x[:, t, :]).then_inc(S.lnst, 1)

            def norm_stats(S, ln, b):
                dve.wait_ge(S.lnst, b * NT + NT)
                mean, sq = (lambda a: ln.st[:, :, 3 * a + 1]), (lambda a: ln.st[:, :, 3 * a + 2])
                dve.tensor_tensor(ln.mv[:, 0], mean(0), mean(1), ALU.add).then_inc(S.lnmv, 1)
                dve.tensor_tensor(ln.mv[:, 1], mean(0), mean(1), ALU.subtract).then_inc(S.lnmv, 1)
                dve.tensor_tensor(ln.mv[:, 2], sq(0), sq(1), ALU.add).then_inc(S.lnmv, 1)
                dve.wait_ge(S.lnmv, b * LN_STEPS + 2)
                dve.tensor_tensor(ln.mv[:, 3], ln.mv[:, 1], ln.mv[:, 1], ALU.mult).then_inc(S.lnmv, 1)
                dve.wait_ge(S.lnmv, b * LN_STEPS + 4)
                dve.scalar_tensor_tensor(ln.mv[:, 4], ln.mv[:, 3], C / 4.0, ln.mv[:, 2], ALU.mult, ALU.add).then_inc(S.lnmv, 1)
                dve.wait_ge(S.lnmv, b * LN_STEPS + LN_STEPS)
                dve.tensor_scalar(ln.rv[:], ln.mv[:, 4], 1.0 / C, EPS, ALU.mult, ALU.add).then_inc(S.lnrv, 1)

            def norm_shift(S, ln, b):
                dve.wait_ge(S.lnrs, b + 1)
                dve.scalar_tensor_tensor(ln.nm[:], ln.mv[:, 0], -0.5, ln.rs[:], ALU.mult, ALU.mult).then_inc(S.lnnm, 1)

            te = [P, NT, E]
            over_t = lambda a: a.unsqueeze(1).to_broadcast(te)
            over_e = lambda a: a.unsqueeze(2).to_broadcast(te)

            def steps(S, b, before):
                n = [before]

                def link(ins):
                    ins.then_inc(S.link, 1)
                    n[0] += 1
                    dve.wait_ge(S.link, b * LINKS + n[0])

                return link, n

            def choices(r, b):
                S = R[r]
                link, n = steps(S, b, 0)
                dve.wait_ge(S.sm, b * 2 + 1)
                dve.tensor_copy(lg[:], bank[7][:, 0:NT * E].rearrange("p (t e) -> p t e", e=E)).then_inc(S.sm_r, 1)
                dve.wait_ge(S.sm_r, b * 2 + 2)
                link(dve.tensor_reduce(red[:, 0, :], lg[:], AX.X, ALU.max))
                link(dve.tensor_tensor(dl[:], lg[:], over_e(red[:, 0, :]), ALU.subtract))
                link(dve.tensor_scalar(dl[:], dl[:], -87.0, None, ALU.max))
                assert n[0] == EXP_LINK
                link(dve.scalar_tensor_tensor(key[:, 0], dl[:], 0.0, over_t(K_["revexp"]), ALU.is_ge, ALU.mult))
                link(dve.tensor_reduce(sel[:, 0, 0:NT], key[:, 0], AX.X, ALU.max))
                link(dve.tensor_tensor(oh[:, 0], key[:, 0], over_e(sel[:, 0, 0:NT]), ALU.is_equal))
                link(dve.scalar_tensor_tensor(d2[:], oh[:, 0], -1.0e30, dl[:], ALU.mult, ALU.add))
                link(dve.tensor_reduce(red[:, 1, :], d2[:], AX.X, ALU.max))
                link(dve.tensor_tensor(key[:, 1], d2[:], over_e(red[:, 1, :]), ALU.is_equal))
                link(dve.tensor_tensor(key[:, 1], key[:, 1], over_t(K_["revexp"]), ALU.mult))
                link(dve.tensor_reduce(sel[:, 0, NT:RT], key[:, 1], AX.X, ALU.max))
                link(dve.tensor_tensor(oh[:, 1], key[:, 1], over_e(sel[:, 0, NT:RT]), ALU.is_equal))
                assert n[0] == OH_LINK

            def weights(r, b):
                S = R[r]
                link, n = steps(S, b, OH_LINK)
                dve.wait_ge(S.exp, b + 1)
                link(dve.tensor_reduce(red[:, 2, :], ex[:], AX.X, ALU.add))
                link(dve.reciprocal(red[:, 3, :], red[:, 2, :]))
                for k in range(TOPK):
                    link(dve.tensor_tensor(key[:, k], oh[:, k], ex[:], ALU.mult))
                link(dve.tensor_reduce(sel[:, 1, :], key[:].rearrange("p k t e -> p (k t) e"), AX.X, ALU.add))
                kt = lambda a: a.rearrange("p (k t) -> p k t", k=TOPK)
                link(dve.tensor_tensor(kt(sel[:, 2, :]), kt(sel[:, 1, :]), red[:, 3, :].unsqueeze(1).to_broadcast([P, TOPK, NT]), ALU.mult))
                assert n[0] == WEIGHT_LINK

            def slots(r, b, q):
                S = R[r]
                link, n = steps(S, b, WEIGHT_LINK)
                dve.wait_ge(S.sm, b * 2 + 2)
                ahead = bank[7][:, 0:RT * E].rearrange("p (k t e) -> p k t e", k=TOPK, t=NT)
                whole = bank[7][:, RT * E:2 * RT * E].rearrange("p (k t e) -> p k t e", k=TOPK, t=NT)
                for k in range(TOPK):
                    link(dve.tensor_copy(cnt[:, k].rearrange("p e t -> p t e"), whole[:, k]))
                flat = lambda a: a.rearrange("p k e t -> p (k e t)")
                link(dve.tensor_tensor_scan(flat(scn[:]), K_["restart"], flat(cnt[:]), 0.0, ALU.mult, ALU.add))
                dve.tensor_tensor(pos[:, 0], ahead[:, 0], cnt[:, 0].rearrange("p e t -> p t e"), ALU.subtract)
                dve.tensor_tensor(pos[:, 1], ahead[:, 1], cnt[:, 1].rearrange("p e t -> p t e"), ALU.subtract).then_inc(S.sm_r, 1)
                dve.wait_ge(S.sm_r, b * 2 + 3)
                for k in range(TOPK):
                    link(dve.tensor_tensor(pos[:, k], pos[:, k], scn[:, k].rearrange("p e t -> p t e"), ALU.add))
                for k in range(TOPK):
                    link(dve.tensor_tensor(pos[:, k], pos[:, k], over_t(base[:, k, :]), ALU.add))
                link(dve.tensor_tensor(base[:], base[:], scn[:, :, :, NT - 1], ALU.add))
                link(dve.tensor_tensor(pos[:], pos[:], oh[:], ALU.mult))
                link(dve.tensor_reduce(sel[:, 3, :], pos[:].rearrange("p k t e -> p (k t) e"), AX.X, ALU.add))
                link(dve.tensor_scalar(sel[:, 4, :], sel[:, 3, :], float(CAP), None, ALU.is_lt))
                link(dve.scalar_tensor_tensor(sel[:, 5, :], sel[:, 0, :], -float(TOPK * CAP), sel[:, 3, :], ALU.mult, ALU.add))
                link(dve.tensor_tensor(sel[:, 5, :], sel[:, 5, :], K_["slotbase"], ALU.add))
                link(dve.tensor_scalar(sel[:, 6, :], sel[:, 4, :], -BIG, BIG, ALU.mult, ALU.add))
                dve.wait_ge(S.sent, b + 1)
                link(dve.tensor_tensor(idx[:, q], sel[:, 5, :], sel[:, 6, :], ALU.add))
                link(dve.scalar_tensor_tensor(pay[:, q, :, 1], sel[:, 2, :], 0.5, sel[:, 4, :], ALU.mult, ALU.mult))
                link(dve.tensor_copy(pay[:, q].bitcast(u32).rearrange("p (k t) w -> p k t w", k=TOPK)[:, :, :, 0],
                                     ids[:].unsqueeze(1).to_broadcast([P, TOPK, NT])))
                dve.tensor_scalar(ids[:], ids[:], float(T), None, ALU.add).then_inc(S.pay, 1)
                dve.wait_ge(S.pay, b + 1)
                assert n[0] == LINKS

            def start_route(r):
                dve.memset(base[:], 0.0).then_inc(S0.base, 1)
                dve.tensor_copy(ids[:], K_["ids"]).then_inc(S0.base, 1)
                dve.wait_ge(S0.base, 2 * r + 2)
                dve.sem_inc(R[r].sm_r, 1)
                dve.sem_inc(R[r].sent, 2 - r)

            xs, x_here = (xr, xb), (R[0].x, R[0].x_odd)

            def first_stats(b, q, value):
                dve.wait_ge(x_here[q], value)
                for t in range(NT):
                    tile_stats(R[0], lnr, xs[q], t)
                norm_stats(R[0], lnr, b)

            def first_route(b, q, p, more):
                dve.wait_ge(R[0].xn, b * NT + NT)
                if more:
                    first_stats(b + 1, 1 - q, (p + q) * 16 + 16)
                dve.tensor_tensor(xs[q][:], xs[q][:], hbias[:].unsqueeze(1).to_broadcast([P, NT, C]), ALU.add).then_inc(R[0].half, 1)
                choices(0, b)
                weights(0, b)
                slots(0, b, q)
                if more:
                    dve.wait_ge(R[0].xnst, b * 16 + 16)
                    norm_shift(R[0], lnr, b + 1)

            start_route(0)
            first_stats(0, 0, 16)
            norm_shift(R[0], lnr, 0)
            with dve.Fori(0, B // 2 - 1) as p:
                for q in range(2):
                    first_route(p * 2 + q, q, p, True)
            first_route(B - 2, 0, B // 2 - 1, True)
            first_route(B - 1, 1, B // 2 - 1, False)

            def ffn(r):
                f = F[r]

                def split_x(j, xh_value):
                    for k in range(KC):
                        dve.wait_ge(f.xh, xh_value + k)
                        dve.tensor_tensor(xl[j % 2][:, k, :], bank[6 + k][:], xh[j % 2][:, k, :].bitcast(fp32), ALU.subtract).then_inc(f.xl, 1)

                def low1(fj, value):
                    w = slice(fj * P, (fj + 1) * P)
                    dve.wait_ge(f.w1h, value)
                    dve.tensor_tensor(w1l[:, :, w], stg1[:, :, w], w1h[:, :, w].bitcast(fp32), ALU.subtract).then_inc(f.w1l, 1)

                def low2(fj, value):
                    dve.wait_ge(f.w2h, value)
                    dve.tensor_tensor(w2l[:, fj, :], stg2[:, fj, :], w2h[:, fj, :].bitcast(fp32), ALU.subtract).then_inc(f.w2l, 1)

                def high(fj, value):
                    dve.wait_ge(f.gelu, value)
                    dve.tensor_copy(hh[:, fj, :], h32[fj % 2][:]).then_inc(f.hh, 1)

                def low(fj, value):
                    dve.wait_ge(f.hh, value)
                    dve.tensor_tensor(hl[:, fj, :], h32[fj % 2][:], hh[:, fj, :].bitcast(fp32), ALU.subtract).then_inc(f.hl, 1)

                for fj in range(FJ):
                    low1(fj, fj + 1)
                split_x(0, 1)
                for fj in range(FJ):
                    low2(fj, fj + 1)
                split_x(1, KC + 1)
                for fj in range(FJ):
                    high(fj, fj + 1)
                    low(fj, fj + 1)

                def expert(e, last):
                    for j in range(GE):
                        for fj in range(FJ):
                            go = not (last and j == GE - 1)
                            value = (e * GE + j + 1) * FJ + fj + 1
                            if go:
                                high(fj, value)
                            if not last and j == GE - 2:
                                low1(fj, (e + 1) * FJ + fj + 1)
                            if not last and j == GE - 1:
                                low2(fj, (e + 1) * FJ + fj + 1)
                            if go:
                                low(fj, value)
                            if fj == 5 and not (last and j + 2 >= GE):
                                split_x((j + 2) % GE, (e * GE + j + 2) * KC + 1)

                expert(0, False)
                with dve.Fori(1, E - 1) as e:
                    expert(e, False)
                expert(E - 1, True)

            ffn(0)

            dve.sem_inc(A.qk_r, 1)
            dve.sem_inc(A.aw, 2)
            dve.sem_inc(A.st_r, 1)

            def front_stats(b):
                dve.wait_ge(A.x, b * 16 + 16)
                for t in range(NT):
                    tile_stats(A, lnf, xb, t)
                norm_stats(A, lnf, b)

            def rotate(b, i):
                dve.wait_ge(A.qk, b * NT + i + 1)
                two = lambda a: a.rearrange("p (c w) -> p c w", w=2)
                dve.tensor_tensor(rt1[:], bank[0][:], rope[:, i % NT, 0, :], ALU.mult)
                dve.tensor_tensor(two(rt2[:])[:, :, 0], two(bank[0][:])[:, :, 1], two(rope[:, i % NT, 1, :])[:, :, 0], ALU.mult)
                dve.tensor_tensor(two(rt2[:])[:, :, 1], two(bank[0][:])[:, :, 0], two(rope[:, i % NT, 1, :])[:, :, 1], ALU.mult)\
                    .then_inc(A.qk_r, 1)
                dve.wait_ge(A.qk_r, b * NT + i + 2)
                dve.tensor_tensor(qk[:, i % 2, :], rt1[:], rt2[:], ALU.add).then_inc(A.roped, 1)

            def mask(b, i, q):
                dve.wait_ge(A.sc, (b * NT + i) * 4 + q + 1)
                dve.tensor_tensor(aw[:, q], bank[3 + q % 2][:].rearrange("p (m x) -> p m x", m=4),
                                  causal.unsqueeze(1).to_broadcast([P, 4, P]), ALU.mult).then_inc(A.aw, 1)

            def channel_stats(b, i):
                dve.wait_ge(A.y_r, b * NT + i + 2)
                for k in range(KC):
                    dve.bn_stats(gst[:, k, i, :], yT[:, k, i * P:(i + 1) * P]).then_inc(A.gst, 1)

            def norm_steps(b, before):
                n = [before]

                def link(ins):
                    ins.then_inc(A.glink, 1)
                    n[0] += 1
                    dve.wait_ge(A.glink, b * GLINKS + n[0])

                return link

            def channels(b):
                link = norm_steps(b, 0)
                part = gst[:].rearrange("p k n (a s) -> p k (n a) s", s=3)
                dve.wait_ge(A.gst, (b * NT + NT) * KC)
                link(dve.tensor_reduce(gsm[:, 7, :], part[:, :, :, 1], AX.X, ALU.add))
                dve.tensor_scalar(gmv[:, :, 0], gsm[:, 7, :], 1.0 / (2 * NT), None, ALU.mult).then_inc(A.gmv, 1)
                dve.wait_ge(A.gmv, b + 1)
                link(dve.tensor_tensor(gdv[:], part[:, :, :, 1], gmv[:, :, 0:1].to_broadcast([P, KC, 2 * NT]), ALU.subtract))
                link(dve.tensor_tensor(gdv[:], gdv[:], gdv[:], ALU.mult))
                link(dve.scalar_tensor_tensor(gdv[:], gdv[:], P / 2.0, part[:, :, :, 2], ALU.mult, ALU.add))
                dve.tensor_reduce(gmv[:, :, 1], gdv[:], AX.X, ALU.add).then_inc(A.gst2, 1)

            def about_head(b):
                link = norm_steps(b, 4)
                dve.wait_ge(A.gs, b * 2 + 1)
                link(dve.tensor_copy(gsm[:, 0, :], bank[7][:, 0:KC]))
                link(dve.tensor_tensor(gsm[:, 1, :], gmv[:, :, 0], gsm[:, 0, :], ALU.subtract))
                link(dve.tensor_tensor(gsm[:, 1, :], gsm[:, 1, :], gsm[:, 1, :], ALU.mult))
                dve.wait_ge(A.gst2, b + 1)
                dve.scalar_tensor_tensor(gsm[:, 1, :], gmv[:, :, 1], 1.0 / T, gsm[:, 1, :], ALU.mult, ALU.add).then_inc(A.gs_r, 1)

            def head_variance(b):
                dve.wait_ge(A.gs, b * 2 + 2)
                dve.tensor_scalar(gsm[:, 2, :], bank[7][:, 0:KC], EPS, None, ALU.add).then_inc(A.grv, 1)

            def affine(b):
                link = norm_steps(b, 7)
                dve.wait_ge(A.grs, b + 1)
                link(dve.tensor_tensor(gsm[:, 4, :], gsm[:, 3, :], gnw[:], ALU.mult))
                link(dve.tensor_tensor(gsm[:, 5, :], gsm[:, 0, :], gsm[:, 4, :], ALU.mult))
                dve.tensor_tensor(gsm[:, 6, :], gnb[:], gsm[:, 5, :], ALU.subtract).then_inc(A.gaff, 1)

            def gating(b):
                for k in range(KC):
                    dve.wait_ge(A.yg, b * KC + k + 1)
                    if k == 0:
                        dve.wait_ge(A.g, b * 4 + 4)
                    dve.tensor_tensor(yg[:, k, :], yg[:, k, :], gT[:, k, :], ALU.mult).then_inc(A.gated, 1)

            def residual(b, t, nth):
                if t == 0:
                    dve.wait_ge(R[1].x, b * 16 + 16)
                dve.wait_ge(A.out, b * NT + t + 1)
                dve.tensor_tensor(xr[:, t, :], xr[:, t, :], bank[3 + nth % 2][:, 0:C], ALU.add).then_inc(R[1].o, 1)

            def residual_stats(b, t):
                dve.wait_ge(R[1].o, b * NT + t + 1)
                tile_stats(R[1], lnr, xr, t)

            def residual_slots(b):
                slots(1, b, 0)
                dve.wait_ge(R[1].xnst, b * 16 + 16)

            def sequence(b, tail, front):
                dve.memset(state[:], 0.0).then_inc(A.state0, 1)
                dve.wait_ge(A.state0, b + 1)
                dve.sem_inc(A.stt, 1)
                for i in range(NT):
                    nb = b * NT + i
                    dve.wait_ge(A.qkT, nb + 1)
                    for m in range(4):
                        last = dve.tensor_scalar(km[:, :, m, :], qkT[:, KC:2 * KC, :], K_["headsel"][:, m:m + 1], None, ALU.mult)
                    last.then_inc(A.kmd, 1)
                    if tail is not None and i == 0:
                        channel_stats(tail, NT - 1)
                        channels(tail)
                    if tail is not None and ROUTE_AT[i][:1] == (0,):
                        norm_shift(R[1], lnr, tail)
                    if front is not None and FRONT_AT[i][:1] == (0,):
                        norm_shift(A, lnf, front)
                    if i + 1 < NT or front is not None:
                        rotate(b, i + 1)
                    if i:
                        channel_stats(b, i - 1)
                    mask(b, i, 0)
                    mask(b, i, 1)
                    if tail is not None and i == 0:
                        about_head(tail)
                    dve.wait_ge(A.st, nb + 1)
                    dve.tensor_tensor(stmp[:], bank[6][:, 0:C].rearrange("p (k x) -> p k x", k=KC),
                                      K_["stateblk"].rearrange("p (k x) -> p k x", k=KC), ALU.mult).then_inc(A.st_r, 1)
                    dve.wait_ge(A.st_r, nb + 2)
                    if i + 1 < NT:
                        for k in range(KC):
                            last = dve.scalar_tensor_tensor(state[:, k, :], state[:, k, :], K_["decay"][:, k:k + 1], stmp[:, k, :],
                                                            ALU.mult, ALU.add)
                        last.then_inc(A.stt, 1)
                        dve.wait_ge(A.stt, nb + 2)
                    if tail is not None:
                        if OUT_AT[i][:1] == (0,):
                            gating(tail)
                        if i == COUNT_STEP:
                            weights(1, tail)
                    mask(b, i, 2)
                    mask(b, i, 3)
                    if tail is not None:
                        if i == 0:
                            head_variance(tail)
                            affine(tail)
                        for n, t in enumerate(OUT_AT[i]):
                            residual(tail, t, n)
                        for t in OUT_AT[i]:
                            residual_stats(tail, t)
                        if OUT_AT[i][-1:] == (NT - 1,):
                            norm_stats(R[1], lnr, tail)
                    if front is not None and i == FRONT_STEP:
                        front_stats(front)
                    if tail is not None:
                        if i == COUNT_STEP - 1:
                            choices(1, tail)
                        if i == COUNT_STEP:
                            residual_slots(tail)

            start_route(1)
            front_stats(0)
            norm_shift(A, lnf, 0)
            dve.wait_ge(S0.rope, NT * 16)
            rotate(0, 0)
            sequence(0, None, 1)
            with dve.Fori(0, B - 2) as i:
                sequence(i + 1, i, i + 2)
            sequence(B - 1, B - 2, None)
            channel_stats(B - 1, NT - 1)
            channels(B - 1)
            about_head(B - 1)
            head_variance(B - 1)
            affine(B - 1)
            gating(B - 1)
            for t in range(NT):
                residual(B - 1, t, t)
                residual_stats(B - 1, t)
            norm_stats(R[1], lnr, B - 1)
            norm_shift(R[1], lnr, B - 1)
            choices(1, B - 1)
            weights(1, B - 1)
            residual_slots(B - 1)
            ffn(1)


GATE_AT = (4, 6)
OUT_AT = ((), (0, 1), (2, 3, 4), (5, 6, 7), (), (), (), ())
ROUTE_AT = ((), (), (), (), (0, 1, 2, 3), (4, 5, 6, 7), (), ())
COUNT_STEP = 7
FRONT_STEP = 4
FRONT_AT = ((), (), (), (), (), (0, 1), (2, 3), (4, 5, 6, 7))


def third(tiles, q):
    return tiles[len(tiles) * q // 3:len(tiles) * (q + 1) // 3]


BANK_USES = NT + 2 + NT // 2 + NT // 2

EXP_LINK, OH_LINK, WEIGHT_LINK, LINKS = 3, 12, 18, 35
GLINKS = 9
LN_STEPS = 5


def shape_constants():
    p = np.arange(P)
    h = np.arange(H, dtype=np.float32)
    gamma = (np.float32(1.0) - np.float32(2.0) ** (np.float32(-5.0) - h)).astype(np.float64)
    at, n = const_at()
    c = np.zeros((P, n), np.float32)

    def put(name, a):
        c[:, at[name][0]:at[name][1]] = a

    head = p // D
    put("ident", np.eye(P))
    put("before", p[:, None] < p[None, :])
    put("causal", p[:, None] <= p[None, :])
    same = head[:, None] == head[None, :]
    put("headmean", same / D)
    decay = np.stack([gamma[k * HH + head] ** P for k in range(KC)], 1)
    put("stateblk", np.concatenate([same * decay[:, k:k + 1] for k in range(KC)], 1))
    put("headsel", head[:, None] == np.arange(HH)[None, :])
    put("decay", decay)
    put("revexp", (E - np.arange(E))[None, :])
    put("restart", (np.arange(RT * E) % NT != 0)[None, :])
    put("slotbase", (E * TOPK * CAP + np.arange(RT) // NT * CAP)[None, :])
    put("mhalf", -0.5)
    put("ids", np.arange(NT)[None, :] * P + p[:, None])
    half = np.arange(0, D, 2, dtype=np.float32)
    inv = (np.float32(1.0) / np.float32(10000.0) ** (half / np.float32(D))).astype(np.float32)
    t = np.arange(T, dtype=np.float32)
    ang = (t[:, None] * inv[None, :]).astype(np.float32).astype(np.float64)
    vec = ((half + np.float32(0.4 * D)) / np.float32(1.4 * D)).astype(np.float64)
    scale = vec[None, :] ** ((t.astype(np.float64) - T // 2) / 512.0)[:, None]
    tau = (np.arange(T) % P).astype(np.float64)
    rope = np.zeros((T, 2, 2, H, D))
    for w, s, g in ((0, scale * D ** -0.5, tau), (1, 1.0 / scale, -tau)):
        dec = gamma[None, :] ** g[:, None]
        for half_ in range(2):
            rope[:, 0, w, :, half_::2] = (np.cos(ang) * s)[:, None, :] * dec[:, :, None]
            rope[:, 1, w, :, half_::2] = (np.sin(ang) * s * (-1.0 if half_ == 0 else 1.0))[:, None, :] * dec[:, :, None]
    rope = rope.reshape(NT, P, 2, 2 * C).astype(np.float32)
    slots = np.zeros((SLOTS, 2), np.uint32)
    slots[:, 0] = N + np.arange(SLOTS) % G
    return c, rope, slots.view(np.float32)


_INS = ["L0_attn_x", "L0_attn_w_qkv", "L0_attn_w_gated", "L0_attn_w_proj", "L0_attn_gn_weight", "L0_attn_gn_bias",
        "L0_ffn_router_w", "L0_ffn_w1", "L0_ffn_w2", "L0_ffn_bias"]


def kernel(**inputs):
    import concourse.bacc as bacc
    from concourse.bass_utils import run_bass_kernel_spmd

    nc = bacc.Bacc("TRN2", target_bir_lowering=False, num_devices=1)
    arrays = {name: np.ascontiguousarray(inputs[name]) for name in _INS}
    arrays["L0_attn_x"] = arrays["L0_attn_x"].reshape(N, C)
    arrays["consts"], arrays["rope"], arrays["slots"] = shape_constants()
    args = [nc.dram_tensor(f"in_{n}", a.shape, mybir.dt.from_np(a.dtype), kind="ExternalInput").ap() for n, a in arrays.items()]
    out = nc.dram_tensor("out_rows", (ROWS, C), DT.float32, kind="ExternalOutput").ap()
    macaron_kernel(nc, *args, out)
    r = run_bass_kernel_spmd(nc, [{f"in_{n}": a for n, a in arrays.items()}], core_ids=[0])
    return r.results[0]["out_rows"][0:N].reshape(B, T, C)
```

```python
import numpy as np
import concourse.bass as bass
from concourse import mybir
from contextlib import ExitStack

DT = mybir.dt
ALU = mybir.AluOpType
ACT = mybir.ActivationFunctionType
AX = mybir.AxisListType

P = 128
B, T, C = 8, 1024, 256
N = B * T
NT = T // P
KC = C // P
H, D = 16, 16
HH = H // KC
E, TOPK, FF = 8, 2, 1024
CAP = N // E
FJ = FF // P
G = 512
GT = G // P
GE = 2 * CAP // G
NP = TOPK * E // 2
NG = NP * GE
SLOTS = NG * G
ROWS = N + G
EPS = 1e-5
BIG = 1.0e6
RT = TOPK * NT

CONST_COLS = dict(ident=P, before=P, causal=P, headmean=P, stateblk=C, headsel=HH, decay=KC,
                  revexp=E, restart=RT * E, slotbase=RT, mhalf=RT, ids=NT)


def const_at():
    at, out = 0, {}
    for name, n in CONST_COLS.items():
        out[name] = (at, at + n)
        at += n
    return out, at


class Names(dict):
    __getattr__ = dict.__getitem__


class Count:

    def __init__(self):
        self.n, self.shift = 0, 0

    def up(self, k=1):
        self.n += k
        return self.n + self.shift

    def enter(self, i, per):
        self.per, self.start, self.shift = per, self.n, i * per

    def leave(self, times):
        assert self.n - self.start == self.per, (self.n - self.start, self.per)
        self.n, self.shift = self.start + self.per * times, 0


def macaron_kernel(nc, x_in, w_qkv, w_gated, w_proj, gn_w, gn_b, router_w, w1, w2, f_bias,
                   consts_in, rope_in, slots_in, out):
    fp32, f32r, u32 = DT.float32, DT.float32r, DT.uint32
    ctx = ExitStack()
    with ctx:
        def sb(name, shape, dt=fp32, mem=ctx):
            return mem.enter_context(nc.sbuf_tensor(name, shape, dt))

        def sems(prefix, names):
            return Names({n: ctx.enter_context(nc.semaphore(f"{prefix}_{n}")) for n in names.split()})

        acc1 = nc.dram_tensor("acc1", [ROWS, C], fp32).ap()
        xn_d = nc.dram_tensor("xn_rows", [ROWS, C], fp32).ap()
        slot_d = [nc.dram_tensor(f"slot_table{r}", [SLOTS, 2], fp32).ap() for r in range(2)]

        at, ncol = const_at()
        cst = sb("cst", [P, ncol])
        K_ = {n: cst[:, a:b] for n, (a, b) in at.items()}
        ident, before, causal, headmean = (K_[n] for n in ("ident", "before", "causal", "headmean"))
        ones = sb("ones", [P, P])
        hbias = sb("hbias", [P, C])
        gnw, gnb = sb("gnw", [P, KC]), sb("gnb", [P, KC])
        rw = sb("rw", [P, KC, E])
        wTh, wTl = sb("wTh", [P, KC, 5 * C], f32r), sb("wTl", [P, KC, 5 * C], f32r)
        W_QK, W_V, W_G, W_P = 0, 2 * C, 3 * C, 4 * C

        wraw = sb("wraw", [P, 10, C])
        zrow = sb("zrow", [P, GT, C])

        xb = sb("xb", [P, NT, C])
        xr = sb("xr", [P, NT, C])
        xn_r = sb("xn_r", [P, NT, C])
        xrT = sb("xrT", [P, 4, KC, P])
        vz = sb("vz", [P, 2, H * 2 * D])

        def stats(n):
            return Names(st=sb(n + "_st", [P, NT, 6]), mv=sb(n + "_mv", [P, 5, NT]), rv=sb(n + "_rv", [P, NT]),
                                   rs=sb(n + "_rs", [P, NT]), nm=sb(n + "_nm", [P, NT]))

        lnf, lnr = stats("lnf"), stats("lnr")
        gst, gmv = sb("gst", [P, KC, NT, 6]), sb("gmv", [P, KC, 2])
        gsm, gdv = sb("gsm", [P, 8, KC]), sb("gdv", [P, KC, 2 * NT])
        dl, ex, d2 = (sb(n, [P, NT, E]) for n in ("dl", "ex", "d2"))
        key = sb("key", [P, TOPK, NT, E])
        oh = sb("oh", [P, TOPK, NT, E])
        cnt, scn = sb("cnt", [P, TOPK, E, NT]), sb("scn", [P, TOPK, E, NT])
        pos = sb("pos", [P, TOPK, NT, E])
        base = sb("base", [P, TOPK, E])
        red = sb("red", [P, 4, NT])
        sel = sb("sel", [P, 8, RT])
        ids = sb("ids", [P, NT])
        pay = sb("pay", [P, B, RT, 2])
        idx = sb("idx", [P, B, RT], u32)
        tab = sb("tab", [P, GE, GT, 2])

        with ExitStack() as mem:
            stg1, stg2 = sb("stg1", [P, KC, FF], fp32, mem), sb("stg2", [P, FJ, C], fp32, mem)
            w1h, w1l = sb("w1h", [P, KC, FF], f32r, mem), sb("w1l", [P, KC, FF], f32r, mem)
            w2h, w2l = sb("w2h", [P, FJ, C], f32r, mem), sb("w2l", [P, FJ, C], f32r, mem)
            xe_both = sb("xe", [P, 2 * GT, C], fp32, mem)
            xe = [xe_both[:, i * GT:(i + 1) * GT, :] for i in range(2)]
            x_half = xe_both[:, 0:NT, :]
            xh = [sb(f"xh{i}", [P, KC, G], f32r, mem) for i in range(2)]
            xl = [sb(f"xl{i}", [P, KC, G], f32r, mem) for i in range(2)]
            h32 = [sb(f"h32_{i}", [P, G], fp32, mem) for i in range(2)]
            hh, hl = sb("hh", [P, FJ, G], f32r, mem), sb("hl", [P, FJ, G], f32r, mem)
            yb_both = sb("yb", [P, 2 * GT, C], fp32, mem)
            yb = [yb_both[:, i * GT:(i + 1) * GT, :] for i in range(2)]
            xn_odd = yb_both[:, 0:NT, :]

        rope = sb("rope", [P, NT, 2, 2 * C])
        xnh, xnl = sb("xnh", [P, KC, T], f32r), sb("xnl", [P, KC, T], f32r)
        qk = sb("qk", [P, 2, 2 * C])
        qkT = sb("qkT", [P, 2 * KC, P])
        qm = sb("qm", [P, KC, HH, P])
        aw = sb("aw", [P, 4, 4, P])
        rt1, rt2 = sb("rt1", [P, 2, 2 * C]), sb("rt2", [P, 2, 2 * C])
        state, stmp = sb("state", [P, KC, P]), sb("stmp", [P, KC, P])
        xn_f = sb("xn_f", [P, 4, C])
        gT, yT, yg = sb("gT", [P, KC, T]), sb("yT", [P, KC, T]), sb("yg", [P, KC, T])
        y0 = sb("y0", [P, KC, P])
        ygh, ygl = sb("ygh", [P, KC, T], f32r), sb("ygl", [P, KC, T], f32r)

        bank = [ctx.enter_context(nc.psum_tensor(f"bank{i}", [P, 512], fp32)) for i in range(8)]

        S0 = sems("setup", "const vec rw zero acc_z out_z xn_z slot0 slot1 rope wraw wT wTh wTl bias memset base passed")
        RN = "x x_odd lnst lnmv lnrv lnrs lnnm xn xnst trp trp_r xT xT_r sm sm_r exp link pay scat scat1 sent stored half o"
        R = [sems(f"route{r}", RN) for r in range(2)]
        F = [sems(f"ffn{r}", "w1raw w2raw w1h w1l w2h w2l tab0 tab1 tab2 tab3 xe0 xe1 xT xh xl up gelu hh hl down y add")
             for r in range(2)]
        A = sems("attn", "x lnst lnmv lnrv lnrs lnnm xn qk qk_r v v_r t t_r roped vz qkT qm "
                         "sc aw y y_r st st_r stt state0 g f gst gst2 gmv gs gs_r glink grv grs gaff yg moved gated ygh ygl fl out")

        block = ctx.enter_context(nc.Block())
        tok = lambda a: a[0:N, :].rearrange("(b t p) c -> b p t c", t=NT, p=P)
        x_t, acc1_t, xn_t, out_t = tok(x_in), tok(acc1), tok(xn_d), tok(out)
        spare = lambda a: a[N:ROWS, :].rearrange("(t p) c -> p t c", p=P)

        def held(eng, sem, value):
            eng.wait_ge(sem, value)
            eng.sem_inc(S0.passed, 1)

        @block.sync
        def _(sp):
            def ffn_weights(r):
                sp.dma_start(stg1[:], w1_t[0, :, :, :]).then_inc(F[r].w1raw, 16)
                sp.dma_start(stg2[:], w2_t[0, :, :, :]).then_inc(F[r].w2raw, 16)

            w1_t = w1.rearrange("e (k p) f -> e p k f", p=P)
            w2_t = w2.rearrange("e (j p) c -> e p j c", p=P)

            def route_store(S, b, x, xn, dst, halves):
                sp.wait_ge(S.xn, b * NT + NT)
                sp.dma_start(xn_t[b, :, :, :], xn).then_inc(S.xnst, 16)
                sp.wait_ge(S.half, b * halves + halves)
                sp.dma_start(dst[b, :, :, :], x).then_inc(S.stored, 16)

            xs, xns, x_here = (xr, xb), (xn_r[:], xn_odd), (R[0].x, R[0].x_odd)
            sp.dma_start(xs[0][:], x_t[0, :, :, :]).then_inc(x_here[0], 16)
            sp.dma_start(cst[:], consts_in).then_inc(S0.const, 16)
            sp.dma_start(rw[:], router_w.rearrange("(k p) e -> p k e", p=P)).then_inc(S0.rw, 16)
            sp.dma_start(hbias[:], f_bias.rearrange("a b c -> (a b) c").to_broadcast([P, C])).then_inc(S0.vec, 16)
            sp.dma_start(xs[1][:], x_t[1, :, :, :]).then_inc(x_here[1], 16)
            sp.dma_start(slot_d[0], slots_in).then_inc(S0.slot0, 16)
            sp.dma_start(slot_d[1], slots_in).then_inc(S0.slot1, 16)
            sp.wait_ge(S0.zero, 1)
            sp.dma_start(spare(acc1), zrow[:]).then_inc(S0.acc_z, 16)
            sp.dma_start(spare(out), zrow[:]).then_inc(S0.out_z, 16)
            sp.dma_start(spare(xn_d), zrow[:]).then_inc(S0.xn_z, 16)
            for k in range(KC):
                half = lambda v: v[k * P:(k + 1) * P].rearrange("(p a) -> p a", a=1)
                sp.dma_start(gnw[:, k:k + 1], half(gn_w)).then_inc(S0.vec, 16)
                sp.dma_start(gnb[:, k:k + 1], half(gn_b)).then_inc(S0.vec, 16)
            sp.dma_start(wraw[:, 0:6, :], w_qkv.rearrange("(j p) c -> p j c", p=P)).then_inc(S0.wraw, 16)
            sp.dma_start(wraw[:, 6:8, :], w_gated.rearrange("(j p) c -> p j c", p=P)).then_inc(S0.wraw, 16)
            sp.dma_start(wraw[:, 8:10, :], w_proj.rearrange("(j p) c -> p j c", p=P)).then_inc(S0.wraw, 16)
            with sp.Fori(0, B // 2 - 1) as p:
                for q in range(2):
                    b = p * 2 + q
                    route_store(R[0], b, x_half, xns[q], acc1_t, 1)
                    sp.dma_start(xs[q][:], x_t[b + 2, :, :, :]).then_inc(x_here[q], 16)
                    held(sp, R[0].xnst, b * 16 + 16)
            ffn_weights(0)
            for q in range(2):
                route_store(R[0], B - 2 + q, x_half, xns[q], acc1_t, 1)

            def ffn(r):
                f = F[r]
                tab_t = slot_d[r].rearrange("(g p t) w -> g p t w", p=P, t=GT)

                def next_w1(q, e):
                    sp.wait_ge(f.w1l, q * FJ)
                    sp.dma_start(stg1[:], w1_t[e, :, :, :]).then_inc(f.w1raw, 16)

                def next_w2(q, e):
                    sp.wait_ge(f.w2l, q * FJ)
                    sp.dma_start(stg2[:], w2_t[e, :, :, :]).then_inc(f.w2raw, 16)

                def pair(p, wraps):
                    for j in range(GE):
                        q = p * 2 + j // 2
                        if j % 2 == 0:
                            next_w2(q + 1, q + 1 - wraps[j])
                        else:
                            next_w1(q + 2, q + 2 - wraps[j])
                        held(sp, f.add, p * (GE * GT * 16) + (j + 1) * GT * 16)
                        sp.dma_start(tab[:, j, :, :], tab_t[p * GE + GE + j, :, :, :]).then_inc(tabs[j], 16)

                tabs = [f.tab0, f.tab1, f.tab2, f.tab3]
                if r == 0:
                    sp.wait_ge(S0.acc_z, 16)
                    sp.wait_ge(S0.out_z, 16)
                    sp.wait_ge(S0.xn_z, 16)
                sp.wait_ge(R[r].scat, B * NT * 16)
                for j in range(GE):
                    sp.dma_start(tab[:, j, :, :], tab_t[j, :, :, :]).then_inc(tabs[j], 16)
                next_w1(1, 1)
                with sp.Fori(0, NP // 2 - 1) as p:
                    pair(p, (0, 0, 0, 0))
                sp.wait_ge(R[r].scat1, B * NT * 16)
                pair(NP // 2 - 1, (0, E, E, E))
                with sp.Fori(NP // 2, NP - 1) as p:
                    pair(p, (E, E, E, E))
                next_w2(TOPK * E - 1, E - 1)

            ffn(0)

            def front(b):
                sp.wait_ge(A.xn, b * NT + 1)
                sp.dma_start(xb[:], acc1_t[b, :, :, :]).then_inc(A.x, 16)

            def tail(b):
                sp.dma_start(xr[:], acc1_t[b, :, :, :]).then_inc(R[1].x, 16)
                route_store(R[1], b, xr[:], xn_r[:], out_t, NT)
                held(sp, R[1].stored, b * 16 + 16)

            sp.wait_ge(F[0].add, NG * GT * 16)
            sp.sem_inc(A.xn, 1)
            front(0)
            for t in range(NT):
                sp.dma_start(rope[:, t, :, :], rope_in[t, :, :, :]).then_inc(S0.rope, 16)
            front(1)
            with sp.Fori(0, B - 2) as i:
                front(i + 2)
                tail(i)
            tail(B - 2)
            sp.wait_ge(A.y, B * NT)
            ffn_weights(1)
            tail(B - 1)
            ffn(1)
            sp.wait_ge(F[1].add, NG * GT * 16)

        @block.gpsimd
        def _(pool):
            pool.memset(zrow[:], 0.0).then_inc(S0.zero, 1)
            pool.memset(ones[:], 1.0).then_inc(S0.memset, 1)
            pool.memset(vz[:], 0.0).then_inc(S0.memset, 1)
            pool.wait_ge(S0.const, 16)

            def power(S, ln, b):
                held(pool, S.lnrv, b + 1)
                pool.tensor_tensor(ln.rs[:], ln.rv[:], K_["mhalf"][:, 0:NT], ALU.pow).then_inc(S.lnrs, 1)

            def scatter(r, b, q, some):
                if 0 in some:
                    held(pool, R[r].pay, b + 1)
                for n in some:
                    pool.indirect_dma_start(
                        out=slot_d[r], out_offset=bass.IndirectOffsetOnAxis(ap=idx[:, q, n:n + 1], axis=0),
                        in_=pay[:, q, n, :], in_offset=None, bounds_check=SLOTS - 1, oob_is_err=False)\
                        .then_inc(R[r].scat if n < NT else R[r].scat1, 16)

            def scattered(r, b):
                for sem in (R[r].scat, R[r].scat1):
                    held(pool, sem, b * NT * 16 + NT * 16)
                pool.sem_inc(R[r].sent, 1)

            FIRST, SECOND = range(NT), range(NT, RT)

            lns = (lnr, lnf)
            power(R[0], lns[0], 0)
            pool.wait_ge(S0.slot0, 16)
            pool.wait_ge(S0.slot1, 16)
            for b in range(B):
                if b + 1 < B:
                    power(R[0], lns[(b + 1) % 2], b + 1)
                scatter(0, b, b, FIRST)

            def ffn(r):
                f = F[r]
                tabs = [f.tab0, f.tab1, f.tab2, f.tab3]
                xes = [f.xe0, f.xe1]
                dst = acc1 if r == 0 else out
                tabu = tab[:].bitcast(u32)

                def gather(j, waits):
                    for sem, value in waits:
                        held(pool, sem, value)
                    for t in range(GT):
                        pool.indirect_dma_start(
                            out=xe[j % 2][:, t, :], out_offset=None, in_=xn_d,
                            in_offset=bass.IndirectOffsetOnAxis(ap=tabu[:, j, t, 0:1], axis=0),
                            bounds_check=ROWS - 1, oob_is_err=True).then_inc(xes[j % 2], 16)

                def add(p, j, end):
                    if not end:
                        held(pool, f.y, p * GE * GT + (j + 1) * GT)
                    if not (isinstance(p, int) and p == 0 and j == 0):
                        held(pool, f.add, p * (GE * GT * 16) + j * GT * 16)
                    for t in range(GT):
                        if end:
                            held(pool, f.y, p * GE * GT + j * GT + t + 1)
                        pool.indirect_dma_start(
                            out=dst, out_offset=bass.IndirectOffsetOnAxis(ap=tabu[:, j, t, 0:1], axis=0),
                            in_=yb[j % 2][:, t, :], in_offset=None, compute_op=ALU.add,
                            bounds_check=ROWS - 1, oob_is_err=True).then_inc(f.add, 16)

                held(pool, R[r].stored, B * 16)
                held(pool, R[r].xnst, B * 16)
                gather(0, [(f.tab0, 16)])
                gather(1, [(f.tab1, 16)])
                gather(2, [(f.tab2, 16), (f.xT, 1)])

                def pair(p, last, late):
                    for j in range(GE):
                        add(p, j, last and j == GE - 1)
                        g3 = j + 3
                        if not (last and g3 >= GE):
                            gather(g3 % GE, [(tabs[g3 % GE], p * 16 + 16 * (g3 // GE) + 16), (f.xT, p * GE + j + 2)])
                        if late and late[j] is not None:
                            scatter(r, late[j], late[j] if r == 0 else 0, SECOND)

                if r == 0:
                    pair(0, False, (0, 1, 2, 3))
                    pair(1, False, (4, 5, 6, 7))
                else:
                    pair(0, False, (B - 1, None, None, None))
                    pair(1, False, None)
                with pool.Fori(2, NP - 1) as p:
                    pair(p, False, None)
                pair(NP - 1, True, None)

            ffn(0)

            def gn_power(b):
                held(pool, A.grv, b + 1)
                pool.tensor_tensor(gsm[:, 3, :], gsm[:, 2, :], K_["mhalf"][:, 0:KC], ALU.pow).then_inc(A.grs, 1)

            def residual_power(b):
                power(R[1], lnr, b)

            def half_bias(b, t):
                held(pool, R[1].xn, b * NT + t + 1)
                pool.tensor_tensor(xr[:, t, :], xr[:, t, :], hbias[:], ALU.add).then_inc(R[1].half, 1)

            def rotated(b, i):
                held(pool, A.qk_r, b * NT + i + 2)
                pool.tensor_tensor(qk[:, i % 2, :], rt1[:, i % 2, :], rt2[:, i % 2, :], ALU.add).then_inc(A.roped, 1)

            def first_output(b, tail):
                held(pool, A.y_r, b * NT + 2)
                if tail is not None:
                    held(pool, A.yg, tail * KC + KC)
                pool.tensor_copy(yT[:, :, 0:P], y0[:]).then_inc(A.moved, 1)

            def sequence(b, tail, front, sent):
                for i in range(NT):
                    if i + 1 < NT or front is not None:
                        rotated(b, i + 1)
                    if i == 1:
                        first_output(b, tail)
                    if tail is not None:
                        if i == 0:
                            gn_power(tail)
                        if sent is not None:
                            scatter(1, sent, 0, SENT_AT[i])
                            if SENT_AT[i][-1:] == (RT - 1,):
                                scattered(1, sent)
                        for t in BIAS_AT[i]:
                            half_bias(tail, t)
                        if OUT_AT[i][-1:] == (NT - 1,):
                            residual_power(tail)
                    if front is not None and STATS_AT[i][-1:] == (NT - 1,):
                        power(A, lnf, front)

            power(A, lnf, 0)
            rotated(0, 0)
            sequence(0, None, 1, None)
            sequence(1, 0, 2, None)
            with pool.Fori(1, B - 2) as b:
                sequence(b + 1, b, b + 2, b - 1)
            sequence(B - 1, B - 2, None, B - 3)
            gn_power(B - 1)
            scatter(1, B - 2, 0, range(RT))
            residual_power(B - 1)
            scattered(1, B - 2)
            for t in range(NT):
                half_bias(B - 1, t)
            scatter(1, B - 1, 0, FIRST)
            ffn(1)

        @block.tensor
        def _(pe):
            pe.wait_ge(S0.const, 16)
            def route_tile(r, b, t, xn, tr_free, tr_full):
                S = R[r]
                pe.wait_ge(S.xn, b * NT + t + 1)
                tr_free(t)
                for k in range(KC):
                    last = pe.transpose(bank[1 + t % 2][:, k * P:(k + 1) * P], xn[:, t, k * P:(k + 1) * P], ident)
                last.then_inc(tr_full(t), 1)
                if t >= 2:
                    logits(S, b, t - 2)

            def counts(r, b):
                S = R[r]
                pe.wait_ge(S.link, b * LINKS + OH_LINK)
                pe.wait_ge(S.sm_r, b * 2 + 2)
                pe.matmul(bank[7][:, 0:RT * E], before, oh[:].rearrange("p k t e -> p (k t e)"), start=True, stop=True)
                pe.matmul(bank[7][:, RT * E:2 * RT * E], ones[:], oh[:].rearrange("p k t e -> p (k t e)"), start=True, stop=True)\
                    .then_inc(S.sm, 1)

            def logits(S, b, t):
                pe.wait_ge(S.xT, b * NT + t + 1)
                if t == 0:
                    pe.wait_ge(S.sm_r, b * 2 + 1)
                for k in range(KC):
                    last = pe.matmul(bank[7][:, t * E:(t + 1) * E], xrT[:, t % 4, k, :], rw[:, k, :],
                                     start=(k == 0), stop=(k == KC - 1))
                last.then_inc(S.xT_r if t < NT - 1 else S.sm, 1)

            pe.wait_ge(S0.rw, 16)
            pe.wait_ge(S0.memset, 2)
            with pe.Fori(0, B // 2) as p:
                for q, xn in enumerate((xn_r, xn_odd)):
                    b = p * 2 + q
                    for t in range(NT):
                        route_tile(0, b, t, xn, lambda t: pe.wait_ge(R[0].trp_r, b * NT + t + 1), lambda t: R[0].trp)
                    for t in range(NT - 2, NT):
                        logits(R[0], b, t)
                    counts(0, b)

            def ffn(r):
                f = F[r]
                xes = [f.xe0, f.xe1]

                def transposes(j, xe_value, xl_value):
                    pe.wait_ge(xes[j % 2], xe_value)
                    if xl_value is not None:
                        pe.wait_ge(f.xl, xl_value)
                    for k in range(KC):
                        for t in range(GT):
                            last = pe.transpose(bank[6 + k][:, t * P:(t + 1) * P], xe[j % 2][:, t, k * P:(k + 1) * P], ident)
                    last.then_inc(f.xT, 1)

                def up(j, fj, up_free):
                    if up_free is not None:
                        pe.wait_ge(f.gelu, up_free)
                    n = 0
                    for k in range(KC):
                        w = slice(fj * P, (fj + 1) * P)
                        for a, c in ((w1h, xh), (w1h, xl), (w1l, xh)):
                            last = pe.matmul(bank[fj % 2][:], a[:, k, w], c[j % 2][:, k, :], start=(n == 0), stop=(n == 5))
                            n += 1
                    last.then_inc(f.up, 1)

                def down(j, fj, tiles=range(GT)):
                    for t in tiles:
                        s = slice(t * P, (t + 1) * P)
                        o = bank[2 + 2 * (j % 2) + t // 2][:, (t % 2) * C:(t % 2 + 1) * C]
                        for n, (a, c) in enumerate(((hh, w2h), (hh, w2l), (hl, w2h))):
                            last = pe.matmul(o, a[:, fj, s], c[:, fj, :], start=(fj == 0 and n == 0 and t % 2 == 0),
                                             stop=(fj == FJ - 1 and n == 2), skip_group_check=True)
                    if fj == FJ - 1:
                        last.then_inc(f.down, 1)

                transposes(0, GT * 16, None)
                transposes(1, GT * 16, KC)
                pe.wait_ge(f.w1l, FJ)
                pe.wait_ge(f.xl, KC)
                for fj in range(FJ):
                    up(0, fj, None if fj < 2 else fj - 1)

                def pair(p, last, first):
                    for j in range(GE - last):
                        for fj in range(FJ):
                            if fj == 0:
                                if not first or j >= 2:
                                    pe.wait_ge(f.y, (p * GE + j - 1) * GT)
                            if j % 2 == 0:
                                pe.wait_ge(f.w2l, (p * 2 + j // 2) * FJ + fj + 1)
                            pe.wait_ge(f.hl, (p * GE + j) * FJ + fj + 1)
                            down(j, fj)
                            if fj == 0:
                                pe.wait_ge(f.xl, (p * GE + j + 2) * KC)
                            if j % 2 == 1:
                                pe.wait_ge(f.w1l, (p * 2 + j // 2 + 1) * FJ + fj + 1)
                            up((j + 1) % GE, fj, (p * GE + j + 1) * FJ + fj - 1)
                            if fj == 5 and not (last and j + 2 >= GE):
                                jj = (j + 2) % GE
                                transposes(jj, (p * (GE // 2) + (j + 2) // 2 + 1) * GT * 16, (p * GE + j + 2) * KC)

                pair(0, False, True)
                with pe.Fori(1, NP - 1) as p:
                    pair(p, False, False)
                pair(NP - 1, True, False)
                pe.wait_ge(f.y, (NG - 2) * GT)
                for tiles in (range(GT // 2), range(GT // 2, GT)):
                    for fj in range(FJ):
                        pe.wait_ge(f.hl, (NG - 1) * FJ + fj + 1)
                        down(GE - 1, fj, tiles)

            pe.wait_ge(R[0].sm_r, 2 * B + 1)
            pe.wait_ge(R[0].trp_r, N // P + 2)
            pe.wait_ge(S0.wraw, 48)
            for n in range(20):
                j, k = n // KC, n % KC
                if n >= 4:
                    pe.wait_ge(S0.wTl, n - 3)
                pe.transpose(bank[n % 4][:, 0:P], wraw[:, j, k * P:(k + 1) * P], ident).then_inc(S0.wT, 1)
            pe.wait_ge(S0.wTl, 20)
            ffn(0)

            c1, c2 = Count(), Count()
            shared, fulls, frees = (c1, c2), (A.v, A.t), (A.v_r, A.t_r)

            def front_tile(b, t):
                pe.wait_ge(A.xn, b * NT + t + 2)
                pe.wait_ge(frees[t % 2], shared[t % 2].up())
                for k in range(KC):
                    last = pe.transpose(bank[1 + t % 2][:, k * P:(k + 1) * P], xn_f[:, t % 4, k * P:(k + 1) * P], ident)
                last.then_inc(fulls[t % 2], 1)

            def split_product(out, x_h, x_l, w_h, w_l, weights_left=False):
                n = 0
                for k in range(KC):
                    for x, w in ((x_h, w_h), (x_h, w_l), (x_l, w_h)):
                        a, c = (w, x) if weights_left else (x, w)
                        last = pe.matmul(out, a(k), c(k), start=(n == 0), stop=(n == 3 * KC - 1))
                        n += 1
                return last

            def w_parts(first, n):
                return (lambda k: wTh[:, k, first:first + n]), (lambda k: wTl[:, k, first:first + n])

            def project(b, i):
                s = slice(i % NT * P, (i % NT + 1) * P)
                x_parts = (lambda k: xnh[:, k, s]), (lambda k: xnl[:, k, s])
                pe.wait_ge(A.fl, b * NT + i + 1)
                pe.wait_ge(A.qk_r, b * NT + i + 1)
                split_product(bank[0][:], *x_parts, *w_parts(W_QK, 2 * C)).then_inc(A.qk, 1)
                pe.wait_ge(A.v_r, c1.up())
                split_product(bank[1][:, 0:C], *x_parts, *w_parts(W_V, C)).then_inc(A.v, 1)

            def gate(half):
                s = slice(half * 512, (half + 1) * 512)
                x_parts = (lambda k: xnh[:, k, s]), (lambda k: xnl[:, k, s])
                for m in (1, 0):
                    pe.wait_ge(frees[m], shared[m].up())
                    split_product(bank[1 + m][:], *x_parts, *w_parts(W_G + m * P, P), True).then_inc(fulls[m], 1)

            def scores(b, i, q):
                half, four = q % 2, q // 2
                if half == 0:
                    pe.wait_ge(A.qm, (b * NT + i) * 2 + four + 1)
                pe.wait_ge(A.aw, (b * NT + i) * 4 + q + 1)
                pe.matmul(bank[3 + half][:], qkT[:, KC + half, :], qm[:, half, four * 4:four * 4 + 4, :].rearrange("p m x -> p (m x)"),
                          start=True, stop=True).then_inc(A.sc, 1)

            def attend(b, i, q):
                half, four = q % 2, q // 2
                pe.wait_ge(A.aw, (b * NT + i) * 4 + q + 3)
                for m in (0, 2, 1, 3):
                    h = half * HH + four * 4 + m
                    r = 32 * ((four * 4 + m) // 2)
                    last = pe.matmul(bank[5][r:r + 32, half * P:(half + 1) * P], vz[:, i % 2, h * 32:(h + 1) * 32],
                                     aw[:, q, m, :], start=False, stop=(m % 2 == 1), skip_group_check=True)
                if q == 3:
                    last.then_inc(A.y, 1)

            def head_means(b):
                pe.wait_ge(A.gmv, b + 1)
                pe.wait_ge(R[1].sm_r, b * 2 + 1)
                pe.matmul(bank[7][:, 0:KC], headmean, gmv[:, :, 0], start=True, stop=True).then_inc(A.gs, 1)

            def head_variances(b):
                pe.wait_ge(A.gs_r, b + 1)
                pe.matmul(bank[7][:, 0:KC], headmean, gsm[:, 1, :], start=True, stop=True).then_inc(A.gs, 1)

            def out_tile(b, t, nth):
                s = slice(t * P, (t + 1) * P)
                if t == 0:
                    pe.wait_ge(A.ygl, b * KC + KC)
                if nth >= 2:
                    pe.wait_ge(R[1].o, b * NT + t - 1)
                split_product(bank[3 + nth % 2][:, 0:C], lambda k: ygh[:, k, s], lambda k: ygl[:, k, s], *w_parts(W_P, C)).then_inc(A.out, 1)

            def residual_route(b, t):
                if t == 0:
                    pe.wait_ge(A.grv, b + 1)
                route_tile(1, b, t, xn_r, lambda t: pe.wait_ge(frees[t % 2], shared[t % 2].up()), lambda t: fulls[t % 2])

            def turn(b, i):
                pe.wait_ge(A.roped, b * NT + i + 1)
                pe.wait_ge(A.t_r, c2.up())
                for n in range(2 * KC):
                    last = pe.transpose(bank[2][:, n * P:(n + 1) * P], qk[:, i % 2, n * P:(n + 1) * P], ident)
                last.then_inc(A.t, 1)

            def sequence(b, tail, front):
                for i in range(NT):
                    more = i + 1 < NT or front is not None
                    if more:
                        project(b, i + 1)
                    if tail is not None and i == 1:
                        head_variances(tail)
                    if i in GATE_AT:
                        gate(GATE_AT.index(i))
                    pe.wait_ge(A.vz, b * NT + i + 1)
                    pe.wait_ge(A.st_r, b * NT + i + 1)
                    for k in range(KC):
                        v = vz[:, i % 2, k * HH * 32:(k + 1) * HH * 32].rearrange("p (m x) -> p m x", x=64)
                        v = v.rearrange("p m (a y) -> p m a y", y=16)[:, :, 0:4:3, :]
                        last = pe.matmul(bank[6][:, k * P:(k + 1) * P], qk[:, i % 2, C + k * P:C + (k + 1) * P], v, start=True, stop=True)
                    last.then_inc(A.st, 1)
                    if tail is not None and OUT_AT[i]:
                        for n, t in enumerate(OUT_AT[i]):
                            out_tile(tail, t, n)
                        pe.wait_ge(R[1].o, tail * NT + OUT_AT[i][-1] + 1)
                    scores(b, i, 0)
                    scores(b, i, 1)
                    pe.wait_ge(A.stt, b * NT + i + 1)
                    pe.wait_ge(A.y_r, b * NT + i + 1)
                    for k in range(KC):
                        last = pe.matmul(bank[5][:, k * P:(k + 1) * P], state[:, k, :], qkT[:, k, :],
                                         start=(k == 0), stop=False, skip_group_check=True)
                    if tail is not None and i == 0:
                        head_means(tail)
                    if tail is not None and i == CHOICE_STEP:
                        counts(1, tail)
                    for q in range(4):
                        if more and q == (3 if ROUTE_AT[i] or FRONT_AT[i] else 2):
                            turn(b, i + 1)
                        attend(b, i, q)
                        if q < 2:
                            scores(b, i, q + 2)
                        if tail is not None:
                            for t in behind(ROUTE_AT[i], q):
                                residual_route(tail, t)
                        if front is not None:
                            for t in behind(FRONT_AT[i], q):
                                front_tile(front, t)
                    if tail is not None:
                        if ROUTE_AT[i][-1:] == (NT - 1,):
                            for t in range(NT - 2, NT):
                                logits(R[1], tail, t)

            pe.wait_ge(F[0].y, NG * GT)
            for t in range(NT):
                front_tile(0, t)
            project(0, 0)
            turn(0, 0)
            sequence(0, None, 1)
            with pe.Fori(0, B - 2) as i:
                for c in shared:
                    c.enter(i, BANK_USES)
                sequence(i + 1, i, i + 2)
            for c in shared:
                c.leave(B - 2)
            sequence(B - 1, B - 2, None)
            head_means(B - 1)
            head_variances(B - 1)
            for t in range(NT):
                out_tile(B - 1, t, t)
            for t in range(NT):
                residual_route(B - 1, t)
            for t in range(NT - 2, NT):
                logits(R[1], B - 1, t)
            counts(1, B - 1)
            pe.wait_ge(R[1].sm_r, 2 * B + 1)
            ffn(1)

        @block.scalar
        def _(act):
            act.sem_inc(R[0].trp_r, 2)

            def normalise(S, ln, dst, src, t):
                act.activation(dst, src[:, t, :], ACT.Identity, bias=ln.nm[:, t:t + 1], scale=ln.rs[:, t:t + 1]).then_inc(S.xn, 1)

            def evac(S, b, t, tr_full, tr_read):
                tr_full(t)
                if t >= 4:
                    act.wait_ge(S.xT_r, b * (NT - 1) + t - 3)
                act.activation(xrT[:, t % 4, :, :], bank[1 + t % 2][:, 0:KC * P].rearrange("p (k x) -> p k x", k=KC), ACT.Copy)\
                    .then_inc(S.xT, 1)
                tr_read(t)

            def exponents(S, b):
                act.wait_ge(S.link, b * LINKS + EXP_LINK)
                act.activation(ex[:], dl[:], ACT.Exp).then_inc(S.exp, 1)

            xs, xns, lns = (xr, xb), (xn_r, xn_odd), (lnr, lnf)
            with act.Fori(0, B // 2) as p:
                for q in range(2):
                    b = p * 2 + q
                    act.wait_ge(R[0].lnnm, b + 1)
                    for t in range(NT + 1):
                        if t < NT:
                            normalise(R[0], lns[q], xns[q][:, t, :], xs[q], t)
                        if t >= 1:
                            evac(R[0], b, t - 1, lambda t: act.wait_ge(R[0].trp, b * NT + t + 1),
                                 lambda t: (act.wait_ge(R[0].xT, b * NT + t + 1), act.sem_inc(R[0].trp_r, 1)))
                    exponents(R[0], b)

            for n in range(20):
                j, k = n // KC, n % KC
                act.wait_ge(S0.wT, n + 1)
                act.activation(wTh[:, k, j * P:(j + 1) * P], bank[n % 4][:, 0:P], ACT.Copy).then_inc(S0.wTh, 1)

            def ffn(r):
                f = F[r]

                def split_x(j, xT_value):
                    act.wait_ge(f.xT, xT_value)
                    for k in range(KC):
                        act.activation(xh[j % 2][:, k, :], bank[6 + k][:], ACT.Copy).then_inc(f.xh, 1)

                def gelu(j, fj, up_value, lo_value):
                    act.wait_ge(f.up, up_value)
                    if lo_value is not None:
                        act.wait_ge(f.hl, lo_value)
                    act.activation(h32[fj % 2][:], bank[fj % 2][:], ACT.Gelu_apprx_tanh).then_inc(f.gelu, 1)

                def high1(fj):
                    w = slice(fj * P, (fj + 1) * P)
                    act.activation(w1h[:, :, w], stg1[:, :, w], ACT.Copy).then_inc(f.w1h, 1)

                def high2(fj):
                    act.activation(w2h[:, fj, :], stg2[:, fj, :], ACT.Copy).then_inc(f.w2h, 1)

                def weigh(p, j, end):
                    act.wait_ge(f.down, p * GE + j + 1)
                    if not (isinstance(p, int) and p == 0 and j < 2):
                        act.wait_ge(f.add, (p * GE + j - 1) * GT * 16)
                    for t in range(GT):
                        if end and t == GT // 2:
                            act.wait_ge(f.down, NG + 1)
                        act.activation(yb[j % 2][:, t, :], bank[2 + 2 * (j % 2) + t // 2][:, (t % 2) * C:(t % 2 + 1) * C],
                                       ACT.Copy, scale=tab[:, j, t, 1:2]).then_inc(f.y, 1)

                act.wait_ge(f.w1raw, 16)
                for fj in range(FJ):
                    high1(fj)
                split_x(0, 1)
                act.wait_ge(f.w2raw, 16)
                for fj in range(FJ):
                    high2(fj)
                split_x(1, 2)
                for fj in range(FJ):
                    gelu(0, fj, fj + 1, None if fj < 2 else fj - 1)

                def pair(p, last):
                    for j in range(GE):
                        for fj in range(FJ):
                            if not (last and j == GE - 1):
                                g1 = (p * GE + j + 1) * FJ + fj
                                gelu((j + 1) % GE, fj, g1 + 1, g1 - 1)
                            if j % 2 == 0 and not (last and j == GE - 2):
                                if fj == 0:
                                    act.wait_ge(f.w1raw, (p * 2 + j // 2 + 2) * 16)
                                high1(fj)
                            if j % 2 == 1 and not (last and j == GE - 1):
                                if fj == 0:
                                    act.wait_ge(f.w2raw, (p * 2 + j // 2 + 2) * 16)
                                high2(fj)
                            if fj == 5 and not (last and j + 2 >= GE):
                                split_x((j + 2) % GE, p * GE + j + 3)
                        weigh(p, j, last and j == GE - 1)

                pair(0, False)
                with act.Fori(1, NP - 1) as p:
                    pair(p, False)
                pair(NP - 1, True)

            ffn(0)

            c1, c2 = Count(), Count()
            shared, fulls, frees = (c1, c2), (A.v, A.t), (A.v_r, A.t_r)
            act.sem_inc(A.v_r, 1)
            act.sem_inc(A.t_r, 1)
            act.sem_inc(A.y_r, 1)

            def front_norm(b, t):
                if t == 0:
                    act.wait_ge(A.lnnm, b + 1)
                if t >= 4:
                    act.wait_ge(A.f, b * NT + t - 3)
                normalise(A, lnf, xn_f[:, t % 4, :], xb, t)

            def front_evac(b, t):
                act.wait_ge(fulls[t % 2], shared[t % 2].up())
                act.activation(xnh[:, :, t * P:(t + 1) * P], bank[1 + t % 2][:, 0:C].rearrange("p (k x) -> p k x", k=KC), ACT.Copy)\
                    .then_inc(A.f, 1)

            def values(b, i):
                act.wait_ge(A.v, c1.up())
                dst = vz[:, i % 2, :].rearrange("p (m a y) -> p m a y", a=4, y=D)[:, :, 0:4:3, :]
                act.activation(dst, bank[1][:, 0:C].rearrange("p (m a y) -> p m a y", a=2, y=D), ACT.Copy).then_inc(A.vz, 1)
                act.wait_ge(A.vz, b * NT + i + 1)
                act.sem_inc(A.v_r, 1)

            def gate(b, half, tail):
                if half == 0 and tail is not None:
                    act.wait_ge(A.gated, tail * KC + KC)
                for n, m in enumerate((1, 0)):
                    act.wait_ge(fulls[m], shared[m].up())
                    act.activation(gT[:, m, half * 512:(half + 1) * 512], bank[1 + m][:], ACT.Silu).then_inc(A.g, 1)
                    act.wait_ge(A.g, b * 4 + half * KC + n + 1)
                    act.sem_inc(frees[m], 1)

            def head_norm(b):
                act.wait_ge(A.gaff, b + 1)
                act.wait_ge(A.moved, b + 1)
                for k in range(KC):
                    act.activation(yg[:, k, :], yT[:, k, :], ACT.Identity, bias=gsm[:, 6, k:k + 1], scale=gsm[:, 4, k:k + 1])\
                        .then_inc(A.yg, 1)

            def queries(four):
                for m in range(4 * four, 4 * four + 4):
                    last = act.activation(qm[:, :, m, :], qkT[:, 0:KC, :], ACT.Copy, scale=K_["headsel"][:, m:m + 1])
                last.then_inc(A.qm, 1)

            def output(b, i, tail=None):
                act.wait_ge(A.y, b * NT + i + 1)
                if i == 0 and tail is not None:
                    act.wait_ge(A.moved, tail + 1)
                dst = yT[:, :, i * P:(i + 1) * P] if i else y0[:]
                act.activation(dst, bank[5][:, 0:C].rearrange("p (k x) -> p k x", k=KC), ACT.Copy)\
                    .then_inc(A.y_r, 1)

            def gated_high(b):
                for k in range(KC):
                    act.wait_ge(A.gated, b * KC + k + 1)
                    act.activation(ygh[:, k, :], yg[:, k, :], ACT.Copy).then_inc(A.ygh, 1)

            def residual_norm(b, t):
                if t == 0:
                    act.wait_ge(R[1].lnnm, b + 1)
                normalise(R[1], lnr, xn_r[:, t, :], xr, t)

            def residual_evac(b, t):
                evac(R[1], b, t, lambda t: act.wait_ge(fulls[t % 2], shared[t % 2].up()),
                     lambda t: (act.wait_ge(R[1].xT, b * NT + t + 1), act.sem_inc(frees[t % 2], 1)))

            def sequence(b, tail, front):
                for i in range(NT):
                    act.wait_ge(A.t, c2.up())
                    act.activation(qkT[:, :, :], bank[2][:].rearrange("p (n x) -> p n x", x=P), ACT.Copy).then_inc(A.qkT, 1)
                    act.wait_ge(A.qkT, b * NT + i + 1)
                    act.sem_inc(A.t_r, 1)
                    queries(0)
                    if i:
                        output(b, i - 1, tail)
                    elif tail is not None:
                        output(tail, NT - 1)
                    if i + 1 < NT or front is not None:
                        values(b, i + 1)
                    queries(1)
                    if tail is not None and i == 1:
                        head_norm(tail)
                    if i in GATE_AT:
                        gate(b, GATE_AT.index(i), tail)
                    if tail is not None:
                        for t in NORM_AT[i]:
                            residual_norm(tail, t)
                        if i == GATING_STEP + 1:
                            gated_high(tail)
                        if i == CHOICE_STEP:
                            exponents(R[1], tail)
                    if front is not None:
                        for t in FRONT_AT[i]:
                            front_norm(front, t)
                    for q in range(3):
                        if tail is not None:
                            for t in behind(ROUTE_AT[i], q):
                                residual_evac(tail, t)
                        if front is not None:
                            for t in behind(FRONT_AT[i], q):
                                front_evac(front, t)

            for t in range(NT + 2):
                if t < NT:
                    front_norm(0, t)
                if t >= 2:
                    front_evac(0, t - 2)
            values(0, 0)
            sequence(0, None, 1)
            with act.Fori(0, B - 2) as i:
                for c in shared:
                    c.enter(i, BANK_USES)
                sequence(i + 1, i, i + 2)
            for c in shared:
                c.leave(B - 2)
            sequence(B - 1, B - 2, None)
            output(B - 1, NT - 1)
            head_norm(B - 1)
            gated_high(B - 1)
            for t in range(NT + 1):
                if t < NT:
                    residual_norm(B - 1, t)
                if t >= 1:
                    residual_evac(B - 1, t - 1)
            exponents(R[1], B - 1)
            ffn(1)

        @block.vector
        def _(dve):
            def tile_stats(S, ln, x, t):
                dve.bn_stats(ln.st[:, t, :], x[:, t, :]).then_inc(S.lnst, 1)

            def norm_stats(S, ln, b):
                dve.wait_ge(S.lnst, b * NT + NT)
                mean, sq = (lambda a: ln.st[:, :, 3 * a + 1]), (lambda a: ln.st[:, :, 3 * a + 2])
                dve.tensor_tensor(ln.mv[:, 0], mean(0), mean(1), ALU.add).then_inc(S.lnmv, 1)
                dve.tensor_tensor(ln.mv[:, 1], mean(0), mean(1), ALU.subtract).then_inc(S.lnmv, 1)
                dve.tensor_tensor(ln.mv[:, 2], sq(0), sq(1), ALU.add).then_inc(S.lnmv, 1)
                dve.wait_ge(S.lnmv, b * LN_STEPS + 2)
                dve.tensor_tensor(ln.mv[:, 3], ln.mv[:, 1], ln.mv[:, 1], ALU.mult).then_inc(S.lnmv, 1)
                dve.wait_ge(S.lnmv, b * LN_STEPS + 4)
                dve.scalar_tensor_tensor(ln.mv[:, 4], ln.mv[:, 3], C / 4.0, ln.mv[:, 2], ALU.mult, ALU.add).then_inc(S.lnmv, 1)
                dve.wait_ge(S.lnmv, b * LN_STEPS + LN_STEPS)
                dve.tensor_scalar(ln.rv[:], ln.mv[:, 4], 1.0 / C, EPS, ALU.mult, ALU.add).then_inc(S.lnrv, 1)

            def norm_shift(S, ln, b):
                dve.wait_ge(S.lnrs, b + 1)
                dve.scalar_tensor_tensor(ln.nm[:], ln.mv[:, 0], -0.5, ln.rs[:], ALU.mult, ALU.mult).then_inc(S.lnnm, 1)

            te = [P, NT, E]
            over_t = lambda a: a.unsqueeze(1).to_broadcast(te)
            over_e = lambda a: a.unsqueeze(2).to_broadcast(te)

            def steps(S, b, before):
                n = [before]

                def did(ins):
                    ins.then_inc(S.link, 1)
                    n[0] += 1

                def after(step):
                    assert step <= n[0]
                    dve.wait_ge(S.link, b * LINKS + step)

                return did, after, n

            def choices(r, b):
                S = R[r]
                did, after, n = steps(S, b, 0)
                logit = bank[7][:, 0:NT * E].rearrange("p (t e) -> p t e", e=E)
                dve.wait_ge(S.sm, b * 2 + 1)
                did(dve.tensor_reduce(red[:, 0, :], logit, AX.X, ALU.max))
                after(1)
                dve.tensor_tensor(dl[:], logit, over_e(red[:, 0, :]), ALU.subtract).then_inc(S.sm_r, 1)
                dve.wait_ge(S.sm_r, b * 2 + 2)
                did(dve.tensor_scalar(dl[:], dl[:], -87.0, None, ALU.max))
                assert n[0] == EXP_LINK
                after(2)
                did(dve.scalar_tensor_tensor(key[:, 0], dl[:], 0.0, over_t(K_["revexp"]), ALU.is_ge, ALU.mult))
                after(3)
                did(dve.tensor_reduce(sel[:, 0, 0:NT], key[:, 0], AX.X, ALU.max))
                after(4)
                did(dve.tensor_tensor(oh[:, 0], key[:, 0], over_e(sel[:, 0, 0:NT]), ALU.is_equal))
                after(5)
                did(dve.scalar_tensor_tensor(d2[:], oh[:, 0], -1.0e30, dl[:], ALU.mult, ALU.add))
                after(6)
                did(dve.tensor_reduce(red[:, 1, :], d2[:], AX.X, ALU.max))
                after(7)
                did(dve.tensor_tensor(key[:, 1], d2[:], over_e(red[:, 1, :]), ALU.is_equal))
                after(8)
                did(dve.tensor_tensor(key[:, 1], key[:, 1], over_t(K_["revexp"]), ALU.mult))
                after(9)
                did(dve.tensor_reduce(sel[:, 0, NT:RT], key[:, 1], AX.X, ALU.max))
                after(10)
                did(dve.tensor_tensor(oh[:, 1], key[:, 1], over_e(sel[:, 0, NT:RT]), ALU.is_equal))
                assert n[0] == OH_LINK

            def places(r, b):
                S = R[r]
                did, after, n = steps(S, b, OH_LINK)
                dve.wait_ge(S.exp, b + 1)
                did(dve.tensor_reduce(red[:, 2, :], ex[:], AX.X, ALU.add))
                after(OH_LINK)
                did(dve.tensor_tensor(key[:], oh[:], ex[:].unsqueeze(1).to_broadcast([P, TOPK, NT, E]), ALU.mult))
                dve.wait_ge(S.sm, b * 2 + 2)
                ahead = bank[7][:, 0:RT * E].rearrange("p (k t e) -> p k t e", k=TOPK, t=NT)
                whole = bank[7][:, RT * E:2 * RT * E].rearrange("p (k t e) -> p k t e", k=TOPK, t=NT)
                flat = lambda a: a.rearrange("p k e t -> p (k e t)")
                by_t = lambda a: a.rearrange("p k e t -> p k t e")
                did(dve.tensor_copy(by_t(cnt[:]), whole))
                after(OH_LINK + 1)
                did(dve.reciprocal(red[:, 3, :], red[:, 2, :]))
                after(OH_LINK + 2)
                did(dve.tensor_reduce(sel[:, 1, :], key[:].rearrange("p k t e -> p (k t) e"), AX.X, ALU.add))
                after(OH_LINK + 3)
                did(dve.tensor_tensor_scan(flat(scn[:]), K_["restart"], flat(cnt[:]), 0.0, ALU.mult, ALU.add))
                dve.tensor_tensor(pos[:], ahead, by_t(cnt[:]), ALU.subtract).then_inc(S.sm_r, 1)
                kt = lambda a: a.rearrange("p (k t) -> p k t", k=TOPK)
                after(OH_LINK + 6)
                did(dve.tensor_tensor(kt(sel[:, 2, :]), kt(sel[:, 1, :]), red[:, 3, :].unsqueeze(1).to_broadcast([P, TOPK, NT]), ALU.mult))
                dve.wait_ge(S.sm_r, b * 2 + 3)
                did(dve.tensor_tensor(pos[:], pos[:], by_t(scn[:]), ALU.add))
                after(OH_LINK + 8)
                did(dve.tensor_tensor(pos[:], pos[:], base[:].unsqueeze(2).to_broadcast([P, TOPK, NT, E]), ALU.add))
                after(OH_LINK + 9)
                did(dve.tensor_tensor(base[:], base[:], scn[:, :, :, NT - 1], ALU.add))
                did(dve.tensor_tensor(pos[:], pos[:], oh[:], ALU.mult))
                after(OH_LINK + 11)
                did(dve.tensor_reduce(sel[:, 3, :], pos[:].rearrange("p k t e -> p (k t) e"), AX.X, ALU.add))
                assert n[0] == PLACE_LINK

            def entries(r, b, q):
                S = R[r]
                did, after, n = steps(S, b, PLACE_LINK)
                after(PLACE_LINK)
                did(dve.tensor_scalar(sel[:, 4, :], sel[:, 3, :], float(CAP), None, ALU.is_lt))
                did(dve.scalar_tensor_tensor(sel[:, 5, :], sel[:, 0, :], -float(CAP), sel[:, 3, :], ALU.mult, ALU.add))
                if r == 1:
                    dve.wait_ge(S.sent, b + 1)
                did(dve.tensor_copy(pay[:, q].bitcast(u32).rearrange("p (k t) w -> p k t w", k=TOPK)[:, :, :, 0],
                                    ids[:].unsqueeze(1).to_broadcast([P, TOPK, NT])))
                after(PLACE_LINK + 2)
                did(dve.tensor_tensor(sel[:, 5, :], sel[:, 5, :], K_["slotbase"], ALU.add))
                did(dve.tensor_scalar(sel[:, 6, :], sel[:, 4, :], -BIG, BIG, ALU.mult, ALU.add))
                did(dve.scalar_tensor_tensor(pay[:, q, :, 1], sel[:, 2, :], 0.5, sel[:, 4, :], ALU.mult, ALU.mult))
                after(PLACE_LINK + 5)
                did(dve.tensor_tensor(idx[:, q], sel[:, 5, :], sel[:, 6, :], ALU.add))
                dve.tensor_scalar(ids[:], ids[:], float(T), None, ALU.add).then_inc(S.pay, 1)
                dve.wait_ge(S.pay, b + 1)
                assert n[0] == LINKS

            def start_route(r):
                dve.memset(base[:], 0.0).then_inc(S0.base, 1)
                dve.tensor_copy(ids[:], K_["ids"]).then_inc(S0.base, 1)
                dve.wait_ge(S0.base, 2 * r + 2)
                dve.sem_inc(R[r].sm_r, 1)
                if r == 1:
                    dve.sem_inc(R[r].sent, 1)

            xs, x_here, lns = (xr, xb), (R[0].x, R[0].x_odd), (lnr, lnf)

            def first_stats(b, q, value):
                dve.wait_ge(x_here[q], value)
                for t in range(NT):
                    tile_stats(R[0], lns[q], xs[q], t)
                norm_stats(R[0], lns[q], b)

            def first_route(b, q, p, first=False, last=False):
                if not last:
                    first_stats(b + 1, 1 - q, (p + q) * 16 + 16)
                dve.wait_ge(R[0].xn, b * NT + NT)
                if not first:
                    dve.wait_ge(R[0].stored, b * 16)
                dve.tensor_tensor(x_half, xs[q][:], hbias[:].unsqueeze(1).to_broadcast([P, NT, C]), ALU.add).then_inc(R[0].half, 1)
                choices(0, b)
                if not last:
                    if not first:
                        dve.wait_ge(R[0].xnst, b * 16)
                    norm_shift(R[0], lns[1 - q], b + 1)
                places(0, b)
                entries(0, b, b)

            first_stats(0, 0, 16)
            dve.wait_ge(S0.vec, 80)
            dve.tensor_scalar(hbias[:], hbias[:], 0.5, None, ALU.mult).then_inc(S0.bias, 1)
            dve.wait_ge(S0.bias, 1)
            dve.wait_ge(S0.const, 16)
            start_route(0)
            norm_shift(R[0], lns[0], 0)
            first_route(0, 0, 0, first=True)
            first_route(1, 1, 0)
            with dve.Fori(1, B // 2 - 1) as p:
                for q in range(2):
                    first_route(p * 2 + q, q, p)
            first_route(B - 2, 0, B // 2 - 1)
            first_route(B - 1, 1, B // 2 - 1, last=True)
            for n in range(20):
                j, k = n // KC, n % KC
                w = slice(j * P, (j + 1) * P)
                dve.wait_ge(S0.wTh, n + 1)
                dve.tensor_tensor(wTl[:, k, w], bank[n % 4][:, 0:P], wTh[:, k, w].bitcast(fp32), ALU.subtract).then_inc(S0.wTl, 1)

            def ffn(r):
                f = F[r]

                def split_x(j, xh_value):
                    for k in range(KC):
                        dve.wait_ge(f.xh, xh_value + k)
                        dve.tensor_tensor(xl[j % 2][:, k, :], bank[6 + k][:], xh[j % 2][:, k, :].bitcast(fp32), ALU.subtract).then_inc(f.xl, 1)

                def low1(fj, value):
                    w = slice(fj * P, (fj + 1) * P)
                    dve.wait_ge(f.w1h, value)
                    dve.tensor_tensor(w1l[:, :, w], stg1[:, :, w], w1h[:, :, w].bitcast(fp32), ALU.subtract).then_inc(f.w1l, 1)

                def low2(fj, value):
                    dve.wait_ge(f.w2h, value)
                    dve.tensor_tensor(w2l[:, fj, :], stg2[:, fj, :], w2h[:, fj, :].bitcast(fp32), ALU.subtract).then_inc(f.w2l, 1)

                def high(fj, value):
                    dve.wait_ge(f.gelu, value)
                    dve.tensor_copy(hh[:, fj, :], h32[fj % 2][:]).then_inc(f.hh, 1)

                def low(fj, value):
                    dve.wait_ge(f.hh, value)
                    dve.tensor_tensor(hl[:, fj, :], h32[fj % 2][:], hh[:, fj, :].bitcast(fp32), ALU.subtract).then_inc(f.hl, 1)

                for fj in range(FJ):
                    low1(fj, fj + 1)
                split_x(0, 1)
                for fj in range(FJ):
                    low2(fj, fj + 1)
                split_x(1, KC + 1)
                for fj in range(FJ):
                    high(fj, fj + 1)
                    low(fj, fj + 1)

                def pair(p, last):
                    for j in range(GE):
                        for fj in range(FJ):
                            go = not (last and j == GE - 1)
                            value = (p * GE + j + 1) * FJ + fj + 1
                            if go:
                                high(fj, value)
                            if j % 2 == 0 and not (last and j == GE - 2):
                                low1(fj, (p * 2 + j // 2 + 1) * FJ + fj + 1)
                            if j % 2 == 1 and not (last and j == GE - 1):
                                low2(fj, (p * 2 + j // 2 + 1) * FJ + fj + 1)
                            if go:
                                low(fj, value)
                            if fj == 5 and not (last and j + 2 >= GE):
                                split_x((j + 2) % GE, (p * GE + j + 2) * KC + 1)

                pair(0, False)
                with dve.Fori(1, NP - 1) as p:
                    pair(p, False)
                pair(NP - 1, True)

            ffn(0)

            dve.sem_inc(A.qk_r, 1)
            dve.sem_inc(A.aw, 2)
            dve.sem_inc(A.st_r, 1)

            def front_stats(b, tiles):
                for t in tiles:
                    if t == 0:
                        dve.wait_ge(A.x, b * 16 + 16)
                    tile_stats(A, lnf, xb, t)
                    if t == NT - 1:
                        norm_stats(A, lnf, b)

            def front_low(b, t):
                dve.wait_ge(A.f, b * NT + t + 1)
                s = slice(t * P, (t + 1) * P)
                dve.tensor_tensor(xnl[:, :, s], bank[1 + t % 2][:, 0:C].rearrange("p (k x) -> p k x", k=KC), xnh[:, :, s].bitcast(fp32),
                                  ALU.subtract).then_inc(A.fl, 1)
                dve.wait_ge(A.fl, b * NT + t + 1)
                dve.sem_inc((A.v_r, A.t_r)[t % 2], 1)

            def rotate(b, i):
                dve.wait_ge(A.qk, b * NT + i + 1)
                two = lambda a: a.rearrange("p (c w) -> p c w", w=2)
                dve.tensor_tensor(rt1[:, i % 2, :], bank[0][:], rope[:, i % NT, 0, :], ALU.mult)
                dve.tensor_tensor(two(rt2[:, i % 2, :])[:, :, 0], two(bank[0][:])[:, :, 1], two(rope[:, i % NT, 1, :])[:, :, 0], ALU.mult)
                dve.tensor_tensor(two(rt2[:, i % 2, :])[:, :, 1], two(bank[0][:])[:, :, 0], two(rope[:, i % NT, 1, :])[:, :, 1], ALU.mult)\
                    .then_inc(A.qk_r, 1)

            def mask(b, i, q):
                dve.wait_ge(A.sc, (b * NT + i) * 4 + q + 1)
                dve.tensor_tensor(aw[:, q], bank[3 + q % 2][:].rearrange("p (m x) -> p m x", m=4),
                                  causal.unsqueeze(1).to_broadcast([P, 4, P]), ALU.mult).then_inc(A.aw, 1)

            def channel_stats(b, i):
                dve.wait_ge(A.y_r, b * NT + i + 2)
                for k in range(KC):
                    dve.bn_stats(gst[:, k, i, :], yT[:, k, i * P:(i + 1) * P] if i else y0[:, k, :]).then_inc(A.gst, 1)

            def norm_steps(b, before):
                n = [before]

                def link(ins):
                    ins.then_inc(A.glink, 1)
                    n[0] += 1
                    dve.wait_ge(A.glink, b * GLINKS + n[0])

                return link

            def channels(b):
                link = norm_steps(b, 0)
                part = gst[:].rearrange("p k n (a s) -> p k (n a) s", s=3)
                dve.wait_ge(A.gst, (b * NT + NT) * KC)
                link(dve.tensor_reduce(gsm[:, 7, :], part[:, :, :, 1], AX.X, ALU.add))
                dve.tensor_scalar(gmv[:, :, 0], gsm[:, 7, :], 1.0 / (2 * NT), None, ALU.mult).then_inc(A.gmv, 1)
                dve.wait_ge(A.gmv, b + 1)
                link(dve.tensor_tensor(gdv[:], part[:, :, :, 1], gmv[:, :, 0:1].to_broadcast([P, KC, 2 * NT]), ALU.subtract))
                link(dve.tensor_tensor(gdv[:], gdv[:], gdv[:], ALU.mult))
                link(dve.scalar_tensor_tensor(gdv[:], gdv[:], P / 2.0, part[:, :, :, 2], ALU.mult, ALU.add))
                dve.tensor_reduce(gmv[:, :, 1], gdv[:], AX.X, ALU.add).then_inc(A.gst2, 1)

            def about_head(b):
                link = norm_steps(b, 4)
                dve.wait_ge(A.gs, b * 2 + 1)
                link(dve.tensor_copy(gsm[:, 0, :], bank[7][:, 0:KC]))
                link(dve.tensor_tensor(gsm[:, 1, :], gmv[:, :, 0], gsm[:, 0, :], ALU.subtract))
                link(dve.tensor_tensor(gsm[:, 1, :], gsm[:, 1, :], gsm[:, 1, :], ALU.mult))
                dve.wait_ge(A.gst2, b + 1)
                dve.scalar_tensor_tensor(gsm[:, 1, :], gmv[:, :, 1], 1.0 / T, gsm[:, 1, :], ALU.mult, ALU.add).then_inc(A.gs_r, 1)

            def head_variance(b):
                dve.wait_ge(A.gs, b * 2 + 2)
                dve.tensor_scalar(gsm[:, 2, :], bank[7][:, 0:KC], EPS, None, ALU.add).then_inc(A.grv, 1)

            def affine(b):
                link = norm_steps(b, 7)
                dve.wait_ge(A.grs, b + 1)
                link(dve.tensor_tensor(gsm[:, 4, :], gsm[:, 3, :], gnw[:], ALU.mult))
                link(dve.tensor_tensor(gsm[:, 5, :], gsm[:, 0, :], gsm[:, 4, :], ALU.mult))
                dve.tensor_tensor(gsm[:, 6, :], gnb[:], gsm[:, 5, :], ALU.subtract).then_inc(A.gaff, 1)

            def gating(b):
                for k in range(KC):
                    dve.wait_ge(A.yg, b * KC + k + 1)
                    if k == 0:
                        dve.wait_ge(A.g, b * 4 + 4)
                    dve.tensor_tensor(yg[:, k, :], yg[:, k, :], gT[:, k, :], ALU.mult).then_inc(A.gated, 1)

            def gated_low(b):
                for k in range(KC):
                    dve.wait_ge(A.ygh, b * KC + k + 1)
                    dve.tensor_tensor(ygl[:, k, :], yg[:, k, :], ygh[:, k, :].bitcast(fp32), ALU.subtract).then_inc(A.ygl, 1)

            def residual(b, t, nth):
                if t == 0:
                    dve.wait_ge(R[1].x, b * 16 + 16)
                dve.wait_ge(A.out, b * NT + t + 1)
                dve.tensor_tensor(xr[:, t, :], xr[:, t, :], bank[3 + nth % 2][:, 0:C], ALU.add).then_inc(R[1].o, 1)

            def residual_stats(b, t):
                dve.wait_ge(R[1].o, b * NT + t + 1)
                tile_stats(R[1], lnr, xr, t)

            def residual_entries(b):
                entries(1, b, 0)
                dve.wait_ge(R[1].xnst, b * 16 + 16)

            def sequence(b, tail, front):
                dve.memset(state[:], 0.0).then_inc(A.state0, 1)
                dve.wait_ge(A.state0, b + 1)
                dve.sem_inc(A.stt, 1)
                for i in range(NT):
                    nb = b * NT + i
                    if tail is not None:
                        if i == 0:
                            channel_stats(tail, NT - 1)
                            channels(tail)
                        if i == CHOICE_STEP:
                            choices(1, tail)
                    if front is not None and FRONT_AT[i][:1] == (0,):
                        norm_shift(A, lnf, front)
                    if tail is not None:
                        for n, t in enumerate(OUT_AT[i]):
                            residual(tail, t, n)
                    if i + 1 < NT or front is not None:
                        rotate(b, i + 1)
                    if tail is not None:
                        if i == 1:
                            head_variance(tail)
                    mask(b, i, 0)
                    mask(b, i, 1)
                    if tail is not None:
                        if i == 1:
                            affine(tail)
                        if NORM_AT[i][:1] == (0,):
                            norm_shift(R[1], lnr, tail)
                        for t in OUT_AT[i][:4]:
                            residual_stats(tail, t)
                    mask(b, i, 2)
                    if tail is not None:
                        for t in OUT_AT[i][4:]:
                            residual_stats(tail, t)
                    if front is not None:
                        for t in behind(FRONT_AT[i], 0):
                            front_low(front, t)
                    mask(b, i, 3)
                    if front is not None:
                        for t in behind(FRONT_AT[i], 1) + behind(FRONT_AT[i], 2):
                            front_low(front, t)
                    if tail is not None and OUT_AT[i][-1:] == (NT - 1,):
                        norm_stats(R[1], lnr, tail)
                    dve.wait_ge(A.st, nb + 1)
                    dve.tensor_tensor(stmp[:], bank[6][:, 0:C].rearrange("p (k x) -> p k x", k=KC),
                                      K_["stateblk"].rearrange("p (k x) -> p k x", k=KC), ALU.mult).then_inc(A.st_r, 1)
                    dve.wait_ge(A.st_r, nb + 2)
                    if i + 1 < NT:
                        dve.wait_ge(A.stt, nb + 1)
                        for k in range(KC):
                            last = dve.scalar_tensor_tensor(state[:, k, :], state[:, k, :], K_["decay"][:, k:k + 1], stmp[:, k, :],
                                                            ALU.mult, ALU.add)
                        last.then_inc(A.stt, 1)
                    if tail is not None:
                        if i == 0:
                            about_head(tail)
                        if i == GATING_STEP:
                            gating(tail)
                        if i == GATING_STEP + 1:
                            gated_low(tail)
                        if i == CHOICE_STEP:
                            places(1, tail)
                        if i == CHOICE_STEP + 1:
                            residual_entries(tail)
                    if front is not None:
                        front_stats(front, STATS_AT[i])
                    if i:
                        channel_stats(b, i - 1)

            start_route(1)
            front_stats(0, range(NT))
            norm_shift(A, lnf, 0)
            for t in range(NT):
                front_low(0, t)
            dve.wait_ge(S0.rope, NT * 16)
            rotate(0, 0)
            sequence(0, None, 1)
            with dve.Fori(0, B - 2) as i:
                sequence(i + 1, i, i + 2)
            sequence(B - 1, B - 2, None)
            channel_stats(B - 1, NT - 1)
            channels(B - 1)
            about_head(B - 1)
            head_variance(B - 1)
            affine(B - 1)
            gating(B - 1)
            gated_low(B - 1)
            for t in range(NT):
                residual(B - 1, t, t)
                residual_stats(B - 1, t)
            norm_stats(R[1], lnr, B - 1)
            norm_shift(R[1], lnr, B - 1)
            choices(1, B - 1)
            places(1, B - 1)
            residual_entries(B - 1)
            ffn(1)


GATE_AT = (5, 6)
GATING_STEP = 1
OUT_AT = ((), (), (), tuple(range(NT)), (), (), (), ())
NORM_AT = ((), (), (), (), (0, 1, 2, 3, 4, 5), (6, 7), (), ())
ROUTE_AT = ((), (), (), (), (0, 1, 2, 3), (4, 5, 6, 7), (), ())
BIAS_AT = ((), (), (), (), (), (0, 1, 2, 3), (4, 5, 6, 7), ())
CHOICE_STEP = 6
SENT_AT = ((), (0, 1, 2), (3, 4, 5), (6, 7, 8), (9, 10, 11), (12, 13, 14, 15), (), ())
STATS_AT = ((0, 1, 2, 3), (), (), (), (4, 5, 6, 7), (), (), ())
FRONT_AT = ((), (), (), (), (), (), (0, 1, 2, 3), (4, 5, 6, 7))


def behind(tiles, q):
    return tiles[2 * q:2 * q + 2]


BANK_USES = NT + 2 + NT // 2 + NT // 2

EXP_LINK, OH_LINK, PLACE_LINK, LINKS = 2, 11, 23, 30
GLINKS = 9
LN_STEPS = 5


def shape_constants():
    p = np.arange(P)
    h = np.arange(H, dtype=np.float32)
    gamma = (np.float32(1.0) - np.float32(2.0) ** (np.float32(-5.0) - h)).astype(np.float64)
    at, n = const_at()
    c = np.zeros((P, n), np.float32)

    def put(name, a):
        c[:, at[name][0]:at[name][1]] = a

    head = p // D
    put("ident", np.eye(P))
    put("before", p[:, None] < p[None, :])
    put("causal", p[:, None] <= p[None, :])
    same = head[:, None] == head[None, :]
    put("headmean", same / D)
    decay = np.stack([gamma[k * HH + head] ** P for k in range(KC)], 1)
    put("stateblk", np.concatenate([same * decay[:, k:k + 1] for k in range(KC)], 1))
    put("headsel", head[:, None] == np.arange(HH)[None, :])
    put("decay", decay)
    put("revexp", (E - np.arange(E))[None, :])
    put("restart", (np.arange(RT * E) % NT != 0)[None, :])
    put("slotbase", (E * CAP + np.arange(RT) // NT * (E * CAP))[None, :])
    put("mhalf", -0.5)
    put("ids", np.arange(NT)[None, :] * P + p[:, None])
    half = np.arange(0, D, 2, dtype=np.float32)
    inv = (np.float32(1.0) / np.float32(10000.0) ** (half / np.float32(D))).astype(np.float32)
    t = np.arange(T, dtype=np.float32)
    ang = (t[:, None] * inv[None, :]).astype(np.float32).astype(np.float64)
    vec = ((half + np.float32(0.4 * D)) / np.float32(1.4 * D)).astype(np.float64)
    scale = vec[None, :] ** ((t.astype(np.float64) - T // 2) / 512.0)[:, None]
    tau = (np.arange(T) % P).astype(np.float64)
    rope = np.zeros((T, 2, 2, H, D))
    for w, s, g in ((0, scale * D ** -0.5, tau), (1, 1.0 / scale, -tau)):
        dec = gamma[None, :] ** g[:, None]
        for half_ in range(2):
            rope[:, 0, w, :, half_::2] = (np.cos(ang) * s)[:, None, :] * dec[:, :, None]
            rope[:, 1, w, :, half_::2] = (np.sin(ang) * s * (-1.0 if half_ == 0 else 1.0))[:, None, :] * dec[:, :, None]
    rope = rope.reshape(NT, P, 2, 2 * C).astype(np.float32)
    slots = np.zeros((SLOTS, 2), np.uint32)
    slots[:, 0] = N + np.arange(SLOTS) % G
    return c, rope, slots.view(np.float32)


_INS = ["L0_attn_x", "L0_attn_w_qkv", "L0_attn_w_gated", "L0_attn_w_proj", "L0_attn_gn_weight", "L0_attn_gn_bias",
        "L0_ffn_router_w", "L0_ffn_w1", "L0_ffn_w2", "L0_ffn_bias"]


def kernel(**inputs):
    import concourse.bacc as bacc
    from concourse.bass_utils import run_bass_kernel_spmd

    nc = bacc.Bacc("TRN2", target_bir_lowering=False, num_devices=1)
    arrays = {name: np.ascontiguousarray(inputs[name]) for name in _INS}
    arrays["L0_attn_x"] = arrays["L0_attn_x"].reshape(N, C)
    arrays["consts"], arrays["rope"], arrays["slots"] = shape_constants()
    args = [nc.dram_tensor(f"in_{n}", a.shape, mybir.dt.from_np(a.dtype), kind="ExternalInput").ap() for n, a in arrays.items()]
    out = nc.dram_tensor("out_rows", (ROWS, C), DT.float32, kind="ExternalOutput").ap()
    macaron_kernel(nc, *args, out)
    r = run_bass_kernel_spmd(nc, [{f"in_{n}": a for n, a in arrays.items()}], core_ids=[0])
    return r.results[0]["out_rows"][0:N].reshape(B, T, C)
```
